# Optimizing a Trainium2 kernel written in Bass

```python
import numpy as np
import jax
import jax.numpy as jnp

def _softmax(x, axis=-1):
    return jax.nn.softmax(x, axis=axis)

def _gelu(x):
    return jax.nn.gelu(x, approximate=True)

def _silu(x):
    return jax.nn.silu(x)

def _sigmoid(x):
    return jax.nn.sigmoid(x)

def _layernorm(x, axis=-1, eps=1e-05):
    m = jnp.mean(x, axis=axis, keepdims=True)
    v = jnp.var(x, axis=axis, keepdims=True)
    return (x - m) / jnp.sqrt(v + eps)

def _scatter_add(tgt, idx, src, axis=0):
    return tgt.at[idx].add(src)

def _segment_sum(src, seg, n):
    return jax.ops.segment_sum(src, seg, n)
kernel_name = 'mk_gnn_resnorm_d4_gnn_r16_58fa3b'

def setup_inputs(seed: int=0):
    np.random.seed(seed)
    _w = jnp.asarray

    def _rec_inputs():
        import jax
        import jax.numpy as jnp
        _gk = jax.random.key(seed)
        x = -0.0003713 + 1 * jax.random.normal(jax.random.fold_in(_gk, 1), (6250, 128), jnp.float32)
        src = jax.random.randint(jax.random.fold_in(_gk, 2), (100000,), 0, 6250, jnp.int32)
        dst = jax.random.randint(jax.random.fold_in(_gk, 3), (100000,), 0, 6250, jnp.int32)
        _o = jnp.argsort(dst, stable=True)
        src = src[_o]
        dst = dst[_o]
        edge_weight = jax.random.uniform(jax.random.fold_in(_gk, 12), (100000,), jnp.float32, 0.0, 0.999999)
        return (x, src, dst, edge_weight)
    x, src, dst, edge_weight = _rec_inputs()

    def _L0_gnn_setup():
        import jax, jax.numpy as jnp
        import numpy as np
        N_NODES = 6250

        def _gcn_norm(edge_index, num_nodes):
            src, dst = (edge_index[0], edge_index[1])
            loop = jnp.arange(num_nodes, dtype=src.dtype)
            src = jnp.concatenate([src, loop])
            dst = jnp.concatenate([dst, loop])
            ones = jnp.ones(src.shape[0], dtype=jnp.float32)
            deg = jax.ops.segment_sum(ones, dst, num_segments=num_nodes)
            dinv = jnp.where(deg > 0, jax.lax.rsqrt(deg), 0.0)
            norm = dinv[src] * dinv[dst]
            return (src, dst, norm)

        def _gcn_layer(x, W, b, src, dst, norm, num_nodes):
            h = x @ W
            msg = h[src] * norm[:, None]
            out = jax.ops.segment_sum(msg, dst, num_segments=num_nodes)
            return out + b
        key = jax.random.key(seed)
        ks = jax.random.split(key, 5)
        F_in, H = (128, 128)
        x = jax.random.normal(ks[0], (N_NODES, F_in), dtype=jnp.float32)
        edge_index = jax.random.randint(ks[1], (2, 100000), 0, N_NODES, dtype=jnp.int64)
        s = 1.0 / np.sqrt(F_in)
        W1 = jax.random.normal(ks[2], (F_in, H), dtype=jnp.float32) * s
        W2 = jax.random.normal(ks[3], (H, H), dtype=jnp.float32) * s
        W3 = jax.random.normal(ks[4], (H, H), dtype=jnp.float32) * s
        b1 = jnp.zeros((H,), jnp.float32)
        b2 = jnp.zeros((H,), jnp.float32)
        b3 = jnp.zeros((H,), jnp.float32)
        return {'x': x, 'edge_index': edge_index, 'W1': W1, 'b1': b1, 'W2': W2, 'b2': b2, 'W3': W3, 'b3': b3}
    _L0_gnn_all = _L0_gnn_setup()
    _L0_gnn_in = {k: v for k, v in _L0_gnn_all.items() if k in ('W1', 'b1', 'W2', 'b2', 'W3', 'b3')}
    del _L0_gnn_all

    def _L1_gnn_setup():
        import jax, jax.numpy as jnp
        import numpy as np
        N, E = (3125, 100000)
        IN_CH, HEADS, OUT_PER_HEAD = (128, 4, 32)
        NEG_SLOPE = 0.2
        key = jax.random.key(seed)
        ks = jax.random.split(key, 10)
        HC = HEADS * OUT_PER_HEAD
        glorot = lambda k, shape: jax.random.uniform(k, shape, jnp.float32, -1.0, 1.0) * jnp.sqrt(6.0 / (shape[0] + shape[-1]))
        return {'x': jax.random.normal(ks[0], (N, IN_CH), jnp.float32), 'edge_index': jax.random.randint(ks[1], (2, E), 0, N), 'edge_weight': jax.random.uniform(ks[2], (E,), jnp.float32), 'Wl': glorot(ks[3], (IN_CH, HC)), 'bl': jnp.zeros((HC,), jnp.float32), 'Wr': glorot(ks[4], (IN_CH, HC)), 'br': jnp.zeros((HC,), jnp.float32), 'We': glorot(ks[5], (1, HC)), 'att': glorot(ks[6], (HEADS, OUT_PER_HEAD)), 'bias': jnp.zeros((HC,), jnp.float32)}
    _L1_gnn_all = _L1_gnn_setup()
    _L1_gnn_in = {k: v for k, v in _L1_gnn_all.items() if k in ('Wl', 'bl', 'Wr', 'br', 'We', 'att', 'bias')}
    del _L1_gnn_all

    def _L2_gnn_setup():
        import jax, jax.numpy as jnp
        import numpy as np
        N_NODES = 3125
        N_EDGES = 100000
        IN_DIM, HID_DIM, OUT_DIM = (128, 256, 128)

        def _sage_conv(x, src, dst, Wl, bl, Wr, n_nodes):
            agg = jax.ops.segment_sum(x[src], dst, num_segments=n_nodes)
            deg = jax.ops.segment_sum(jnp.ones_like(dst, dtype=x.dtype), dst, num_segments=n_nodes)
            mean = agg / jnp.maximum(deg, 1.0)[:, None]
            return mean @ Wl + bl + x @ Wr
        key = jax.random.key(seed)
        ks = jax.random.split(key, 8)
        x = jax.random.normal(ks[0], (N_NODES, IN_DIM), dtype=jnp.float32)
        edge_index = jax.random.randint(ks[1], (2, N_EDGES), 0, N_NODES, dtype=jnp.int64)
        s = 0.05
        Wl1 = jax.random.normal(ks[2], (IN_DIM, HID_DIM), dtype=jnp.float32) * s
        bl1 = jnp.zeros((HID_DIM,), dtype=jnp.float32)
        Wr1 = jax.random.normal(ks[3], (IN_DIM, HID_DIM), dtype=jnp.float32) * s
        Wl2 = jax.random.normal(ks[4], (HID_DIM, OUT_DIM), dtype=jnp.float32) * s
        bl2 = jnp.zeros((OUT_DIM,), dtype=jnp.float32)
        Wr2 = jax.random.normal(ks[5], (HID_DIM, OUT_DIM), dtype=jnp.float32) * s
        return {'x': x, 'edge_index': edge_index, 'Wl1': Wl1, 'bl1': bl1, 'Wr1': Wr1, 'Wl2': Wl2, 'bl2': bl2, 'Wr2': Wr2}
    _L2_gnn_all = _L2_gnn_setup()
    _L2_gnn_in = {k: v for k, v in _L2_gnn_all.items() if k in ('Wl1', 'bl1', 'Wr1', 'Wl2', 'bl2', 'Wr2')}
    del _L2_gnn_all

    def _L3_gnn_setup():
        import jax, jax.numpy as jnp
        import numpy as np
        N_NODES = 3125
        N_EDGES = 37500
        D = 128
        key = jax.random.key(seed)
        k1, k2, k3, k4, k5, k6 = jax.random.split(key, 6)
        x = jax.random.normal(k1, (N_NODES, D), dtype=jnp.float32)
        edge_index = jax.random.randint(k2, (2, N_EDGES), 0, N_NODES, dtype=jnp.int64)
        bound = 1.0 / np.sqrt(D)
        W1 = jax.random.uniform(k3, (D, D), minval=-bound, maxval=bound, dtype=jnp.float32)
        b1 = jax.random.uniform(k4, (D,), minval=-bound, maxval=bound, dtype=jnp.float32)
        W2 = jax.random.uniform(k5, (D, D), minval=-bound, maxval=bound, dtype=jnp.float32)
        b2 = jax.random.uniform(k6, (D,), minval=-bound, maxval=bound, dtype=jnp.float32)
        return {'x': x, 'edge_index': edge_index, 'W1': W1, 'b1': b1, 'W2': W2, 'b2': b2}
    _L3_gnn_all = _L3_gnn_setup()
    _L3_gnn_in = {k: v for k, v in _L3_gnn_all.items() if k in ('W1', 'b1', 'W2', 'b2')}
    del _L3_gnn_all
    return {'x': x, 'src': src, 'dst': dst, 'edge_weight': edge_weight, 'L0_gnn_W1': _L0_gnn_in['W1'], 'L0_gnn_b1': _L0_gnn_in['b1'], 'L0_gnn_W2': _L0_gnn_in['W2'], 'L0_gnn_b2': _L0_gnn_in['b2'], 'L0_gnn_W3': _L0_gnn_in['W3'], 'L0_gnn_b3': _L0_gnn_in['b3'], 'L1_gnn_Wl': _L1_gnn_in['Wl'], 'L1_gnn_bl': _L1_gnn_in['bl'], 'L1_gnn_Wr': _L1_gnn_in['Wr'], 'L1_gnn_br': _L1_gnn_in['br'], 'L1_gnn_We': _L1_gnn_in['We'], 'L1_gnn_att': _L1_gnn_in['att'], 'L1_gnn_bias': _L1_gnn_in['bias'], 'L2_gnn_Wl1': _L2_gnn_in['Wl1'], 'L2_gnn_bl1': _L2_gnn_in['bl1'], 'L2_gnn_Wr1': _L2_gnn_in['Wr1'], 'L2_gnn_Wl2': _L2_gnn_in['Wl2'], 'L2_gnn_bl2': _L2_gnn_in['bl2'], 'L2_gnn_Wr2': _L2_gnn_in['Wr2'], 'L3_gnn_W1': _L3_gnn_in['W1'], 'L3_gnn_b1': _L3_gnn_in['b1'], 'L3_gnn_W2': _L3_gnn_in['W2'], 'L3_gnn_b2': _L3_gnn_in['b2']}

def reference(x, src, dst, edge_weight, L0_gnn_W1, L0_gnn_b1, L0_gnn_W2, L0_gnn_b2, L0_gnn_W3, L0_gnn_b3, L1_gnn_Wl, L1_gnn_bl, L1_gnn_Wr, L1_gnn_br, L1_gnn_We, L1_gnn_att, L1_gnn_bias, L2_gnn_Wl1, L2_gnn_bl1, L2_gnn_Wr1, L2_gnn_Wl2, L2_gnn_bl2, L2_gnn_Wr2, L3_gnn_W1, L3_gnn_b1, L3_gnn_W2, L3_gnn_b2):
    import jax
    import jax.numpy as jnp

    def _L0_gnn_ref(x, edge_index, W1, b1, W2, b2, W3, b3):
        import jax, jax.numpy as jnp
        import numpy as np
        N_NODES = 6250

        def _gcn_norm(edge_index, num_nodes):
            src, dst = (edge_index[0], edge_index[1])
            loop = jnp.arange(num_nodes, dtype=src.dtype)
            src = jnp.concatenate([src, loop])
            dst = jnp.concatenate([dst, loop])
            ones = jnp.ones(src.shape[0], dtype=jnp.float32)
            deg = jax.ops.segment_sum(ones, dst, num_segments=num_nodes)
            dinv = jnp.where(deg > 0, jax.lax.rsqrt(deg), 0.0)
            norm = dinv[src] * dinv[dst]
            return (src, dst, norm)

        def _gcn_layer(x, W, b, src, dst, norm, num_nodes):
            h = x @ W
            msg = h[src] * norm[:, None]
            out = jax.ops.segment_sum(msg, dst, num_segments=num_nodes)
            return out + b
        num_nodes = x.shape[0]
        src, dst, norm = _gcn_norm(edge_index, num_nodes)
        h = _gcn_layer(x, W1, b1, src, dst, norm, num_nodes)
        h = jax.nn.relu(h)
        h = _gcn_layer(h, W2, b2, src, dst, norm, num_nodes)
        h = jax.nn.relu(h)
        h = _gcn_layer(h, W3, b3, src, dst, norm, num_nodes)
        return h

    def _L1_gnn_ref(x, edge_index, edge_weight, Wl, bl, Wr, br, We, att, bias):
        import jax, jax.numpy as jnp
        import numpy as np
        N, E = (3125, 100000)
        IN_CH, HEADS, OUT_PER_HEAD = (128, 4, 32)
        NEG_SLOPE = 0.2
        n = x.shape[0]
        H, C = att.shape
        src, dst = (edge_index[0], edge_index[1])
        loop_attr = jax.ops.segment_max(edge_weight, dst, num_segments=n)
        loop_attr = jnp.where(jnp.isfinite(loop_attr), loop_attr, 0.0)
        loop = jnp.arange(n)
        src_f = jnp.concatenate([src, loop])
        dst_f = jnp.concatenate([dst, loop])
        ea_f = jnp.concatenate([edge_weight, loop_attr])[:, None]
        x_l = (x @ Wl + bl).reshape(n, H, C)
        x_r = (x @ Wr + br).reshape(n, H, C)
        e = (ea_f @ We).reshape(-1, H, C)
        m = jax.nn.leaky_relu(x_l[src_f] + x_r[dst_f] + e, NEG_SLOPE)
        alpha = jnp.einsum('ehc,hc->eh', m, att)
        amax = jax.ops.segment_max(alpha, dst_f, num_segments=n)
        amax = jnp.where(jnp.isfinite(amax), amax, 0.0)
        aexp = jnp.exp(alpha - amax[dst_f])
        asum = jax.ops.segment_sum(aexp, dst_f, num_segments=n)
        alpha = aexp / (asum[dst_f] + 1e-16)
        out = jax.ops.segment_sum(x_l[src_f] * alpha[..., None], dst_f, num_segments=n)
        return out.reshape(n, H * C) + bias

    def _L2_gnn_ref(x, edge_index, Wl1, bl1, Wr1, Wl2, bl2, Wr2):
        import jax, jax.numpy as jnp
        import numpy as np
        N_NODES = 3125
        N_EDGES = 100000
        IN_DIM, HID_DIM, OUT_DIM = (128, 256, 128)

        def _sage_conv(x, src, dst, Wl, bl, Wr, n_nodes):
            agg = jax.ops.segment_sum(x[src], dst, num_segments=n_nodes)
            deg = jax.ops.segment_sum(jnp.ones_like(dst, dtype=x.dtype), dst, num_segments=n_nodes)
            mean = agg / jnp.maximum(deg, 1.0)[:, None]
            return mean @ Wl + bl + x @ Wr
        src, dst = (edge_index[0], edge_index[1])
        n = x.shape[0]
        h = _sage_conv(x, src, dst, Wl1, bl1, Wr1, n)
        h = jax.nn.relu(h)
        out = _sage_conv(h, src, dst, Wl2, bl2, Wr2, n)
        return out

    def _L3_gnn_ref(x, edge_index, W1, b1, W2, b2):
        import jax, jax.numpy as jnp
        import numpy as np
        N_NODES = 3125
        N_EDGES = 37500
        D = 128
        row, col = (edge_index[0], edge_index[1])
        n = x.shape[0]
        deg = jax.ops.segment_sum(jnp.ones(row.shape, dtype=x.dtype), row, num_segments=n)
        deg = jnp.maximum(deg, 1.0)[:, None]
        agg = jax.ops.segment_sum(x[col], row, num_segments=n)
        h = jax.nn.relu(agg / deg @ W1.T + b1)
        agg2 = jax.ops.segment_sum(h[col], row, num_segments=n)
        return jax.nn.relu(agg2 / deg @ W2.T + b2)
    edge_index = jnp.stack([src, dst])
    x = _layernorm(x + _L0_gnn_ref(x, edge_index, L0_gnn_W1, L0_gnn_b1, L0_gnn_W2, L0_gnn_b2, L0_gnn_W3, L0_gnn_b3), axis=-1)
    x = _layernorm(x + _L1_gnn_ref(x, edge_index, edge_weight, L1_gnn_Wl, L1_gnn_bl, L1_gnn_Wr, L1_gnn_br, L1_gnn_We, L1_gnn_att, L1_gnn_bias), axis=-1)
    x = _layernorm(x + _L2_gnn_ref(x, edge_index, L2_gnn_Wl1, L2_gnn_bl1, L2_gnn_Wr1, L2_gnn_Wl2, L2_gnn_bl2, L2_gnn_Wr2), axis=-1)
    x = _layernorm(x + _L3_gnn_ref(x, edge_index, L3_gnn_W1, L3_gnn_b1, L3_gnn_W2, L3_gnn_b2), axis=-1)
    return x

_drawn_inputs = setup_inputs


def setup_inputs(seed=0):
    import zlib

    import numpy as np

    out = dict(_drawn_inputs(seed))
    spreads = {'L0_gnn_b1': (0.0, 0.1),
     'L0_gnn_b2': (0.0, 0.1),
     'L0_gnn_b3': (0.0, 0.1),
     'L1_gnn_bl': (0.0, 0.1),
     'L1_gnn_br': (0.0, 0.632),
     'L1_gnn_bias': (0.0, 0.1),
     'L2_gnn_bl1': (0.0, 0.1),
     'L2_gnn_bl2': (0.0, 0.1)}
    factors = {'edge_weight': 5.317, 'L0_gnn_W1': 4.272, 'L1_gnn_We': 4.655, 'L3_gnn_b1': 3.666}
    for name, (base, spread) in spreads.items():
        noise = np.random.default_rng([zlib.crc32(name.encode()), seed]).standard_normal(out[name].shape)
        drawn = base * np.exp(spread * noise) if base else spread * noise
        out[name] = jnp.asarray(drawn.astype(out[name].dtype))
    for name, factor in factors.items():
        out[name] = (out[name] * factor).astype(out[name].dtype)
    return out
```

```python
from contextlib import ExitStack

import concourse.bass as bass
from concourse import mybir

ALU = mybir.AluOpType
ACT = mybir.ActivationFunctionType
AX = mybir.AxisListType
F32 = mybir.dt.float32
I32 = mybir.dt.int32
U32 = mybir.dt.uint32

P = 128
U = 8
RING = 4
EPS = 1e-5
FAR = 1 << 20


def build(nc, x, src, dst, edge_weight, W1, b1, W2, b2, W3, b3, gWl, gbl, gWr, gbr, gWe, gatt, gbias,
          sWl1, sbl1, sWr1, sWl2, sbl2, sWr2, mW1, mb1, mW2, mb2, out):
    N, D = x.shape
    E = src.shape[0]
    H, HC = gatt.shape
    HID = sWl1.shape[1]
    TILES = -(-N // P)
    CHUNKS = -(-E // P)
    VISITS = -(-(CHUNKS + TILES - 1) // (U * RING)) * U * RING
    GROUPS = VISITS // U
    ROUNDS = GROUPS // RING
    VT = -(-VISITS // P)
    COLS = -(-E // (P * 16)) * 16
    EPAD = COLS * P
    CH2 = EPAD // P
    NPAD = TILES * P
    BINS = TILES + 1
    NODES_LAST = N - (TILES - 1) * P
    TW = TILES * P
    assert D == P and CH2 >= CHUNKS and COLS % 16 == 0

    ctx = ExitStack()
    with ctx:
        def sb(name, shape, dt=F32):
            return ctx.enter_context(nc.sbuf_tensor(name, shape, dt))

        def pb(name, shape, dt=F32):
            return ctx.enter_context(nc.psum_tensor(name, shape, dt))

        def sem(name):
            return ctx.enter_context(nc.semaphore(name))

        def dram(name, shape, dt=F32):
            return nc.dram_tensor(name, shape, dt, kind="Internal").ap()

        tab = [dram(f"tab{k}", (NPAD, D)) for k in range(8)]
        edge_key = dram("edge_key", (CH2, P), I32)
        edge_oth = dram("edge_oth", (CH2, P), I32)
        gathered = dram("gathered", (VISITS // U * P, U * D))
        edge_w = dram("edge_w", (CH2, P))
        pairs = dram("pairs", (EPAD, 2), I32)

        BIG = 1e30
        ident = sb("ident", [P, P])
        ones = sb("ones", [P, P])
        lower = sb("lower", [P, P])
        zeros = sb("zeros", [P, P])
        epsb = sb("epsb", [P, 1])
        iota_f = sb("iota_f", [P, COLS])
        vcol_i = sb("vcol_i", [P, VT], I32)
        vcol = sb("vcol", [P, VT])
        X = sb("X", [P, TILES, D])
        EXT = H + H + 1
        GW = D + EXT
        EXT0 = -(-TILES * GW // 64) * 64
        big = sb("big", [P, max(EXT0 + VISITS * EXT, 2 * TW)])
        acc = big[:, 0:TW].rearrange("p (t f) -> p t f", f=D)
        Y = big[:, TW:2 * TW].rearrange("p (t f) -> p t f", f=D)
        accG = big[:, 0:TILES * GW]
        ext = big[:, EXT0:EXT0 + VISITS * EXT].rearrange("p (v a) -> p v a", a=EXT)
        Z = sb("Z", [P, TILES, D])
        V = sb("V", [P, TILES, D])
        diag = sb("diag", [P, 2, U, P])
        msg = sb("msg", [P, RING, U, D])
        oh = sb("oh", [P, 2, U, P])
        idxA = sb("idxA", [P, VT * P], I32)
        relA = sb("relA", [P, VT * P])
        idxB = sb("idxB", [P, VT * P], I32)
        relB = sb("relB", [P, VT * P])
        wA = sb("wA", [P, VT * P])
        tvA = sb("tvA", [1, VT * P], I32)
        tvB = sb("tvB", [1, VT * P], I32)
        stage = sb("stage", [P, 6 * U], I32)
        W = sb("W", [P, 15, D])
        bcol = sb("bcol", [P, 2])
        brow = sb("brow", [P, 11, D])
        degin = sb("degin", [P, TILES])
        dinv = sb("dinv", [P, TILES])
        degout = sb("degout", [P, TILES])
        hasin = sb("hasin", [P, TILES])
        stat = sb("stat", [P, 3, TILES])

        banks = pb("banks", [P, 8, 512])
        ps = banks[:, 0:4, :].rearrange("p (h b) (u f) -> p h (b u) f", h=2, f=P)
        pm = banks[:, 4:8, :].rearrange("p (h b) n -> p h (b n)", h=2)

        s_edges = sem("s_edges")
        s_list = sem("s_list")
        s_first = sem("s_first")
        s_tv = sem("s_tv")
        s_rows = sem("s_rows")
        s_scst = sem("s_scst")
        s_root = sem("s_root")
        s_doh = sem("s_doh")
        s_dmm = sem("s_dmm")
        s_deg = sem("s_deg")
        s_diag = sem("s_diag")
        s_bin = sem("s_bin")
        s_oT = sem("s_oT")
        s_oTc = sem("s_oTc")
        s_p1 = sem("s_p1")
        s_xl = sem("s_xl")
        s_xlback = sem("s_xlback")
        s_mask = sem("s_mask")
        s_exp = sem("s_exp")
        s_msgs = sem("s_msgs")
        s_const = sem("s_const")
        s_xin = sem("s_xin")
        s_w = sem("s_w")
        s_load = sem("s_load")
        s_chain = sem("s_chain")
        s_staged = sem("s_staged")
        s_pass = sem("s_pass")
        s_dpass = sem("s_dpass")
        s_gath = [sem(f"s_gath{j}") for j in range(RING)]
        s_oh = sem("s_oh")
        s_mm = sem("s_mm")
        s_add = sem("s_add")
        s_tab = sem("s_tab")
        s_pe = sem("s_pe")
        s_ev = [sem("s_ev0"), sem("s_ev1")]
        s_store = [sem(f"s_store{j}") for j in range(RING)]
        s_back = [sem(f"s_back{j}") for j in range(RING)]
        s_scat = [sem("s_scat0"), sem("s_scat1")]
        s_go = sem("s_go")
        s_out = sem("s_out")
        block = ctx.enter_context(nc.Block())
        Xf, Zf, Vf = [t[:, :, :].rearrange("p t f -> p (t f)") for t in (X, Z, V)]
        accf, Yf = big[:, 0:TW], big[:, TW:2 * TW]
        BF = mybir.dt.bfloat16
        Yi, Zi = Yf.bitcast(I32), Zf.bitcast(I32)
        dst_far, src_far, dst_zero, src_zero = [Yi[:, k * COLS:(k + 1) * COLS] for k in range(4)]
        w_row = Yf[:, 4 * COLS:5 * COLS]
        hi_i = Zi[:, 0:COLS]
        onesw = Vf[:, 5 * COLS:6 * COLS]
        hi_dst, lo_dst, hi_src, lo_src = [Zf[:, k * COLS:(k + 1) * COLS] for k in range(1, 5)]
        iota_i = Zi[:, 7 * COLS:8 * COLS]
        cum, mask = [Zf[:, k * COLS:(k + 1) * COLS] for k in (5, 6)]
        pos, posi = accf[:, 0:COLS], accf[:, COLS:2 * COLS].bitcast(I32)
        cnt, base, tot, run = [accf[:, 2 * COLS + 64 * k:2 * COLS + 64 * k + BINS] for k in range(4)]
        firsts_i = accf[0:1, 3 * COLS:4 * COLS].bitcast(I32)
        firsts = accf[0:1, 4 * COLS:5 * COLS]
        firsts_s = Zf[0:1, 7 * COLS:8 * COLS].bitcast(I32)
        before = accf[:, 5 * COLS:6 * COLS]
        cv, tv, tv128, tvc = [accf[:, 6 * COLS + 8 * k:6 * COLS + 8 * k + VT] for k in range(4)]
        cvi = accf[:, 6 * COLS + 32:6 * COLS + 32 + VT].bitcast(I32)
        tvT = accf[0:VT, 6 * COLS + 64:6 * COLS + 64 + P].bitcast(I32)
        rows = Vf[:, 0:3 * VT * P].rearrange("p (a g e) -> p g a e", a=3, g=VT)
        rowsi = Vf[:, 0:3 * VT * P].bitcast(I32).rearrange("p (a g e) -> p g a e", a=3, g=VT)
        prow = Vf[:, 0:2 * VT * P].bitcast(I32).rearrange("p (g e a) -> p g e a", g=VT, a=2)
        relR = Vf[:, 3 * VT * P:4 * VT * P].rearrange("p (g e) -> p g e", g=VT)
        othR = Vf[:, 4 * VT * P:5 * VT * P].rearrange("p (g e) -> p g e", g=VT)
        ohl = msg[:, 0, :, :].rearrange("p u f -> p (u f)").bitcast(BF).rearrange("p (b u f) -> p b u f", b=2, u=U)
        ohh = msg[:, 1, :, :].rearrange("p u f -> p (u f)").bitcast(BF).rearrange("p (b u f) -> p b u f", b=2, u=U)
        scat_pos = stage[:, 0:2 * U].rearrange("p (b u) -> p b u", b=2)
        scat_rec = stage[:, 2 * U:6 * U].rearrange("p (b u a) -> p b u a", b=2, a=2)
        deg_ps = [ps[:, b, 0, 0:TILES] for b in range(2)]

        def gsum(h, u):
            return banks[:, 4 * h + u // 3, (u % 3) * GW:(u % 3 + 1) * GW]

        extf = big[:, EXT0:EXT0 + VISITS * EXT]
        msgf = msg[:, :, :, :].rearrange("p j u f -> p (j u f)")
        VP = VT * P
        sc_a, sc_b = [Zf[:, k * U * D:(k + 1) * U * D].rearrange("p (u f) -> p u f", f=D) for k in range(2)]
        C5_ = H + 1
        A5 = Zf[:, 0:C5_ * VP].rearrange("p (c g e) -> p c g e", c=C5_, g=VT)
        F5 = big[:, 0:C5_ * VP].rearrange("p (c g e) -> p c g e", c=C5_, g=VT)
        keyR, penF, penB, lastR = [msgf[:, k * VP:(k + 1) * VP].rearrange("p (g e) -> p g e", g=VT) for k in range(4)]
        ohf = oh[:, :, :, :].rearrange("p b u f -> p (b u f)")
        ends = msgf[:, 4 * VP:4 * VP + 5 * VT * C5_].rearrange("p (q g c) -> p q g c", q=5, g=VT)
        backs = msgf[:, 4 * VP + 256:4 * VP + 256 + 3 * VT * C5_].rearrange("p (q g c) -> p q g c", q=3, g=VT)
        lastT = ohf[:, 0:VP]
        tmpR = ohf[:, VP:2 * VP].rearrange("p (g e) -> p g e", g=VT)
        diagf = diag[:, :, :, :].rearrange("p b u f -> p (b u f)")
        rowbuf = [Zf[0:C5_, C5_ * VP:(C5_ + 1) * VP], Zf[0:C5_, (C5_ + 1) * VP:(C5_ + 2) * VP],
                  big[0:C5_, C5_ * VP:(C5_ + 1) * VP], big[0:C5_, (C5_ + 1) * VP:(C5_ + 2) * VP],
                  diagf[0:C5_, 0:VP], diagf[0:C5_, VP:2 * VP]]
        crow = [rowbuf[4], rowbuf[2], rowbuf[3]]
        small = [msgf[:, k * TILES * H:(k + 1) * TILES * H].rearrange("p (t h) -> p t h", h=H) for k in range(6)]
        c12 = msgf[:, 0:2 * TILES * H]
        selfT = big[:, EXT0:EXT0 + TW].rearrange("p (t f) -> p t f", f=D)

        def pmv(h, n=7):
            return pm[:, h, 0:n * P].rearrange("p (t f) -> p t f", f=P)

        STAGES = [("bins", 1), ("broadcast A", 1), ("relA", 1), ("idxA", 1), ("weights", 1), ("tvA", 1),
                  ("broadcast B", 1), ("relB", 1), ("idxB", 1), ("tvB", 1), ("turn mW", 1)]
        BT = 7
        NB = TILES // BT
        assert NB * BT == TILES
        for k in range(3):
            STAGES += [(f"self {k}", NB), (f"gcn {k}", NB)]
        STAGES += [("turn X1", NB), ("x_l", NB), ("x_r", NB), ("rows of keys", 1), ("rows of weights", 1)]
        STAGES += [(f"rows of scores {h}", 1) for h in range(H)]
        STAGES += [(f"ends {q}", 1) for q in range(5)] + [(f"carries {q}", 1) for q in range(3)]
        C5 = H + 1
        STAGES += [("lasts", 1)] + [(f"largest {c}", 1) for c in range(C5)]
        STAGES += [("turn X", NB), ("rdeg", NB), ("hidden", 26), ("p", NB), ("q", NB), ("mean 0", NB), ("mean 1", NB)]
        BATCH, n0 = {}, 0
        for name, n in STAGES:
            BATCH[name] = n0
            n0 += n

        GO = ["halves", "counts", "positions", "firsts A", "cvA", "tv sources A", "tvT A", "degrees",
              "firsts B", "cvB", "tv sources B", "tvT B",
              "table 0", "table 1", "table 2", "var 0", "x1", "x_l", "carry sources", "carries", "largest", "shifted", "self shifted", "var 1", "x2",
              "scaled", "p ready", "var 2", "x3", "h3", "var 3", "x4"]

        def gathers_before(k):
            return k - (k > 4)

        def go(name):
            return GO.index(name) + 1

        @block.sync
        def _(sp):
            def row_layout(to, of, rows_, s):
                full = E // COLS
                sp.dma_start(to[0:full, :], of[0:full * COLS].rearrange("(p c) -> p c", c=COLS)).then_inc(s, 16)
                sp.dma_start(to[full:full + 1, 0:E - full * COLS],
                             of[full * COLS:E].rearrange("(p c) -> p c", p=1)).then_inc(s, 16)

            sp.wait_ge(s_const, 15)
            for to, of in ((dst_far, dst), (src_far, src), (dst_zero, dst), (src_zero, src), (w_row, edge_weight)):
                row_layout(to, of, COLS, s_edges)
            sp.dma_start(X[:, 0:TILES - 1, :], x[0:(TILES - 1) * P, :].rearrange("(t p) f -> p t f", p=P)).then_inc(s_xin, 16)
            sp.dma_start(X[0:NODES_LAST, TILES - 1, :], x[(TILES - 1) * P:N, :]).then_inc(s_xin, 16)
            for k, w in enumerate((W1, W2, W3, gWl, gWr)):
                sp.dma_start(W[:, k, :], w).then_inc(s_w, 16)
            for k, w in ((5, sWl1), (7, sWr1)):
                sp.dma_start(W[:, k:k + 2, :], w.rearrange("f (a b) -> f a b", a=2)).then_inc(s_w, 16)
            for k, w in ((9, sWl2), (11, sWr2)):
                sp.dma_start(W[:, k:k + 2, :], w.rearrange("(a f) b -> f a b", a=2)).then_inc(s_w, 16)
            for k, w in ((13, mW1), (14, mW2)):
                sp.dma_start(W[:, k, :], w).then_inc(s_w, 16)
            for k, b in enumerate((b1, b2, b3, sbl2, mb1, mb2, gbl, gbr, gbias, gWe.rearrange("a b -> (a b)"), gatt.rearrange("a b -> (a b)"))):
                sp.dma_start(brow[:, k, :], b.rearrange("(a f) -> a f", a=1).to_broadcast([P, D])).then_inc(s_w, 16)
            with nc.allow_non_contiguous_dma(reason="256 numbers, one to a partition"):
                sp.dma_start(bcol[:, :], sbl1.rearrange("(a f) -> f a", a=2)).then_inc(s_w, 16)
            sp.wait_ge(s_edges, 16 * 10)
            for to, of in ((edge_key, dst_far), (edge_oth, src_zero), (edge_w, w_row)):
                sp.dma_start(to.rearrange("c e -> (c e)").rearrange("(p c) -> p c", c=COLS), of).then_inc(s_list, 16)
            sp.wait_ge(s_list, 48)
            with nc.allow_non_contiguous_dma(reason="the first key of each chunk"):
                sp.dma_start(firsts_i[:, 0:CH2], edge_key[:, 0:1].rearrange("c a -> a c")).then_inc(s_first, 16)
            sp.wait_ge(s_go, go("tvT A"))
            for g in range(VT):
                sp.dma_start(tvA[0:1, g * P:(g + 1) * P], tvT[g:g + 1, :]).then_inc(s_tv, 16)
            sp.wait_ge(s_scat[0], 128 * (COLS // (2 * U)))
            sp.wait_ge(s_scat[1], 128 * (COLS // (2 * U)))
            with nc.allow_non_contiguous_dma(reason="the first key of each chunk"):
                sp.dma_start(firsts_i[:, 0:CH2], pairs.rearrange("(c e) a -> c (e a)", e=P)[:, 0:1].rearrange("c a -> a c")).then_inc(s_first, 16)
            sp.wait_ge(s_go, go("tvT B"))
            for g in range(VT):
                sp.dma_start(tvB[0:1, g * P:(g + 1) * P], tvT[g:g + 1, :]).then_inc(s_tv, 16)

            def table(k, milestone, buf):
                sp.wait_ge(s_go, go(milestone))
                sp.dma_start(tab[k].rearrange("(t p) f -> p t f", p=P), buf[:, :, :]).then_inc(s_tab, 16)

            table(0, "table 0", Y)
            table(1, "table 1", Y)
            table(2, "table 2", Y)
            table(3, "x_l", Z)
            with sp.Fori(0, ROUNDS) as i:
                for j in range(RING):
                    sp.wait_ge(s_gath[j], i * (16 * U) + 16 * U * (3 * ROUNDS + 1))
                    sp.dma_start(gathered[bass.ds(i * (RING * P) + j * P, P), :], msg[:, j, :, :].rearrange("p u f -> p (u f)")).then_inc(s_store[j], 16)
            sp.wait_ge(s_add, U * GROUPS * 4 + 2 * U)
            sp.dma_start(Z[:, :, :], tab[3].rearrange("(t p) f -> p t f", p=P)).then_inc(s_xlback, 16)
            sp.wait_ge(s_go, go("shifted"))
            sp.dma_start(Z[:, :, :], tab[3].rearrange("(t p) f -> p t f", p=P)).then_inc(s_xlback, 16)
            with sp.Fori(0, ROUNDS) as i:
                for j in range(RING):
                    sp.wait_ge(s_mm, i * RING + (4 * GROUPS + j + 1))
                    sp.dma_start(msg[:, j, :, :].rearrange("p u f -> p (u f)"), gathered[bass.ds(i * (RING * P) + j * P, P), :]).then_inc(s_back[j], 16)
            table(4, "x2", X)
            table(5, "p ready", Y)
            table(6, "x3", X)
            table(7, "h3", Y)
            sp.wait_ge(s_go, go("x4"))
            sp.dma_start(out[0:(TILES - 1) * P, :].rearrange("(t p) f -> p t f", p=P), X[:, 0:TILES - 1, :]).then_inc(s_out, 16)
            sp.dma_start(out[(TILES - 1) * P:N, :], X[0:NODES_LAST, TILES - 1, :]).then_inc(s_out, 16)
            sp.wait_ge(s_out, 32)

        @block.gpsimd
        def _(pool):
            pool.memset(dst_far, FAR).then_inc(s_const, 1)
            pool.memset(src_far, FAR).then_inc(s_const, 1)
            pool.memset(dst_zero, 0).then_inc(s_const, 1)
            pool.memset(src_zero, 0).then_inc(s_const, 1)
            pool.memset(w_row, 0.0).then_inc(s_const, 1)
            pool.memset(X[:, TILES - 1, :], 0.0).then_inc(s_const, 1)
            pool.memset(onesw, 1.0).then_inc(s_const, 1)
            pool.memset(ident[:, :], 0.0).then_inc(s_const, 1)
            pool.memset(ones[:, :], 1.0).then_inc(s_const, 1)
            pool.memset(zeros[:, :], 0.0).then_inc(s_const, 1)
            pool.memset(epsb[:, :], EPS).then_inc(s_const, 1)
            pool.iota(iota_i[:, 0:COLS], pattern=[[1, COLS]], base=0, channel_multiplier=0).then_inc(s_const, 1)
            pool.iota(vcol_i[:, :], pattern=[[P, VT]], base=0, channel_multiplier=1).then_inc(s_const, 1)
            pool.wait_ge(s_const, 13)
            pool.affine_select(out=ident[:, :], in_=ident[:, :], compare_op=ALU.not_equal, fill=1.0, base=0,
                               pattern=[[-1, P]], channel_multiplier=1).then_inc(s_const, 1)
            pool.affine_select(out=lower[:, :], in_=ones[:, :], compare_op=ALU.is_ge, fill=0.0, base=-1,
                               pattern=[[1, P]], channel_multiplier=-1).then_inc(s_const, 1)

            pool.wait_ge(s_go, go("cvA"))
            for g in range(VT):
                for a, of in enumerate((edge_key, edge_oth, edge_w)):
                    to = rows if a == 2 else rowsi
                    pool.indirect_dma_start(to[:, g, a, :], None, of[:, :],
                                            bass.IndirectOffsetOnAxis(ap=cvi[:, g:g + 1].bitcast(U32), axis=0)).then_inc(s_rows, 16)
            with pool.Fori(0, COLS // (2 * U)) as i:
                for b in range(2):
                    pool.wait_ge(s_scst, i * 2 + (b + 1))
                    pool.sem_inc(s_pass, 1)
                    for u in range(U):
                        pool.indirect_dma_start(pairs[:, :], bass.IndirectOffsetOnAxis(ap=scat_pos[:, b, u:u + 1].bitcast(U32), axis=0),
                                                scat_rec[:, b, u, :], None).then_inc(s_scat[b], 16)
            pool.wait_ge(s_go, go("cvB"))
            for g in range(VT):
                pool.indirect_dma_start(prow[:, g, :, :].rearrange("p e a -> p (e a)"), None,
                                        pairs.rearrange("(c e) a -> c (e a)", e=P),
                                        bass.IndirectOffsetOnAxis(ap=cvi[:, g:g + 1].bitcast(U32), axis=0)).then_inc(s_rows, 16)

            def walk(k):
                with pool.Fori(0, ROUNDS) as i:
                    for j in range(RING):
                        pool.wait_ge(s_staged, i * RING + (gathers_before(k) * GROUPS + j + 1))
                        pool.sem_inc(s_pass, 1)
                        for u in range(U):
                            pool.indirect_dma_start(msg[:, j, u, :], None, tab[gathers_before(k)][:, :],
                                                    bass.IndirectOffsetOnAxis(ap=stage[:, j * U + u:j * U + u + 1].bitcast(U32), axis=0)).then_inc(s_gath[j], 16)

            for k in (0, 1, 2, 3, 5, 6, 7, 8):
                walk(k)

        @block.scalar
        def _(act):
            def walk(k, idx):
                act.wait_ge(s_tab, 16 * (gathers_before(k) + 1))
                with act.Fori(0, ROUNDS) as i:
                    for j in range(RING):
                        act.wait_ge(s_mm, i * RING + (k * GROUPS + j + 1))
                        act.copy(stage[:, j * U:(j + 1) * U], idx[:, bass.ds(i * (RING * U) + j * U, U)]).then_inc(s_staged, 1)

            def root(milestone, of, n):
                act.wait_ge(s_go, go(milestone))
                act.activation(of, of, ACT.Sqrt).then_inc(s_root, 1)

            act.wait_ge(s_go, go("positions"))
            def stage_scatter(i, h, first):
                if not first:
                    act.wait_ge(s_scat[h], i * (16 * U))
                cols = slice(h * U, (h + 1) * U) if first else bass.ds(i * (2 * U) + h * U, U)
                act.copy(scat_rec[:, h, :, 0], src_far[:, cols])
                act.copy(scat_rec[:, h, :, 1], dst_zero[:, cols])
                act.copy(scat_pos[:, h, :], posi[:, cols]).then_inc(s_scst, 1)

            for h in range(2):
                stage_scatter(0, h, True)
            with act.Fori(1, COLS // (2 * U)) as i:
                for h in range(2):
                    stage_scatter(i, h, False)
            root("degrees", dinv[:, :], 0)
            for h in range(2):
                act.wait_ge(s_scat[h], 16 * U * (COLS // (2 * U)))
            walk(0, idxA)
            walk(1, idxA)
            walk(2, idxA)
            root("var 0", stat[:, 1, :], 1)
            act.wait_ge(s_tab, 16 * 4)
            with act.Fori(0, ROUNDS) as i:
                for j in range(RING):
                    act.wait_ge(s_add, i * (RING * U) + (U * (3 * GROUPS + j - RING + 1) + 2 * U))
                    act.copy(stage[:, j * U:(j + 1) * U], idxA[:, bass.ds(i * (RING * U) + j * U, U)]).then_inc(s_staged, 1)
                    act.wait_ge(s_oT, i * RING + (j + 1))
                    act.copy(diag[:, j % 2, :, :], pm[:, j % 2, :].rearrange("p (u f) -> p u f", f=P)).then_inc(s_oTc, 1)
            act.wait_ge(s_go, go("shifted"))
            act.activation(ext[:, :, 0:H], ext[:, :, 0:H], ACT.Exp).then_inc(s_exp, 1)
            act.wait_ge(s_go, go("self shifted"))
            act.activation(c12, c12, ACT.Exp).then_inc(s_exp, 1)
            root("var 1", stat[:, 1, :], 0)
            walk(5, idxA)
            act.wait_ge(s_w, 16 * 23)
            for n in range(26):
                b = BATCH["hidden"] + n
                act.wait_ge(s_pe, b + 1)
                a, c = n // 13, n % 13
                w = min(512, TW - c * 512)
                act.activation((Vf if a == 0 else Zf)[:, c * 512:c * 512 + w], pm[:, b % 2, 0:w], ACT.Relu,
                               bias=bcol[:, a:a + 1]).then_inc(s_ev[b % 2], 1)
            walk(6, idxA)
            root("var 2", stat[:, 1, :], 2)
            walk(7, idxB)
            walk(8, idxB)
            root("var 3", stat[:, 1, :], 3)

        @block.tensor
        def _(pe):
            pe.sem_inc(s_mm, RING)
            pe.sem_inc(s_dmm, 2)
            pe.wait_ge(s_const, 15)

            def room(b):
                if b >= 2:
                    pe.wait_ge(s_ev[b % 2], (b - 2) // 2 + 1)

            def turns(stage_name, n, of, height=P):
                for k in range(-(-n // BT)):
                    b = BATCH[stage_name] + k
                    room(b)
                    for i in range(min(BT, n - k * BT)):
                        m = of(k * BT + i)
                        last = pe.transpose(pm[0:m.shape[1], b % 2, i * P:i * P + m.shape[0]], m, ident[0:m.shape[0], 0:m.shape[0]])
                    last.then_inc(s_pe, 1)

            def lists(name, mats):
                b = BATCH["broadcast " + name]
                pe.wait_ge(s_go, go("firsts " + name))
                room(b)
                pe.matmul(pm[:, b % 2, 0:512], ones[0:1, :], firsts[:, 0:512], start=True, stop=True)
                pe.matmul(pm[:, b % 2, 512:COLS], ones[0:1, :], firsts[:, 512:COLS], start=True, stop=True).then_inc(s_pe, 1)
                pe.wait_ge(s_go, go("tv sources " + name))
                for stage_name, of in mats:
                    turns(stage_name, VT, of)
                turns("tv" + name, 1, lambda i: tvc)

            b = BATCH["bins"]
            pe.wait_ge(s_go, go("counts"))
            room(b)
            pe.matmul(pm[:, b % 2, 0:BINS], lower[:, :], cnt, start=True, stop=True)
            pe.matmul(pm[:, b % 2, 512:512 + BINS], ones[:, :], cnt, start=True, stop=True).then_inc(s_pe, 1)
            for b in range(2):
                pe.matmul(deg_ps[b], zeros[:, :], zeros[:, 0:TILES], start=True, stop=False, skip_group_check=True)
            for b in range(2):
                with pe.Fori(0, COLS // (2 * U)) as i:
                    for h in range(2):
                        pe.wait_ge(s_doh, i * 2 + (b * (COLS // U) + h + 1))
                        for u in range(U):
                            last = pe.matmul(deg_ps[b], ohl[:, h, u, :], ohh[:, h, u, 0:TILES], start=False, stop=False, skip_group_check=True)
                        last.then_inc(s_dmm, 1)
            for b in range(2):
                last = pe.matmul(deg_ps[b], zeros[:, :], zeros[:, 0:TILES], start=False, stop=True, skip_group_check=True)
            last.then_inc(s_deg, 1)

            lists("A", (("relA", lambda g: relR[:, g, :]), ("idxA", lambda g: othR[:, g, :]), ("weights", lambda g: rows[:, g, 2, :])))
            lists("B", (("relB", lambda g: relR[:, g, :]), ("idxB", lambda g: othR[:, g, :])))
            pe.wait_ge(s_w, 16 * 23)
            turns("turn mW", 2, lambda i: W[:, 13 + i, :])

            def walk(k, nodes_first):
                with pe.Fori(0, ROUNDS) as i:
                    for j in range(RING):
                        G = i * RING + (k * GROUPS + j)
                        pe.wait_ge(s_oh, i * RING + (k * (GROUPS + 1) + j + 1))
                        pe.wait_ge(s_add, G * U + U)
                        pe.wait_ge(s_gath[j], i * (16 * U) + 16 * U * (gathers_before(k) * ROUNDS + 1))
                        for u in range(U):
                            if nodes_first:
                                last = pe.matmul(ps[:, j % 2, u, :], oh[:, j % 2, u, :], msg[:, j, u, :], start=True, stop=True)
                            else:
                                last = pe.matmul(ps[:, j % 2, u, :], msg[:, j, u, :], oh[:, j % 2, u, :], start=True, stop=True)
                        last.then_inc(s_mm, 1)

            def products(stage_name, pairs_of):
                for k in range(NB):
                    b = BATCH[stage_name] + k
                    room(b)
                    for i in range(BT):
                        ab = pairs_of(k * BT + i)
                        for n, (lhsT, rhs) in enumerate(ab):
                            last = pe.matmul(pm[:, b % 2, i * P:(i + 1) * P], lhsT, rhs, start=(n == 0), stop=(n == len(ab) - 1))
                    last.then_inc(s_pe, 1)

            def passed(k):
                pe.wait_ge(s_add, U * GROUPS * (k + 1) + 2 * U)

            for k in range(3):
                pe.wait_ge(s_go, go(f"table {k}"))
                turns(f"self {k}", TILES, lambda t: Y[:, t, :])
                walk(k, False)
                passed(k)
                products(f"gcn {k}", lambda t: [(acc[:, t, :], W[:, k, :])])
            pe.wait_ge(s_go, go("x1"))
            turns("turn X1", TILES, lambda t: X[:, t, :])
            for h in range(2):
                pe.wait_ge(s_ev[h], (BATCH["x_l"] + 1 - h) // 2)
            products("x_l", lambda t: [(Y[:, t, :], W[:, 3, :])])
            products("x_r", lambda t: [(Y[:, t, :], W[:, 4, :])])
            for h in range(2):
                pe.wait_ge(s_ev[h], (BATCH["rows of keys"] + 1 - h) // 2)
            with pe.Fori(0, ROUNDS) as i:
                for j in range(RING):
                    G = i * RING + (3 * GROUPS + j)
                    pe.wait_ge(s_oh, i * RING + (3 * (GROUPS + 1) + j + 1))
                    for u in range(U):
                        last = pe.transpose(pm[:, j % 2, u * P:(u + 1) * P], oh[:, j % 2, u, :], ident[:, :])
                    last.then_inc(s_oT, 1)
                    tiles = [pe.value_load(tvA[0:1, bass.ds(i * (RING * U) + (j * U + u), 1)], min_val=0, max_val=TILES - 1) for u in range(U)]
                    pe.wait_ge(s_oTc, i * RING + (j + 1))
                    pe.wait_ge(s_add, G * U + U)
                    for u, t in enumerate(tiles):
                        last = pe.matmul(ps[:, j % 2, u, :], diag[:, j % 2, u, :], Vf[:, bass.ds(t * P, P)], start=True, stop=True)
                    last.then_inc(s_mm, 1)

            pe.wait_ge(s_add, U * GROUPS * 4 + 2 * U)
            turns("rows of keys", VT, lambda g: relA[:, g * P:(g + 1) * P])
            turns("rows of weights", VT, lambda g: wA[:, g * P:(g + 1) * P])
            for h in range(H):
                turns(f"rows of scores {h}", VT, lambda g: ext[:, g * P:min((g + 1) * P, VISITS), h])
            pe.wait_ge(s_go, go("carry sources"))
            for q in range(5):
                turns(f"ends {q}", VT, lambda g: ends[:, q, g, :])
            pe.wait_ge(s_go, go("carries"))
            for q in range(3):
                turns(f"carries {q}", VT, lambda g: crow[q][:, g * P:(g + 1) * P])
            pe.wait_ge(s_go, go("largest"))
            turns("lasts", VT, lambda g: lastR[:, g, :])
            for c in range(C5):
                turns(f"largest {c}", VT, lambda g: F5[:, c, g, :])

            for h in range(2):
                pe.wait_ge(s_ev[h], (BATCH["turn X"] + 1 - h) // 2)
            with pe.Fori(0, ROUNDS) as i:
                for j in range(RING):
                    G = i * RING + (4 * GROUPS + j)
                    pe.wait_ge(s_oh, i * RING + (4 * (GROUPS + 1) + j + 1))
                    pe.wait_ge(s_add, G * U + U)
                    pe.wait_ge(s_msgs, i * RING + (j + 1))
                    for u in range(U):
                        to = gsum(j % 2, u)
                        pe.matmul(to[:, 0:D], oh[:, j % 2, u, :], msg[:, j, u, :], start=True, stop=True)
                        last = pe.matmul(to[:, D:GW], oh[:, j % 2, u, :], extf[:, bass.ds(i * (RING * U * EXT) + (j * U + u) * EXT, EXT)], start=True, stop=True)
                    last.then_inc(s_mm, 1)
            passed(4)

            pe.wait_ge(s_go, go("x2"))
            turns("turn X", TILES, lambda t: X[:, t, :])
            walk(5, False)
            passed(5)
            for n in range(NB):
                b = BATCH["rdeg"] + n
                room(b)
                pe.wait_ge(s_diag, n + 1)
                for i in range(BT):
                    last = pe.matmul(pm[:, b % 2, i * P:(i + 1) * P], ones[:, :], diag[:, n % 2, i, :], start=True, stop=True)
                last.then_inc(s_pe, 1)
            pe.wait_ge(s_go, go("scaled"))
            for n in range(26):
                b = BATCH["hidden"] + n
                a, c = n // 13, n % 13
                w = min(512, TW - c * 512)
                room(b)
                pe.matmul(pm[:, b % 2, 0:w], W[:, 5 + a, :], accf[:, c * 512:c * 512 + w], start=True, stop=False)
                pe.matmul(pm[:, b % 2, 0:w], W[:, 7 + a, :], Yf[:, c * 512:c * 512 + w], start=False, stop=True).then_inc(s_pe, 1)
            for b in range(2):
                pe.wait_ge(s_ev[b], (BATCH["p"] + 1 - b) // 2)
            products("p", lambda t: [(V[:, t, :], W[:, 9, :]), (Z[:, t, :], W[:, 10, :])])
            products("q", lambda t: [(V[:, t, :], W[:, 11, :]), (Z[:, t, :], W[:, 12, :])])
            walk(6, True)
            walk(7, False)
            passed(7)
            products("mean 0", lambda t: [(acc[:, t, :], W[:, 13, :])])
            walk(8, False)
            passed(8)
            products("mean 1", lambda t: [(acc[:, t, :], W[:, 14, :])])

        @block.vector
        def _(dve):
            n_chain = [0]
            n_go = [0]

            def link(ins):
                n_chain[0] += 1
                ins.then_inc(s_chain, 1)
                dve.wait_ge(s_chain, n_chain[0])

            def reached(name):
                n_go[0] += 1
                assert go(name) == n_go[0], name
                dve.sem_inc(s_go, 1)

            def wide(a, n=D):
                return a.rearrange("p (t o) -> p t o", o=1).to_broadcast([P, a.shape[1], n])

            def over(a, n=TILES):
                return a.rearrange("p (o f) -> p o f", o=1).to_broadcast([P, n, a.shape[1]])

            dve.sem_inc(s_add, 2 * U)
            dve.sem_inc(s_bin, 1)
            dve.wait_ge(s_const, 15)
            link(dve.tensor_copy(iota_f[:, :], iota_i[:, :]))
            link(dve.tensor_copy(vcol[:, :], vcol_i[:, :]))
            dve.wait_ge(s_edges, 16 * 10)
            for far, hi, lo in ((dst_far, hi_dst, lo_dst), (src_far, hi_src, lo_src)):
                link(dve.tensor_scalar(hi_i, far, 7, None, ALU.logical_shift_right))
                link(dve.tensor_copy(hi, hi_i))
                link(dve.tensor_copy(lo, far))
                link(dve.scalar_tensor_tensor(out=lo, in0=hi, scalar=-128.0, in1=lo, op0=ALU.mult, op1=ALU.add))
            reached("halves")
            link(dve.tensor_scalar(hi_src, hi_src, float(BINS - 1), None, ALU.min))
            with dve.Fori(0, BINS) as i:
                dve.wait_ge(s_bin, i + 1)
                dve.tensor_scalar(mask, hi_src, iota_f[:, bass.ds(i, 1)], None, ALU.is_equal, ALU.add,
                                  accum_out=cnt[:, bass.ds(i, 1)]).then_inc(s_bin, 1)
            dve.wait_ge(s_bin, BINS + 1)
            reached("counts")
            b = BATCH["bins"]
            dve.wait_ge(s_pe, b + 1)
            link(dve.tensor_copy(tot, pm[:, b % 2, 512:512 + BINS]))
            link(dve.tensor_tensor_scan(run, ones[:, 0:BINS], tot, 0.0, ALU.mult, ALU.add))
            link(dve.tensor_tensor(run, run, tot, ALU.subtract))
            link(dve.scalar_tensor_tensor(out=base, in0=run, scalar=-1.0, in1=pm[:, b % 2, 0:BINS], op0=ALU.add, op1=ALU.add))
            dve.sem_inc(s_ev[b % 2], 1)
            link(dve.memset(pos, 0.0))
            with dve.Fori(0, BINS) as i:
                dve.wait_ge(s_bin, i * 3 + (BINS + 1))
                dve.tensor_scalar(mask, hi_src, iota_f[:, bass.ds(i, 1)], None, ALU.is_equal).then_inc(s_bin, 1)
                dve.wait_ge(s_bin, i * 3 + (BINS + 2))
                dve.tensor_tensor_scan(cum, onesw, mask, base[:, bass.ds(i, 1)], ALU.mult, ALU.add).then_inc(s_bin, 1)
                dve.wait_ge(s_bin, i * 3 + (BINS + 3))
                dve.sem_inc(s_dpass, 1)
                dve.copy_predicated(pos, mask.bitcast(I32), cum).then_inc(s_bin, 1)
            dve.wait_ge(s_bin, 4 * BINS + 1)
            link(dve.tensor_copy(posi, pos))
            reached("positions")

            def evac(name, n, of):
                for k in range(n):
                    b = BATCH[name] + k
                    dve.wait_ge(s_pe, b + 1)
                    of(k, pmv(b % 2))
                    dve.sem_inc(s_ev[b % 2], 1)

            def lists(name, rel, idx, tvx, key_rows, oth_rows, more):
                dve.wait_ge(s_first, 16 if name == "A" else 32)
                link(dve.tensor_scalar(firsts_s, firsts_i, 7, None, ALU.logical_shift_right))
                link(dve.tensor_copy(firsts, firsts_s))
                link(dve.tensor_tensor(firsts, firsts, iota_f[0:1, :], ALU.add))
                reached("firsts " + name)
                b = BATCH["broadcast " + name]
                dve.wait_ge(s_pe, b + 1)
                for g in range(VT):
                    link(dve.tensor_scalar(before[:, 0:CHUNKS - 1], pm[:, b % 2, 1:CHUNKS], vcol[:, g:g + 1], None, ALU.is_le))
                    link(dve.tensor_reduce(cv[:, g:g + 1], before[:, 0:CHUNKS - 1], AX.X, ALU.add))
                dve.sem_inc(s_ev[b % 2], 1)
                link(dve.tensor_copy(cvi, cv))
                reached("cv" + name)
                link(dve.tensor_tensor(tv, vcol[:, :], cv, ALU.subtract))
                link(dve.tensor_scalar(tv128, tv, 128.0, None, ALU.mult))
                link(dve.tensor_scalar(tvc, tv, float(TILES - 1), None, ALU.min))
                dve.wait_ge(s_rows, 16 * VT * (3 if name == "A" else 4))
                link(dve.tensor_copy(relR, key_rows))
                link(dve.tensor_copy(othR, oth_rows))
                link(dve.tensor_tensor(relR, relR, wide(tv128, P), ALU.subtract))
                reached("tv sources " + name)
                evac("rel" + name, 1, lambda k, s: link(dve.tensor_copy(rel[:, :].rearrange("p (g v) -> p g v", g=VT), s)))
                evac("idx" + name, 1, lambda k, s: link(dve.tensor_copy(idx[:, :].rearrange("p (g v) -> p g v", g=VT), s)))
                if more:
                    evac("weights", 1, lambda k, s: link(dve.tensor_copy(wA[:, :].rearrange("p (g v) -> p g v", g=VT), s)))
                if name == "B":
                    dve.wait_ge(s_tv, 16 * VT)
                evac("tv" + name, 1, lambda k, s: link(dve.tensor_copy(tvT, s[0:VT, 0, :])))
                reached("tvT " + name)

            for b, (hi, lo) in enumerate(((hi_dst, lo_dst), (hi_src, lo_src))):
                with dve.Fori(0, COLS // (2 * U)) as i:
                    for h in range(2):
                        dve.wait_ge(s_dmm, i * 2 + (b * (COLS // U) + h + 1))
                        cols = lambda a, n: a[:, bass.ds(i * (2 * U) + h * U, U)].rearrange("p (u o) -> p u o", o=1).to_broadcast([P, U, n])
                        dve.tensor_tensor(ohh[:, h, :, 0:TILES], over(iota_f[:, 0:TILES], U), cols(hi, TILES), ALU.is_equal)
                        dve.tensor_tensor(ohl[:, h, :, :], over(iota_f[:, 0:P], U), cols(lo, P), ALU.is_equal).then_inc(s_doh, 1)

            def finish_degrees():
                dve.wait_ge(s_deg, 1)
                link(dve.tensor_scalar(dinv[:, :], deg_ps[0], 1.0, None, ALU.add))
                link(dve.tensor_scalar(degin[:, :], deg_ps[0], 1.0, None, ALU.max))
                link(dve.tensor_scalar(degout[:, :], deg_ps[1], 1.0, None, ALU.max))
                link(dve.tensor_scalar(hasin[:, :], deg_ps[0], 1.0, None, ALU.min))
                link(dve.reciprocal(degin[:, :], degin[:, :]))
                link(dve.reciprocal(degout[:, :], degout[:, :]))

            dve.wait_ge(s_list, 48)
            lists("A", relA, idxA, tvA, rowsi[:, :, 0, :], rowsi[:, :, 1, :], True)
            finish_degrees()
            reached("degrees")
            lists("B", relB, idxB, tvB, prow[:, :, :, 0], prow[:, :, :, 1], False)
            evac("turn mW", 1, lambda k, s: link(dve.tensor_copy(W[:, 13:15, :], s[:, 0:2, :])))
            dve.wait_ge(s_root, 1)
            link(dve.reciprocal(dinv[:, :], dinv[:, :]))
            dve.wait_ge(s_xin, 32)
            dve.wait_ge(s_tv, 32 * VT)

            def walk(k, rel, tvx):
                def onehot(first, j, at):
                    dve.wait_ge(s_mm, at)
                    dve.tensor_tensor(oh[:, j % 2, :, :], over(iota_f[:, 0:P], U),
                                      rel[:, first].rearrange("p (u o) -> p u o", o=1).to_broadcast([P, U, P]),
                                      ALU.is_equal).then_inc(s_oh, 1)
                if k:
                    dve.wait_ge(s_oh, k * (GROUPS + 1))
                onehot(slice(0, U), 0, k * GROUPS + RING)
                with dve.Fori(0, ROUNDS) as i:
                    for j in range(RING):
                        g8 = i * (RING * U)
                        onehot(bass.ds(g8 + (j + 1) * U, U), j + 1, i * RING + (k * GROUPS + j + RING))
                        tiles = [dve.value_load(tvx[0:1, bass.ds(g8 + (j * U + u), 1)], min_val=0, max_val=TILES - 1) for u in range(U)]
                        dve.wait_ge(s_mm, i * RING + (k * GROUPS + j + 1 + RING))
                        for u, t in enumerate(tiles):
                            dve.wait_ge(s_add, g8 + (U * (k * GROUPS + j) + u + 2 * U))
                            part = accf[:, bass.ds(t * P, P)]
                            dve.tensor_tensor(part, part, ps[:, j % 2, u, :], ALU.add).then_inc(s_add, 1)
                dve.wait_ge(s_add, U * GROUPS * (k + 1) + 2 * U)

            def layer_norm(before_root, after, n_root):
                link(dve.tensor_reduce(stat[:, 0, :], Z[:, :, :], AX.X, ALU.add))
                link(dve.tensor_scalar(stat[:, 0, :], stat[:, 0, :], 1.0 / D, None, ALU.mult))
                link(dve.tensor_tensor(Z[:, :, :], Z[:, :, :], wide(stat[:, 0, :]), ALU.subtract))
                link(dve.tensor_tensor(Y, Z[:, :, :], Z[:, :, :], ALU.mult))
                link(dve.tensor_reduce(stat[:, 1, :], Y, AX.X, ALU.add))
                link(dve.tensor_scalar(stat[:, 1, :], stat[:, 1, :], 1.0 / D, EPS, ALU.mult, ALU.add))
                reached(before_root)
                dve.wait_ge(s_root, n_root)
                link(dve.reciprocal(stat[:, 2, :], stat[:, 1, :]))
                link(dve.tensor_tensor(X[:, :, :], Z[:, :, :], wide(stat[:, 2, :]), ALU.mult))
                reached(after)

            def batch_of(buf, k):
                return buf[:, k * BT:(k + 1) * BT, :]

            link(dve.tensor_tensor(Y, X[:, :, :], wide(dinv[:, :]), ALU.mult))
            dve.wait_ge(s_w, 16 * 23)
            for k in range(3):
                reached(f"table {k}")
                evac(f"self {k}", NB, lambda n, s: link(dve.tensor_copy(batch_of(acc, n), s)))
                walk(k, relA, tvA)
                evac(f"gcn {k}", NB, lambda n, s: link(dve.tensor_tensor(batch_of(Z, n), s, wide(dinv[:, n * BT:(n + 1) * BT]), ALU.mult)))
                link(dve.tensor_tensor(Z[:, :, :], Z[:, :, :], over(brow[:, k, :]), ALU.add))
                if k < 2:
                    dve.wait_ge(s_tab, 16 * (k + 1))
                    link(dve.scalar_tensor_tensor(out=Y, in0=Z[:, :, :], scalar=0.0, in1=wide(dinv[:, :]), op0=ALU.max, op1=ALU.mult))
            link(dve.tensor_tensor(Z[:, :, :], Z[:, :, :], X[:, :, :], ALU.add))
            dve.wait_ge(s_tab, 48)
            layer_norm("var 0", "x1", 2)

            evac("turn X1", NB, lambda n, s: link(dve.tensor_copy(batch_of(Y, n), s)))
            evac("x_l", NB, lambda n, s: link(dve.tensor_tensor(batch_of(Z, n), s, over(brow[:, 6, :], BT), ALU.add)))
            reached("x_l")
            evac("x_r", NB, lambda n, s: link(dve.tensor_tensor(batch_of(V, n), s, over(brow[:, 7, :], BT), ALU.add)))
            We, att = brow[:, 9, :], brow[:, 10, :]

            def onehot(k, first, j, at):
                dve.wait_ge(s_mm, at)
                dve.tensor_tensor(oh[:, j % 2, :, :], over(iota_f[:, 0:P], U),
                                  relA[:, first].rearrange("p (u o) -> p u o", o=1).to_broadcast([P, U, P]),
                                  ALU.is_equal).then_inc(s_oh, 1)

            dve.wait_ge(s_tab, 16 * 4)
            dve.wait_ge(s_oh, 3 * (GROUPS + 1))
            onehot(3, slice(0, U), 0, 3 * GROUPS + RING)
            with dve.Fori(0, ROUNDS) as i:
                for j in range(RING):
                    g8 = i * (RING * U)
                    at = i * (RING * 6) + 6 * j
                    onehot(3, bass.ds(g8 + (j + 1) * U, U), j + 1, i * RING + (3 * GROUPS + j + RING))
                    dve.wait_ge(s_mm, i * RING + (3 * GROUPS + j + 1 + RING))
                    dve.wait_ge(s_gath[j], i * (16 * U) + 16 * U * (3 * ROUNDS + 1))
                    dve.tensor_tensor(sc_a, ps[:, j % 2, :, :], msg[:, j, :, :], ALU.add).then_inc(s_p1, 1)
                    dve.tensor_tensor(sc_b, over(We, U), wA[:, bass.ds(g8 + j * U, U)].rearrange("p (u o) -> p u o", o=1).to_broadcast([P, U, D]),
                                      ALU.mult).then_inc(s_p1, 1)
                    dve.wait_ge(s_p1, at + 2)
                    dve.tensor_tensor(sc_a, sc_a, sc_b, ALU.add).then_inc(s_p1, 1)
                    dve.wait_ge(s_p1, at + 3)
                    dve.scalar_tensor_tensor(out=sc_b, in0=sc_a, scalar=0.2, in1=sc_a, op0=ALU.mult, op1=ALU.max).then_inc(s_p1, 1)
                    dve.wait_ge(s_p1, at + 4)
                    dve.tensor_tensor(sc_a, sc_b, over(att, U), ALU.mult).then_inc(s_p1, 1)
                    dve.wait_ge(s_p1, at + 5)
                    dve.tensor_reduce(ext[:, bass.ds(g8 + j * U, U), 0:H], sc_a.rearrange("p u (h c) -> p u h c", h=H), AX.X, ALU.add).then_inc(s_p1, 1)
                    dve.wait_ge(s_p1, at + 6)
                    dve.wait_ge(s_store[j], i * 16 + 16)
                    dve.sem_inc(s_add, U)
            dve.wait_ge(s_add, U * GROUPS * 4 + 2 * U)
            dve.wait_ge(s_xlback, 16)
            link(dve.tensor_tensor(V[:, :, :], V[:, :, :], Z[:, :, :], ALU.add))

            def masks(k, s):
                link(dve.tensor_scalar(tmpR, s, 0.0, None, ALU.is_ge))
                link(dve.scalar_tensor_tensor(out=tmpR, in0=s, scalar=P - 0.5, in1=tmpR, op0=ALU.is_le, op1=ALU.mult))
                link(dve.scalar_tensor_tensor(out=keyR, in0=s, scalar=1.0, in1=tmpR, op0=ALU.add, op1=ALU.mult))
                link(dve.tensor_scalar(keyR, keyR, -1.0, None, ALU.add))
                link(dve.tensor_scalar(tmpR, tmpR, -1.0, BIG, ALU.add, ALU.mult))
            evac("rows of keys", 1, masks)
            link(dve.memset(penF, -BIG))
            link(dve.memset(penB, -BIG))
            link(dve.memset(A5[:, :, VT - 1, :], -BIG))
            link(dve.tensor_tensor(penF[:, :, 1:P], keyR[:, :, 1:P], keyR[:, :, 0:P - 1], ALU.is_equal))
            link(dve.tensor_scalar(penF[:, :, 1:P], penF[:, :, 1:P], -1.0, BIG, ALU.add, ALU.mult))
            link(dve.tensor_copy(penB[:, :, 0:P - 1], penF[:, :, 1:P]))
            link(dve.tensor_reduce(ends[:, 4, :, 0:1].rearrange("p g a -> p (g a)"), penF[:, :, 1:P], AX.X, ALU.min))
            evac("rows of weights", 1, lambda k, s: link(dve.tensor_tensor(A5[:, H, :, :], s, tmpR, ALU.add)))
            VL = VISITS - (VT - 1) * P

            def scores_rows(h):
                def of(k, s):
                    link(dve.tensor_tensor(A5[:, h, 0:VT - 1, :], s[:, 0:VT - 1, :], tmpR[:, 0:VT - 1, :], ALU.add))
                    link(dve.tensor_tensor(A5[0:VL, h, VT - 1, :], s[0:VL, VT - 1, :], tmpR[0:VL, VT - 1, :], ALU.add))
                return of
            for h in range(H):
                evac(f"rows of scores {h}", 1, scores_rows(h))
            flat = lambda a: a.rearrange("p g e -> p (g e)")
            for c in range(C5):
                link(dve.tensor_tensor_scan(flat(F5[:, c, :, :]), flat(penF), flat(A5[:, c, :, :]), -BIG, ALU.add, ALU.max))
                link(dve.tensor_tensor_scan(flat(A5[:, c, :, :])[:, ::-1], flat(penB)[:, ::-1], flat(A5[:, c, :, :])[:, ::-1], -BIG, ALU.add, ALU.max))
            bc = lambda a: a.to_broadcast([P, VT, C5])
            link(dve.tensor_copy(ends[:, 4, :, 1:C5], ends[:, 4, :, 0:1].to_broadcast([P, VT, C5 - 1])))
            link(dve.tensor_copy(ends[:, 0, :, :], F5[:, :, :, P - 1].rearrange("p c g -> p g c")))
            link(dve.tensor_copy(ends[:, 1, :, :], A5[:, :, :, 0].rearrange("p c g -> p g c")))
            link(dve.tensor_copy(ends[:, 2, :, :], bc(keyR[:, :, 0:1])))
            link(dve.tensor_copy(ends[:, 3, :, :], bc(keyR[:, :, P - 1:P])))
            reached("carry sources")
            for q in range(5):
                b = BATCH[f"ends {q}"]
                dve.wait_ge(s_pe, b + 1)
                link(dve.tensor_copy(rowbuf[q], pm[0:C5, b % 2, 0:VP]))
                dve.sem_inc(s_ev[b % 2], 1)
            rF, rB, rfirst, rlast, rwhole, rlink = rowbuf
            link(dve.memset(rlink[:, 0:1], -BIG))
            link(dve.tensor_tensor(rlink[:, 1:VP], rfirst[:, 1:VP], rlast[:, 0:VP - 1], ALU.is_equal))
            link(dve.tensor_scalar(rlink[:, 1:VP], rlink[:, 1:VP], -1.0, BIG, ALU.add, ALU.mult))
            link(dve.tensor_tensor(rfirst, rlink, rwhole, ALU.add))
            link(dve.memset(rlast[:, VP - 1:VP], -BIG))
            link(dve.tensor_tensor(rlast[:, 0:VP - 1], rlink[:, 1:VP], rwhole[:, 0:VP - 1], ALU.add))
            link(dve.tensor_tensor_scan(rF, rfirst, rF, -BIG, ALU.add, ALU.max))
            link(dve.tensor_tensor_scan(rB[:, ::-1], rlast[:, ::-1], rB[:, ::-1], -BIG, ALU.add, ALU.max))
            cF, cB, cL = crow
            for c in (cF[:, 0:1], cB[:, VP - 1:VP], cL[:, VP - 1:VP]):
                link(dve.memset(c, -BIG))
            link(dve.tensor_tensor(cF[:, 1:VP], rF[:, 0:VP - 1], rlink[:, 1:VP], ALU.add))
            link(dve.tensor_tensor(cB[:, 0:VP - 1], rB[:, 1:VP], rlink[:, 1:VP], ALU.add))
            link(dve.tensor_copy(cL[:, 0:VP - 1], rlink[:, 1:VP]))
            reached("carries")
            for q in range(3):
                evac(f"carries {q}", 1, lambda k, s: link(dve.tensor_copy(backs[:, q, :, :], s[:, :, 0:C5])))
            link(dve.tensor_tensor(F5, F5, A5, ALU.max))
            for q, end in ((0, 0), (1, P - 1)):
                link(dve.tensor_tensor(tmpR, keyR, keyR[:, :, end:end + 1].to_broadcast([P, VT, P]), ALU.is_equal))
                link(dve.tensor_scalar(tmpR, tmpR, -1.0, BIG, ALU.add, ALU.mult))
                for c in range(C5):
                    for g in range(VT):
                        link(dve.scalar_tensor_tensor(out=F5[:, c, g, :], in0=tmpR[:, g, :], scalar=backs[:, q, g, c:c + 1],
                                                      in1=F5[:, c, g, :], op0=ALU.add, op1=ALU.max))
            link(dve.tensor_scalar(lastR[:, :, 0:P - 1], penB[:, :, 0:P - 1], -1.0, None, ALU.is_lt))
            link(dve.tensor_scalar(lastR[:, :, P - 1:P], backs[:, 2, :, 0:1], -1.0, None, ALU.is_lt))
            reached("largest")
            evac("lasts", 1, lambda k, s: link(dve.tensor_copy(lastT.rearrange("p (g e) -> p g e", g=VT), s)))
            for c in range(C5):
                def shift(k, s):
                    m = s.rearrange("p g e -> p (g e)")[:, 0:VISITS]
                    link(dve.tensor_tensor(ext[:, :, H + c], m, lastT[:, 0:VISITS], ALU.mult))
                    if c < H:
                        link(dve.tensor_tensor(ext[:, :, c], ext[:, :, c], m, ALU.subtract))
                evac(f"largest {c}", 1, shift)
            link(dve.tensor_scalar(ext[:, :, 0:H], ext[:, :, 0:H], 0.0, None, ALU.min))
            link(dve.memset(accG, 0.0))
            reached("shifted")
            dve.wait_ge(s_exp, 1)

            dve.wait_ge(s_oh, 4 * (GROUPS + 1))
            onehot(4, slice(0, U), 0, 4 * GROUPS + RING)
            with dve.Fori(0, ROUNDS) as i:
                for j in range(RING):
                    g8 = i * (RING * U)
                    onehot(4, bass.ds(g8 + (j + 1) * U, U), j + 1, i * RING + (4 * GROUPS + j + RING))
                    dve.wait_ge(s_back[j], i * 16 + 16)
                    m = msg[:, j, :, :].rearrange("p u (h c) -> p u h c", h=H)
                    w = ext[:, bass.ds(g8 + j * U, U), 0:H].rearrange("p u (h o) -> p u h o", o=1).to_broadcast([P, U, H, HC])
                    dve.tensor_tensor(m, m, w, ALU.mult).then_inc(s_msgs, 1)
                    tiles = [dve.value_load(tvA[0:1, bass.ds(g8 + (j * U + u), 1)], min_val=0, max_val=TILES - 1) for u in range(U)]
                    dve.wait_ge(s_mm, i * RING + (4 * GROUPS + j + 1 + RING))
                    for u, t in enumerate(tiles):
                        dve.wait_ge(s_add, g8 + (U * (4 * GROUPS + j) + u + 2 * U))
                        part = accG[:, bass.ds(t * GW, GW)]
                        dve.tensor_tensor(part, part, gsum(j % 2, u), ALU.add).then_inc(s_add, 1)
            dve.wait_ge(s_add, U * GROUPS * 5 + 2 * U)

            aG = accG.rearrange("p (t a) -> p t a", a=GW)
            heads = lambda a: a.rearrange("p t (h c) -> p t h c", h=H)
            per_head = lambda a: a.rearrange("p t (h o) -> p t h o", o=1).to_broadcast([P, TILES, H, HC])
            m_in, m_all, c_in, c_self, den, a_self = small[4], small[5], small[0], small[1], small[2], small[3]
            dve.wait_ge(s_xlback, 32)
            link(dve.tensor_tensor(selfT, aG[:, :, GW - 1:GW].to_broadcast([P, TILES, D]), over(We), ALU.mult))
            link(dve.tensor_tensor(selfT, selfT, V[:, :, :], ALU.add))
            link(dve.scalar_tensor_tensor(out=selfT, in0=selfT, scalar=0.2, in1=selfT, op0=ALU.mult, op1=ALU.max))
            link(dve.tensor_tensor(selfT, selfT, over(att), ALU.mult))
            link(dve.tensor_reduce(a_self, heads(selfT), AX.X, ALU.add))
            link(dve.tensor_scalar(hasin[:, :], hasin[:, :], -1.0, BIG, ALU.add, ALU.mult))
            link(dve.tensor_tensor(m_in, aG[:, :, D + H:D + 2 * H], wide(hasin[:, :], H), ALU.add))
            link(dve.tensor_tensor(m_all, m_in, a_self, ALU.max))
            link(dve.tensor_tensor(c_in, m_in, m_all, ALU.subtract))
            link(dve.tensor_tensor(c_self, a_self, m_all, ALU.subtract))
            reached("self shifted")
            dve.wait_ge(s_exp, 2)
            link(dve.tensor_tensor(den, c_in, aG[:, :, D:D + H], ALU.mult))
            link(dve.tensor_tensor(den, den, c_self, ALU.add))
            link(dve.tensor_scalar(den, den, 1e-16, None, ALU.add))
            link(dve.reciprocal(den, den))
            link(dve.tensor_tensor(c_in, c_in, den, ALU.mult))
            link(dve.tensor_tensor(c_self, c_self, den, ALU.mult))
            link(dve.tensor_tensor(heads(selfT), heads(aG[:, :, 0:D]), per_head(c_in), ALU.mult))
            link(dve.tensor_tensor(heads(Z[:, :, :]), heads(Z[:, :, :]), per_head(c_self), ALU.mult))
            link(dve.tensor_tensor(Z[:, :, :], Z[:, :, :], selfT, ALU.add))
            link(dve.tensor_tensor(Z[:, :, :], Z[:, :, :], over(brow[:, 8, :]), ALU.add))
            link(dve.tensor_tensor(Z[:, :, :], Z[:, :, :], X[:, :, :], ALU.add))
            layer_norm("var 1", "x2", 3)

            evac("turn X", NB, lambda n, s: link(dve.tensor_copy(batch_of(Y, n), s)))
            link(dve.memset(acc, 0.0))
            walk(5, relA, tvA)

            def diagonal(n):
                dve.tensor_tensor(diag[:, n % 2, 0:BT, :], over(ident[:, :], BT), wide(degin[:, n * BT:(n + 1) * BT]), ALU.mult).then_inc(s_diag, 1)

            diagonal(0)
            for n in range(NB):
                if n + 1 < NB:
                    diagonal(n + 1)
                b = BATCH["rdeg"] + n
                dve.wait_ge(s_pe, b + 1)
                link(dve.tensor_tensor(batch_of(acc, n), batch_of(acc, n), pmv(b % 2), ALU.mult))
                dve.sem_inc(s_ev[b % 2], 1)
            reached("scaled")
            evac("p", NB, lambda n, s: link(dve.tensor_copy(batch_of(Y, n), s)))
            reached("p ready")
            evac("q", NB, lambda n, s: link(dve.tensor_tensor(batch_of(acc, n), s, over(brow[:, 3, :], BT), ALU.add)))
            link(dve.tensor_tensor(Z[:, :, :], acc, X[:, :, :], ALU.add))
            link(dve.memset(acc, 0.0))
            walk(6, relA, tvA)
            link(dve.tensor_tensor(acc, acc, wide(degin[:, :]), ALU.mult))
            link(dve.tensor_tensor(Z[:, :, :], Z[:, :, :], acc, ALU.add))
            dve.wait_ge(s_tab, 16 * 6)
            layer_norm("var 2", "x3", 4)

            for k in range(2):
                link(dve.memset(acc, 0.0))
                walk(7 + k, relB, tvB)
                evac(f"mean {k}", NB, lambda n, s: link(dve.tensor_tensor(batch_of(Z, n), s, wide(degout[:, n * BT:(n + 1) * BT]), ALU.mult)))
                link(dve.tensor_tensor(Z[:, :, :], Z[:, :, :], over(brow[:, 4 + k, :]), ALU.add))
                if k == 0:
                    link(dve.tensor_scalar(Y, Z[:, :, :], 0.0, None, ALU.max))
                    reached("h3")
            link(dve.scalar_tensor_tensor(out=Z[:, :, :], in0=Z[:, :, :], scalar=0.0, in1=X[:, :, :], op0=ALU.max, op1=ALU.add))
            dve.wait_ge(s_tab, 16 * 8)
            layer_norm("var 3", "x4", 5)


_INS = ["x", "src", "dst", "edge_weight", "L0_gnn_W1", "L0_gnn_b1", "L0_gnn_W2", "L0_gnn_b2", "L0_gnn_W3", "L0_gnn_b3",
        "L1_gnn_Wl", "L1_gnn_bl", "L1_gnn_Wr", "L1_gnn_br", "L1_gnn_We", "L1_gnn_att", "L1_gnn_bias",
        "L2_gnn_Wl1", "L2_gnn_bl1", "L2_gnn_Wr1", "L2_gnn_Wl2", "L2_gnn_bl2", "L2_gnn_Wr2",
        "L3_gnn_W1", "L3_gnn_b1", "L3_gnn_W2", "L3_gnn_b2"]


def kernel(**inputs):
    import numpy as _np
    import concourse.bacc as _bacc
    from concourse import mybir as _mybir
    from concourse.bass_utils import run_bass_kernel_spmd as _run

    nc = _bacc.Bacc("TRN2", target_bir_lowering=False, num_devices=1)
    arrays, args = {}, []
    for name in _INS:
        a = _np.ascontiguousarray(inputs[name])
        arrays[f"in_{name}_dram"] = a
        args.append(nc.dram_tensor(f"in_{name}_dram", a.shape, _mybir.dt.from_np(a.dtype), kind="ExternalInput").ap())
    shape = inputs["x"].shape
    args.append(nc.dram_tensor("out_0_dram", shape, _mybir.dt.float32, kind="ExternalOutput").ap())
    build(nc, *args)
    r = _run(nc, [arrays], core_ids=[0])
    return r.results[0]["out_0_dram"]
```

```python
from contextlib import ExitStack

import concourse.bass as bass
from concourse import mybir

ALU = mybir.AluOpType
ACT = mybir.ActivationFunctionType
AX = mybir.AxisListType
F32 = mybir.dt.float32
I32 = mybir.dt.int32
U32 = mybir.dt.uint32

P = 128
U = 8
RING = 4
EPS = 1e-5
FAR = 1 << 20


def build(nc, x, src, dst, edge_weight, W1, b1, W2, b2, W3, b3, gWl, gbl, gWr, gbr, gWe, gatt, gbias,
          sWl1, sbl1, sWr1, sWl2, sbl2, sWr2, mW1, mb1, mW2, mb2, out):
    N, D = x.shape
    E = src.shape[0]
    H, HC = gatt.shape
    HID = sWl1.shape[1]
    TILES = -(-N // P)
    CHUNKS = -(-E // P)
    VISITS = -(-(CHUNKS + TILES - 1) // (U * RING)) * U * RING
    GROUPS = VISITS // U
    ROUNDS = GROUPS // RING
    VT = -(-VISITS // P)
    COLS = -(-E // (P * 16)) * 16
    EPAD = COLS * P
    CH2 = EPAD // P
    NPAD = TILES * P
    BINS = TILES + 1
    BINS2 = 2 * ROUNDS
    NODES_LAST = N - (TILES - 1) * P
    TW = TILES * P
    assert D == P and CH2 >= CHUNKS and COLS % 16 == 0

    ctx = ExitStack()
    with ctx:
        def sb(name, shape, dt=F32):
            return ctx.enter_context(nc.sbuf_tensor(name, shape, dt))

        def pb(name, shape, dt=F32):
            return ctx.enter_context(nc.psum_tensor(name, shape, dt))

        def sem(name):
            return ctx.enter_context(nc.semaphore(name))

        def dram(name, shape, dt=F32):
            return nc.dram_tensor(name, shape, dt, kind="Internal").ap()

        tab = [dram(f"tab{k}", (NPAD, D)) for k in range(8)]
        edge_key = dram("edge_key", (CH2, P), I32)
        edge_oth = dram("edge_oth", (CH2, P), I32)
        gathered = dram("gathered", (VISITS // U * P, U * D))
        edge_w = dram("edge_w", (CH2, P))
        pairs = dram("pairs", (EPAD, 2), I32)

        BIG = 1e30
        BF = mybir.dt.bfloat16
        ident = sb("ident", [P, P])
        ones = sb("ones", [P, P])
        lower = sb("lower", [P, P])
        zeros = sb("zeros", [P, P])
        epsb = sb("epsb", [P, 1])
        iota_f = sb("iota_f", [P, P])
        chunk_no = sb("chunk_no", [1, COLS])
        vcol_i = sb("vcol_i", [P, VT], I32)
        vcol = sb("vcol", [P, VT])
        X = sb("X", [P, TILES, D])
        EXT = H + H + 1
        GW = D + EXT
        EXT0 = -(-TILES * GW // 64) * 64
        big = sb("big", [P, max(EXT0 + VISITS * EXT, 2 * TW)])
        acc = big[:, 0:TW].rearrange("p (t f) -> p t f", f=D)
        Y = big[:, TW:2 * TW].rearrange("p (t f) -> p t f", f=D)
        accG = big[:, 0:TILES * GW]
        ext = big[:, EXT0:EXT0 + VISITS * EXT].rearrange("p (v a) -> p v a", a=EXT)
        Z = sb("Z", [P, TILES, D])
        V = sb("V", [P, TILES, D])
        diag = sb("diag", [P, 2, U, P])
        msg = sb("msg", [P, RING, U, D])
        oh = sb("oh", [P, 2, U, P])
        idxA = sb("idxA", [P, VT * P], I32)
        relA = sb("relA", [P, VT * P])
        idxB = sb("idxB", [P, VT * P], I32)
        relB = sb("relB", [P, VT * P])
        lst = sb("lst", [P, 40])
        posi = sb("posi", [P, COLS], I32)
        wA = sb("wA", [P, VT * P])
        tiles_row = sb("tiles_row", [1, VT * P], I32)
        tvT = sb("tvT", [VT, P], I32)
        stage = sb("stage", [P, 6 * U], I32)
        W = sb("W", [P, 15, D])
        bcol = sb("bcol", [P, 2])
        brow = sb("brow", [P, 11, D])
        degin = sb("degin", [P, TILES])
        dinv = sb("dinv", [P, TILES])
        degout = sb("degout", [P, TILES])
        hasin = sb("hasin", [P, TILES])
        stat = sb("stat", [P, 3, TILES])

        banks = pb("banks", [P, 8, 512])
        ps = banks[:, 0:4, :].rearrange("p (h b) (u f) -> p h (b u) f", h=2, f=P)
        pm = banks[:, 4:8, :].rearrange("p (h b) n -> p h (b n)", h=2)

        s_edges = sem("s_edges")
        s_list = sem("s_list")
        s_first = sem("s_first")
        s_tv = sem("s_tv")
        s_rows = sem("s_rows")
        s_up = sem("s_up")
        s_var = sem("s_var")
        s_scst = sem("s_scst")
        s_root = sem("s_root")
        s_doh = sem("s_doh")
        s_dmm = sem("s_dmm")
        s_deg = sem("s_deg")
        s_diag = sem("s_diag")
        s_bin = sem("s_bin")
        s_oT = sem("s_oT")
        s_oTc = sem("s_oTc")
        s_p1 = sem("s_p1")
        s_xl = sem("s_xl")
        s_xlback = sem("s_xlback")
        s_mask = sem("s_mask")
        s_exp = sem("s_exp")
        s_msgs = sem("s_msgs")
        s_const = sem("s_const")
        s_xin = sem("s_xin")
        s_w = sem("s_w")
        s_load = sem("s_load")
        s_chain = sem("s_chain")
        s_staged = sem("s_staged")
        s_pass = sem("s_pass")
        s_dpass = sem("s_dpass")
        s_gath = [sem(f"s_gath{j}") for j in range(RING)]
        s_oh = sem("s_oh")
        s_mm = sem("s_mm")
        s_add = sem("s_add")
        s_tab = sem("s_tab")
        s_pe = sem("s_pe")
        s_ev = [sem("s_ev0"), sem("s_ev1")]
        s_store = [sem(f"s_store{j}") for j in range(RING)]
        s_back = [sem(f"s_back{j}") for j in range(RING)]
        s_scat = [sem("s_scat0"), sem("s_scat1")]
        s_go = sem("s_go")
        s_out = sem("s_out")
        block = ctx.enter_context(nc.Block())
        Xf, Zf, Vf = [t[:, :, :].rearrange("p t f -> p (t f)") for t in (X, Z, V)]
        accf, Yf = big[:, 0:TW], big[:, TW:2 * TW]
        Yi, Zi = Yf.bitcast(I32), Zf.bitcast(I32)
        dst_far, src_zero = Yi[:, 0:COLS], Yi[:, COLS:2 * COLS]
        w_row = Yf[:, 2 * COLS:3 * COLS]
        src_far, dst_zero = relB[:, 0:COLS].bitcast(I32), idxB[:, 0:COLS]
        spare = big[:, 2 * TW:2 * TW + VISITS + P * U // 2].bitcast(BF)
        hi_src, lo_src = spare[:, 0:VISITS], spare[:, VISITS:2 * VISITS]
        iota8 = spare[:, 2 * VISITS:].rearrange("p (n u) -> p n u", u=U)
        hi_i, hi_f, lo_f = Zi[:, 0:COLS], Zf[:, COLS:2 * COLS], Zf[:, 2 * COLS:3 * COLS]
        hi_dst, lo_dst = [Zf[:, (3 + k) * COLS:(4 + k) * COLS].bitcast(BF)[:, 0:COLS] for k in range(2)]
        iota_i = Zi[:, 5 * COLS:5 * COLS + P]
        mask, cum, pos, onesw = [Vf[:, k * COLS:(k + 1) * COLS] for k in range(4)]
        cnt, base, tot, run = [Vf[:, 4 * COLS + 64 * k:4 * COLS + 64 * k + BINS2] for k in range(4)]
        before = Zf[:, 0:COLS]
        firsts_i = Zi[0:1, COLS:2 * COLS]
        firsts = Zf[0:1, 2 * COLS:3 * COLS]
        firsts_s = Zi[0:1, 0:COLS]
        cv, tv, tv128, tvc = [lst[:, 8 * k:8 * k + VT] for k in range(4)]
        cvi = lst[:, 32:32 + VT].bitcast(I32)
        rows = Vf[:, 0:3 * VT * P].rearrange("p (a g e) -> p g a e", a=3, g=VT)
        rowsi = Vf[:, 0:3 * VT * P].bitcast(I32).rearrange("p (a g e) -> p g a e", a=3, g=VT)
        prow = Vf[:, 0:2 * VT * P].bitcast(I32).rearrange("p (g e a) -> p g e a", g=VT, a=2)
        relR = Vf[:, 3 * VT * P:4 * VT * P].rearrange("p (g e) -> p g e", g=VT)
        othR = Vf[:, 4 * VT * P:5 * VT * P].rearrange("p (g e) -> p g e", g=VT)
        ohb = diag[:, :, :, :].rearrange("p b u f -> p (b u f)").bitcast(BF)
        ohl = ohb[:, 0:2 * P * U].rearrange("p (b n u) -> p b n u", b=2, u=U)
        ohh = ohb[:, 2 * P * U:2 * P * U + 2 * TILES * U].rearrange("p (b n u) -> p b n u", b=2, u=U)
        scat_pos = stage[:, 0:2 * U].rearrange("p (b u) -> p b u", b=2)
        scat_rec = stage[:, 2 * U:6 * U].rearrange("p (b u a) -> p b u a", b=2, a=2)
        deg_ps = [banks[:, b, 0:TILES] for b in (0, 6)]

        def gsum(h, u):
            return banks[:, 4 * h + u // 3, (u % 3) * GW:(u % 3 + 1) * GW]

        extf = big[:, EXT0:EXT0 + VISITS * EXT]
        msgf = msg[:, :, :, :].rearrange("p j u f -> p (j u f)")
        VP = VT * P
        sc_a, sc_b = [Zf[:, k * U * D:(k + 1) * U * D].rearrange("p (u f) -> p u f", f=D) for k in range(2)]
        C5_ = H + 1
        A5 = Zf[:, 0:C5_ * VP].rearrange("p (c g e) -> p c g e", c=C5_, g=VT)
        F5 = big[:, 0:C5_ * VP].rearrange("p (c g e) -> p c g e", c=C5_, g=VT)
        keyR, penF, penB, lastR = [msgf[:, k * VP:(k + 1) * VP].rearrange("p (g e) -> p g e", g=VT) for k in range(4)]
        ohf = oh[:, :, :, :].rearrange("p b u f -> p (b u f)")
        ends = msgf[:, 4 * VP:4 * VP + 5 * VT * C5_].rearrange("p (q g c) -> p q g c", q=5, g=VT)
        backs = msgf[:, 4 * VP + 256:4 * VP + 256 + 3 * VT * C5_].rearrange("p (q g c) -> p q g c", q=3, g=VT)
        lastT = ohf[:, 0:VP]
        tmpR = ohf[:, VP:2 * VP].rearrange("p (g e) -> p g e", g=VT)
        diagf = diag[:, :, :, :].rearrange("p b u f -> p (b u f)")
        rowbuf = [Zf[0:C5_, C5_ * VP:(C5_ + 1) * VP], Zf[0:C5_, (C5_ + 1) * VP:(C5_ + 2) * VP],
                  big[0:C5_, C5_ * VP:(C5_ + 1) * VP], big[0:C5_, (C5_ + 1) * VP:(C5_ + 2) * VP],
                  diagf[0:C5_, 0:VP], diagf[0:C5_, VP:2 * VP]]
        crow = [rowbuf[4], rowbuf[2], rowbuf[3]]
        small = [msgf[:, k * TILES * H:(k + 1) * TILES * H].rearrange("p (t h) -> p t h", h=H) for k in range(6)]
        c12 = msgf[:, 0:2 * TILES * H]
        selfT = big[:, EXT0:EXT0 + TW].rearrange("p (t f) -> p t f", f=D)

        def pmv(h, n=7):
            return pm[:, h, 0:n * P].rearrange("p (t f) -> p t f", f=P)

        STAGES = [("broadcast A", 1), ("tvA", 1), ("relA", 1), ("idxA", 1), ("weights", 1), ("turn mW", 1)]
        BT = 7
        NB = TILES // BT
        assert NB * BT == TILES
        for k in range(3):
            STAGES += [(f"self {k}", NB), (f"gcn {k}", NB)] + [("bins", 1)] * (k == 0)
        STAGES += [("turn X1", NB), ("x_l", NB), ("x_r", NB), ("rows of keys", 1), ("rows of weights", 1)]
        STAGES += [(f"rows of scores {h}", 1) for h in range(H)]
        STAGES += [(f"ends {q}", 1) for q in range(5)] + [(f"carries {q}", 1) for q in range(3)]
        C5 = H + 1
        STAGES += [("lasts", 1)] + [(f"largest {c}", 1) for c in range(C5)]
        STAGES += [("turn X", NB), ("broadcast B", 1), ("tvB", 1), ("relB", 1), ("idxB", 1), ("rdeg", NB), ("hidden", 26), ("p", NB), ("q", NB), ("mean 0", NB), ("mean 1", NB)]
        BATCH, n0 = {}, 0
        for name, n in STAGES:
            BATCH[name] = n0
            n0 += n

        GO = ["halves", "firsts A", "cvA", "tvT A", "rows A", "degrees", "counts", "positions",
              "carry sources", "carries", "largest", "shifted", "self shifted",
              "firsts B", "cvB", "tvT B", "rows B", "scaled"]
        UP = ["t0", "t1", "t2", "x1", "x_l", "x2", "p", "x3", "h3", "x4"]
        TABLES = ["t0", "t1", "t2", "x_l", "x2", "p", "x3", "h3"]

        def up(name, n=NB - 1):
            return UP.index(name) * NB + n + 1

        def stored(name):
            return (TABLES.index(name) + 1) * NB * 16

        def gathers_before(k):
            return k - (k > 4)

        def segments(cuts):
            at = [0, *sorted(cuts), ROUNDS]
            return list(zip(at, at[1:]))

        def go(name):
            return GO.index(name) + 1

        def tiles_of(engine, first):
            return nc.values_load_multi_w_load_instructions(
                tiles_row[0:1, bass.ds(first, U)], engines=[engine], min_val=0, max_val=TILES - 1,
                skip_runtime_bounds_check_because="t(v) is clipped to the last tile when the list is made")[1]

        @block.sync
        def _(sp):
            def row_layout(to, of, rows_, s):
                full = E // COLS
                sp.dma_start(to[0:full, :], of[0:full * COLS].rearrange("(p c) -> p c", c=COLS)).then_inc(s, 16)
                sp.dma_start(to[full:full + 1, 0:E - full * COLS],
                             of[full * COLS:E].rearrange("(p c) -> p c", p=1)).then_inc(s, 16)

            sp.wait_ge(s_const, 15)
            row_layout(dst_far, dst, COLS, s_edges)
            row_layout(src_far, src, COLS, s_edges)
            row_layout(src_zero, src, COLS, s_edges)
            row_layout(w_row, edge_weight, COLS, s_edges)
            row_layout(dst_zero, dst, COLS, s_edges)
            sp.wait_ge(s_edges, 16 * 10)
            for to, of in ((edge_key, dst_far), (edge_oth, src_zero), (edge_w, w_row)):
                sp.dma_start(to.rearrange("c e -> (c e)").rearrange("(p c) -> p c", c=COLS), of).then_inc(s_list, 16)
            sp.dma_start(X[:, 0:TILES - 1, :], x[0:(TILES - 1) * P, :].rearrange("(t p) f -> p t f", p=P)).then_inc(s_xin, 16)
            sp.dma_start(X[0:NODES_LAST, TILES - 1, :], x[(TILES - 1) * P:N, :]).then_inc(s_xin, 16)
            for k, w in enumerate((W1, W2, W3, gWl, gWr)):
                sp.dma_start(W[:, k, :], w).then_inc(s_w, 16)
            for k, w in ((5, sWl1), (7, sWr1)):
                sp.dma_start(W[:, k:k + 2, :], w.rearrange("f (a b) -> f a b", a=2)).then_inc(s_w, 16)
            for k, w in ((9, sWl2), (11, sWr2)):
                sp.dma_start(W[:, k:k + 2, :], w.rearrange("(a f) b -> f a b", a=2)).then_inc(s_w, 16)
            for k, w in ((13, mW1), (14, mW2)):
                sp.dma_start(W[:, k, :], w).then_inc(s_w, 16)
            for k, b in enumerate((b1, b2, b3, sbl2, mb1, mb2, gbl, gbr, gbias, gWe.rearrange("a b -> (a b)"), gatt.rearrange("a b -> (a b)"))):
                sp.dma_start(brow[:, k, :], b.rearrange("(a f) -> a f", a=1).to_broadcast([P, D])).then_inc(s_w, 16)
            with nc.allow_non_contiguous_dma(reason="256 numbers, one to a partition"):
                sp.dma_start(bcol[:, :], sbl1.rearrange("(a f) -> f a", a=2)).then_inc(s_w, 16)
            sp.wait_ge(s_list, 48)
            sp.wait_ge(s_deg, 1)
            with nc.allow_non_contiguous_dma(reason="the first key of each chunk"):
                sp.dma_start(firsts_i[:, 0:CH2], edge_key[:, 0:1].rearrange("c a -> a c")).then_inc(s_first, 16)
            sp.wait_ge(s_go, go("tvT A"))
            for g in range(VT):
                sp.dma_start(tiles_row[0:1, g * P:(g + 1) * P], tvT[g:g + 1, :]).then_inc(s_tv, 16)

            def rows_out(k, n, buf):
                sp.dma_start(tab[k][n * BT * P:(n + 1) * BT * P, :].rearrange("(t p) f -> p t f", p=P),
                             buf[:, n * BT:(n + 1) * BT, :]).then_inc(s_tab, 16)

            def table(name, buf):
                for n in range(NB):
                    sp.wait_ge(s_up, up(name, n))
                    rows_out(TABLES.index(name), n, buf)

            table("t0", Y)
            table("t1", Y)
            table("t2", Y)
            table("x_l", Z)
            with sp.Fori(0, ROUNDS) as i:
                for j in range(RING):
                    sp.wait_ge(s_gath[j], i * (16 * U) + 16 * U * (3 * ROUNDS + 1))
                    sp.dma_start(gathered[bass.ds(i * (RING * P) + j * P, P), :], msg[:, j, :, :].rearrange("p u f -> p (u f)")).then_inc(s_store[j], 16)
            sp.wait_ge(s_add, U * GROUPS * 4 + 2 * U)
            sp.dma_start(Z[:, :, :], tab[3].rearrange("(t p) f -> p t f", p=P)).then_inc(s_xlback, 16)
            sp.wait_ge(s_go, go("shifted"))
            sp.dma_start(Z[:, :, :], tab[3].rearrange("(t p) f -> p t f", p=P)).then_inc(s_xlback, 16)
            with sp.Fori(0, ROUNDS) as i:
                for j in range(RING):
                    sp.wait_ge(s_mm, i * RING + (4 * GROUPS + j + 1))
                    sp.dma_start(msg[:, j, :, :].rearrange("p u f -> p (u f)"), gathered[bass.ds(i * (RING * P) + j * P, P), :]).then_inc(s_back[j], 16)
            table("x2", X)
            for h in range(2):
                sp.wait_ge(s_scat[h], 16 * U * (COLS // (2 * U)))
            with nc.allow_non_contiguous_dma(reason="the first key of each chunk"):
                sp.dma_start(firsts_i[:, 0:CH2], pairs.rearrange("(c e) a -> c (e a)", e=P)[:, 0:1].rearrange("c a -> a c")).then_inc(s_first, 16)
            table("p", Y)
            sp.wait_ge(s_go, go("tvT B"))
            sp.wait_ge(s_add, U * GROUPS * 7 + 2 * U)
            for g in range(VT):
                sp.dma_start(tiles_row[0:1, g * P:(g + 1) * P], tvT[g:g + 1, :]).then_inc(s_tv, 16)
            table("x3", X)
            table("h3", Y)
            for n in range(NB):
                sp.wait_ge(s_up, up("x4", n))
                full = BT if n < NB - 1 else BT - 1
                sp.dma_start(out[n * BT * P:(n * BT + full) * P, :].rearrange("(t p) f -> p t f", p=P), X[:, n * BT:n * BT + full, :]).then_inc(s_out, 16)
            sp.dma_start(out[(TILES - 1) * P:N, :], X[0:NODES_LAST, TILES - 1, :]).then_inc(s_out, 16)
            sp.wait_ge(s_out, 16 * (NB + 1))

        @block.gpsimd
        def _(pool):
            pool.memset(dst_far, FAR).then_inc(s_const, 1)
            pool.memset(src_far, FAR).then_inc(s_const, 1)
            pool.memset(dst_zero, 0).then_inc(s_const, 1)
            pool.memset(src_zero, 0).then_inc(s_const, 1)
            pool.memset(w_row, 0.0).then_inc(s_const, 1)
            pool.memset(X[:, TILES - 1, :], 0.0).then_inc(s_const, 1)
            pool.memset(ident[:, :], 0.0).then_inc(s_const, 1)
            pool.memset(ones[:, :], 1.0).then_inc(s_const, 1)
            pool.memset(zeros[:, :], 0.0).then_inc(s_const, 1)
            pool.memset(epsb[:, :], EPS).then_inc(s_const, 1)
            pool.iota(iota_i, pattern=[[1, P]], base=0, channel_multiplier=0).then_inc(s_const, 1)
            pool.iota(chunk_no[:, :], pattern=[[1, COLS]], base=0, channel_multiplier=0, allow_small_or_imprecise_dtypes=True).then_inc(s_const, 1)
            pool.iota(vcol_i[:, :], pattern=[[P, VT]], base=0, channel_multiplier=1).then_inc(s_const, 1)
            pool.wait_ge(s_const, 13)
            pool.affine_select(out=ident[:, :], in_=ident[:, :], compare_op=ALU.not_equal, fill=1.0, base=0,
                               pattern=[[-1, P]], channel_multiplier=1).then_inc(s_const, 1)
            pool.affine_select(out=lower[:, :], in_=ones[:, :], compare_op=ALU.is_ge, fill=0.0, base=-1,
                               pattern=[[1, P]], channel_multiplier=-1).then_inc(s_const, 1)

            pool.wait_ge(s_go, go("cvA"))
            for g in range(VT):
                for a, of in enumerate((edge_key, edge_oth, edge_w)):
                    to = rows if a == 2 else rowsi
                    pool.indirect_dma_start(to[:, g, a, :], None, of[:, :],
                                            bass.IndirectOffsetOnAxis(ap=cvi[:, g:g + 1].bitcast(U32), axis=0)).then_inc(s_rows, 16)
            def gather_list_b():
                pool.wait_ge(s_go, go("cvB"))
                for g in range(VT):
                    pool.indirect_dma_start(prow[:, g, :, :].rearrange("p e a -> p (e a)"), None,
                                            pairs.rearrange("(c e) a -> c (e a)", e=P),
                                            bass.IndirectOffsetOnAxis(ap=cvi[:, g:g + 1].bitcast(U32), axis=0)).then_inc(s_rows, 16)

            def scatter(i, b, first):
                if not first:
                    pool.wait_ge(s_scat[b], i * (16 * U))
                    pool.sem_inc(s_pass, 1)
                cols = slice(b * U, (b + 1) * U) if first else bass.ds(i * (2 * U) + b * U, U)
                pool.tensor_copy(scat_rec[:, b, :, 0], src_far[:, cols])
                pool.tensor_copy(scat_rec[:, b, :, 1], dst_zero[:, cols])
                pool.tensor_copy(scat_pos[:, b, :], posi[:, cols]).then_inc(s_scst, 1)
                pool.wait_ge(s_scst, b + 1 if first else i * 2 + (b + 1))
                pool.sem_inc(s_pass, 1)
                for u in range(U):
                    pool.indirect_dma_start(pairs[:, :], bass.IndirectOffsetOnAxis(ap=scat_pos[:, b, u:u + 1].bitcast(U32), axis=0),
                                            scat_rec[:, b, u, :], None).then_inc(s_scat[b], 16)

            def walk(k, cuts={}):
                for a, z in segments(cuts):
                    if a:
                        cuts[a]()
                    with pool.Fori(a, z) as i:
                        for j in range(RING):
                            pool.wait_ge(s_staged, i * RING + (gathers_before(k) * GROUPS + j + 1))
                            pool.sem_inc(s_pass, 1)
                            for u in range(U):
                                pool.indirect_dma_start(msg[:, j, u, :], None, tab[gathers_before(k)][:, :],
                                                        bass.IndirectOffsetOnAxis(ap=stage[:, j * U + u:j * U + u + 1].bitcast(U32), axis=0)).then_inc(s_gath[j], 16)

            for k in range(4):
                walk(k)
            pool.wait_ge(s_go, go("positions"))
            for j in range(RING):
                pool.wait_ge(s_gath[j], 16 * U * 4 * ROUNDS)
            for b in range(2):
                scatter(0, b, True)
            with pool.Fori(1, COLS // (2 * U)) as i:
                for b in range(2):
                    scatter(i, b, False)
            walk(5, {14: gather_list_b})
            for k in (6, 7, 8):
                walk(k)

        @block.scalar
        def _(act):
            def walk(k, idx):
                act.wait_ge(s_tab, 16 * NB * (gathers_before(k) + 1))
                with act.Fori(0, ROUNDS) as i:
                    for j in range(RING):
                        act.wait_ge(s_mm, i * RING + (k * GROUPS + j + 1))
                        act.copy(stage[:, j * U:(j + 1) * U], idx[:, bass.ds(i * (RING * U) + j * U, U)]).then_inc(s_staged, 1)

            def root(milestone, of, n):
                act.wait_ge(s_go, go(milestone))
                act.activation(of, of, ACT.Sqrt).then_inc(s_root, 1)

            def roots(m):
                for n in range(NB):
                    act.wait_ge(s_var, m * NB + n + 1)
                    part = stat[:, 1, n * BT:(n + 1) * BT]
                    act.activation(part, part, ACT.Sqrt).then_inc(s_root, 1)

            root("degrees", dinv[:, :], 0)
            walk(0, idxA)
            walk(1, idxA)
            walk(2, idxA)
            roots(0)
            act.wait_ge(s_tab, stored("x_l"))
            with act.Fori(0, ROUNDS) as i:
                for j in range(RING):
                    act.wait_ge(s_add, i * (RING * U) + (U * (3 * GROUPS + j - RING + 1) + 2 * U))
                    act.copy(stage[:, j * U:(j + 1) * U], idxA[:, bass.ds(i * (RING * U) + j * U, U)]).then_inc(s_staged, 1)
                    act.wait_ge(s_oT, i * RING + (j + 1))
                    act.copy(diag[:, j % 2, :, :], pm[:, j % 2, :].rearrange("p (u f) -> p u f", f=P)).then_inc(s_oTc, 1)
            act.wait_ge(s_go, go("shifted"))
            act.activation(ext[:, :, 0:H], ext[:, :, 0:H], ACT.Exp).then_inc(s_exp, 1)
            act.wait_ge(s_go, go("self shifted"))
            act.activation(c12, c12, ACT.Exp).then_inc(s_exp, 1)
            roots(1)
            for h in range(2):
                act.wait_ge(s_scat[h], 16 * U * (COLS // (2 * U)))
            walk(5, idxA)
            act.wait_ge(s_w, 16 * 23)
            for n in range(26):
                b = BATCH["hidden"] + n
                act.wait_ge(s_pe, b + 1)
                a, c = n // 13, n % 13
                w = min(512, TW - c * 512)
                act.activation((Vf if a == 0 else Zf)[:, c * 512:c * 512 + w], pm[:, b % 2, 0:w], ACT.Relu,
                               bias=bcol[:, a:a + 1]).then_inc(s_ev[b % 2], 1)
            walk(6, idxA)
            roots(2)
            walk(7, idxB)
            walk(8, idxB)
            roots(3)

        @block.tensor
        def _(pe):
            pe.sem_inc(s_mm, RING)
            pe.sem_inc(s_dmm, 2)
            pe.wait_ge(s_const, 15)

            def room(b):
                if b >= 2:
                    pe.wait_ge(s_ev[b % 2], (b - 2) // 2 + 1)

            def turns(stage_name, n, of, ready=None):
                for k in range(-(-n // BT)):
                    b = BATCH[stage_name] + k
                    room(b)
                    if ready:
                        pe.wait_ge(s_up, up(ready, k))
                    for i in range(min(BT, n - k * BT)):
                        m = of(k * BT + i)
                        last = pe.transpose(pm[0:m.shape[1], b % 2, i * P:i * P + m.shape[0]], m, ident[0:m.shape[0], 0:m.shape[0]])
                    last.then_inc(s_pe, 1)

            def broadcast_firsts(name):
                b = BATCH["broadcast " + name]
                pe.wait_ge(s_go, go("firsts " + name))
                room(b)
                pe.matmul(pm[:, b % 2, 0:512], ones[0:1, :], firsts[:, 0:512], start=True, stop=True)
                pe.matmul(pm[:, b % 2, 512:COLS], ones[0:1, :], firsts[:, 512:COLS], start=True, stop=True).then_inc(s_pe, 1)

            def turn_tiles(name):
                pe.wait_ge(s_go, go("cv" + name))
                turns("tv" + name, 1, lambda i: tvc)

            def turn_lists(name):
                pe.wait_ge(s_go, go("rows " + name))
                turns("rel" + name, VT, lambda g: relR[:, g, :])
                turns("idx" + name, VT, lambda g: othR[:, g, :])
                if name == "A":
                    turns("weights", VT, lambda g: rows[:, g, 2, :])

            def degree_step(b, h, sem_value):
                pe.wait_ge(s_doh, sem_value)
                for u in range(U):
                    last = pe.matmul(deg_ps[b], ohl[:, h, :, u], ohh[:, h, :, u], start=False, stop=False, skip_group_check=True)
                last.then_inc(s_dmm, 1)

            def degree_ends(b, first):
                last = pe.matmul(deg_ps[b], zeros[:, :], zeros[:, 0:TILES], start=first, stop=not first, skip_group_check=True)
                if not first:
                    last.then_inc(s_deg, 1)

            pe.wait_ge(s_go, go("halves"))
            degree_ends(0, True)
            with pe.Fori(0, COLS // (2 * U)) as i:
                for h in range(2):
                    degree_step(0, h, i * 2 + (h + 1))
            degree_ends(0, False)
            broadcast_firsts("A")
            turn_tiles("A")
            turn_lists("A")
            pe.wait_ge(s_w, 16 * 23)
            turns("turn mW", 2, lambda i: W[:, 13 + i, :])

            def walk(k, nodes_first, cuts={}, degrees=False):
                for a, z in segments(cuts):
                    if a:
                        cuts[a]()
                    with pe.Fori(a, z) as i:
                        for j in range(RING):
                            G = i * RING + (k * GROUPS + j)
                            pe.wait_ge(s_oh, i * RING + (k * (GROUPS + 1) + j + 1))
                            pe.wait_ge(s_add, G * U + U)
                            pe.wait_ge(s_gath[j], i * (16 * U) + 16 * U * (gathers_before(k) * ROUNDS + 1))
                            for u in range(U):
                                if nodes_first:
                                    last = pe.matmul(ps[:, j % 2, u, :], oh[:, j % 2, u, :], msg[:, j, u, :], start=True, stop=True)
                                else:
                                    last = pe.matmul(ps[:, j % 2, u, :], msg[:, j, u, :], oh[:, j % 2, u, :], start=True, stop=True)
                            last.then_inc(s_mm, 1)
                            if degrees:
                                degree_step(1, j % 2, i * RING + (COLS // U + j + 1))

            def products(stage_name, pairs_of):
                for k in range(NB):
                    b = BATCH[stage_name] + k
                    room(b)
                    for i in range(BT):
                        ab = pairs_of(k * BT + i)
                        for n, (lhsT, rhs) in enumerate(ab):
                            last = pe.matmul(pm[:, b % 2, i * P:(i + 1) * P], lhsT, rhs, start=(n == 0), stop=(n == len(ab) - 1))
                    last.then_inc(s_pe, 1)

            def passed(k):
                pe.wait_ge(s_add, U * GROUPS * (k + 1) + 2 * U)

            def bins():
                b = BATCH["bins"]
                pe.wait_ge(s_go, go("counts"))
                room(b)
                pe.matmul(pm[:, b % 2, 0:BINS2], lower[:, :], cnt, start=True, stop=True)
                pe.matmul(pm[:, b % 2, 512:512 + BINS2], ones[:, :], cnt, start=True, stop=True).then_inc(s_pe, 1)

            for k in range(3):
                turns(f"self {k}", TILES, lambda t: Y[:, t, :], f"t{k}")
                walk(k, False)
                passed(k)
                products(f"gcn {k}", lambda t: [(acc[:, t, :], W[:, k, :])])
                if k == 0:
                    bins()
            turns("turn X1", TILES, lambda t: X[:, t, :], "x1")
            for h in range(2):
                pe.wait_ge(s_ev[h], (BATCH["x_l"] + 1 - h) // 2)
            products("x_l", lambda t: [(Y[:, t, :], W[:, 3, :])])
            products("x_r", lambda t: [(Y[:, t, :], W[:, 4, :])])
            for h in range(2):
                pe.wait_ge(s_ev[h], (BATCH["rows of keys"] + 1 - h) // 2)
            with pe.Fori(0, ROUNDS) as i:
                for j in range(RING):
                    G = i * RING + (3 * GROUPS + j)
                    pe.wait_ge(s_oh, i * RING + (3 * (GROUPS + 1) + j + 1))
                    for u in range(U):
                        last = pe.transpose(pm[:, j % 2, u * P:(u + 1) * P], oh[:, j % 2, u, :], ident[:, :])
                    last.then_inc(s_oT, 1)
                    tiles = tiles_of(mybir.EngineType.PE, i * (RING * U) + j * U)
                    pe.wait_ge(s_oTc, i * RING + (j + 1))
                    pe.wait_ge(s_add, G * U + U)
                    for u, t in enumerate(tiles):
                        last = pe.matmul(ps[:, j % 2, u, :], diag[:, j % 2, u, :], Vf[:, bass.ds(t * P, P)], start=True, stop=True)
                    last.then_inc(s_mm, 1)

            pe.wait_ge(s_add, U * GROUPS * 4 + 2 * U)
            turns("rows of keys", VT, lambda g: relA[:, g * P:(g + 1) * P])
            turns("rows of weights", VT, lambda g: wA[:, g * P:(g + 1) * P])
            for h in range(H):
                turns(f"rows of scores {h}", VT, lambda g: ext[:, g * P:min((g + 1) * P, VISITS), h])
            pe.wait_ge(s_go, go("carry sources"))
            for q in range(5):
                turns(f"ends {q}", VT, lambda g: ends[:, q, g, :])
            pe.wait_ge(s_go, go("carries"))
            for q in range(3):
                turns(f"carries {q}", VT, lambda g: crow[q][:, g * P:(g + 1) * P])
            pe.wait_ge(s_go, go("largest"))
            turns("lasts", VT, lambda g: lastR[:, g, :])
            for c in range(C5):
                turns(f"largest {c}", VT, lambda g: F5[:, c, g, :])

            for h in range(2):
                pe.wait_ge(s_ev[h], (BATCH["turn X"] + 1 - h) // 2)
            with pe.Fori(0, ROUNDS) as i:
                for j in range(RING):
                    G = i * RING + (4 * GROUPS + j)
                    pe.wait_ge(s_oh, i * RING + (4 * (GROUPS + 1) + j + 1))
                    pe.wait_ge(s_add, G * U + U)
                    pe.wait_ge(s_msgs, i * RING + (j + 1))
                    for u in range(U):
                        to = gsum(j % 2, u)
                        pe.matmul(to[:, 0:D], oh[:, j % 2, u, :], msg[:, j, u, :], start=True, stop=True)
                        last = pe.matmul(to[:, D:GW], oh[:, j % 2, u, :], extf[:, bass.ds(i * (RING * U * EXT) + (j * U + u) * EXT, EXT)], start=True, stop=True)
                    last.then_inc(s_mm, 1)
            passed(4)

            turns("turn X", TILES, lambda t: X[:, t, :], "x2")
            walk(5, False, {6: lambda: broadcast_firsts("B"), 12: lambda: turn_tiles("B"), 20: lambda: turn_lists("B")})
            passed(5)
            for n in range(NB):
                b = BATCH["rdeg"] + n
                room(b)
                pe.wait_ge(s_diag, n + 1)
                for i in range(BT):
                    last = pe.matmul(pm[:, b % 2, i * P:(i + 1) * P], ones[:, :], diag[:, n % 2, i, :], start=True, stop=True)
                last.then_inc(s_pe, 1)
            pe.wait_ge(s_go, go("scaled"))
            for n in range(26):
                b = BATCH["hidden"] + n
                a, c = n // 13, n % 13
                w = min(512, TW - c * 512)
                room(b)
                pe.matmul(pm[:, b % 2, 0:w], W[:, 5 + a, :], accf[:, c * 512:c * 512 + w], start=True, stop=False)
                pe.matmul(pm[:, b % 2, 0:w], W[:, 7 + a, :], Yf[:, c * 512:c * 512 + w], start=False, stop=True).then_inc(s_pe, 1)
            for b in range(2):
                pe.wait_ge(s_ev[b], (BATCH["p"] + 1 - b) // 2)
            products("p", lambda t: [(V[:, t, :], W[:, 9, :]), (Z[:, t, :], W[:, 10, :])])
            products("q", lambda t: [(V[:, t, :], W[:, 11, :]), (Z[:, t, :], W[:, 12, :])])
            for h in range(2):
                pe.wait_ge(s_ev[h], (BATCH["mean 0"] + 1 - h) // 2)
            degree_ends(1, True)
            walk(6, True, degrees=True)
            degree_ends(1, False)
            walk(7, False)
            passed(7)
            products("mean 0", lambda t: [(acc[:, t, :], W[:, 13, :])])
            walk(8, False)
            passed(8)
            products("mean 1", lambda t: [(acc[:, t, :], W[:, 14, :])])

        @block.vector
        def _(dve):
            n_chain = [0]
            n_go = [0]

            def link(ins):
                n_chain[0] += 1
                ins.then_inc(s_chain, 1)
                dve.wait_ge(s_chain, n_chain[0])

            def reached(name):
                n_go[0] += 1
                assert go(name) == n_go[0], name
                dve.sem_inc(s_go, 1)

            n_up = [0]

            def arose(name, n):
                n_up[0] += 1
                assert up(name, n) == n_up[0], name
                dve.sem_inc(s_up, 1)

            def wide(a, n=D):
                return a.rearrange("p (t o) -> p t o", o=1).to_broadcast([P, a.shape[1], n])

            def over(a, n=TILES):
                return a.rearrange("p (o f) -> p o f", o=1).to_broadcast([P, n, a.shape[1]])

            dve.sem_inc(s_add, 2 * U)
            dve.sem_inc(s_bin, 1)
            dve.wait_ge(s_const, 15)
            link(dve.tensor_copy(iota_f[:, :], iota_i))
            link(dve.tensor_copy(vcol[:, :], vcol_i[:, :]))
            dve.wait_ge(s_edges, 16 * 10)
            def node_halves(node, hi, lo):
                link(dve.tensor_scalar(hi_i, node, 7, None, ALU.logical_shift_right))
                link(dve.tensor_copy(hi_f, hi_i))
                link(dve.tensor_copy(lo_f, node))
                link(dve.scalar_tensor_tensor(out=lo, in0=hi_f, scalar=-128.0, in1=lo_f, op0=ALU.mult, op1=ALU.add))
                link(dve.tensor_scalar(hi, hi_f, float(BINS - 1), None, ALU.min))

            def source_halves():
                link(dve.memset(hi_src, float(BINS2 + 8)))
                link(dve.memset(lo_src, 0.0))
                link(dve.tensor_copy(iota8, iota_f[:, :].rearrange("p (n o) -> p n o", o=1).to_broadcast([P, P, U])))
                node_halves(src_far, hi_src[:, 0:COLS], lo_src[:, 0:COLS])

            source_halves()
            node_halves(dst_far, hi_dst, lo_dst)
            reached("halves")

            def degree_step(hi, lo, first, h, at):
                dve.wait_ge(s_dmm, at)
                cols = lambda a, n: a[:, first].rearrange("p (o u) -> p o u", o=1).to_broadcast([P, n, U])
                dve.tensor_tensor(ohh[:, h, :, :], iota8[:, 0:TILES, :], cols(hi, TILES), ALU.is_equal)
                dve.tensor_tensor(ohl[:, h, :, :], iota8, cols(lo, P), ALU.is_equal).then_inc(s_doh, 1)

            with dve.Fori(0, COLS // (2 * U)) as i:
                for h in range(2):
                    degree_step(hi_dst, lo_dst, bass.ds(i * (2 * U) + h * U, U), h, i * 2 + (h + 1))

            def count_bin(at, col):
                dve.wait_ge(s_bin, at + 1)
                dve.tensor_scalar(mask, hi_src[:, 0:COLS], iota_f[:, col], 0.0, ALU.is_equal, ALU.add,
                                  accum_out=cnt[:, col]).then_inc(s_bin, 1)

            def bin_bases():
                b = BATCH["bins"]
                dve.wait_ge(s_pe, b + 1)
                link(dve.tensor_copy(tot, pm[:, b % 2, 512:512 + BINS2]))
                link(dve.tensor_tensor_scan(run, ones[:, 0:BINS2], tot, 0.0, ALU.mult, ALU.add))
                link(dve.tensor_tensor(run, run, tot, ALU.subtract))
                link(dve.scalar_tensor_tensor(out=base, in0=run, scalar=-1.0, in1=pm[:, b % 2, 0:BINS2], op0=ALU.add, op1=ALU.add))
                dve.sem_inc(s_ev[b % 2], 1)
                link(dve.memset(pos, 0.0))
                link(dve.memset(onesw, 1.0))

            def number_bin(at, col):
                dve.wait_ge(s_bin, at + (BINS2 + 1))
                dve.tensor_scalar(mask, hi_src[:, 0:COLS], iota_f[:, col], None, ALU.is_equal).then_inc(s_bin, 1)
                dve.wait_ge(s_bin, at + (BINS2 + 2))
                dve.tensor_tensor_scan(cum, onesw, mask, base[:, col], ALU.mult, ALU.add).then_inc(s_bin, 1)
                dve.wait_ge(s_bin, at + (BINS2 + 3))
                dve.sem_inc(s_dpass, 1)
                dve.copy_predicated(pos, mask.bitcast(I32), cum).then_inc(s_bin, 1)

            def evac(name, n, of):
                for k in range(n):
                    b = BATCH[name] + k
                    dve.wait_ge(s_pe, b + 1)
                    of(k, pmv(b % 2))
                    dve.sem_inc(s_ev[b % 2], 1)

            def list_firsts(name):
                dve.wait_ge(s_first, 16 if name == "A" else 32)
                link(dve.tensor_scalar(firsts_s, firsts_i, 7, None, ALU.logical_shift_right))
                link(dve.tensor_copy(firsts, firsts_s))
                link(dve.tensor_tensor(firsts, firsts, chunk_no[:, :], ALU.add))
                reached("firsts " + name)

            def list_chunks(name):
                b = BATCH["broadcast " + name]
                dve.wait_ge(s_pe, b + 1)
                for g in range(VT):
                    link(dve.tensor_scalar(before[:, 0:CHUNKS - 1], pm[:, b % 2, 1:CHUNKS], vcol[:, g:g + 1], None, ALU.is_le))
                    link(dve.tensor_reduce(cv[:, g:g + 1], before[:, 0:CHUNKS - 1], AX.X, ALU.add))
                dve.sem_inc(s_ev[b % 2], 1)
                link(dve.tensor_copy(cvi, cv))
                link(dve.tensor_tensor(tv, vcol[:, :], cv, ALU.subtract))
                link(dve.tensor_scalar(tv128, tv, 128.0, None, ALU.mult))
                link(dve.tensor_scalar(tvc, tv, float(TILES - 1), None, ALU.min))
                reached("cv" + name)

            def list_rows(name):
                evac("tv" + name, 1, lambda k, s: link(dve.tensor_copy(tvT[:, :], s[0:VT, 0, :])))
                reached("tvT " + name)
                key_rows, oth_rows = (rowsi[:, :, 0, :], rowsi[:, :, 1, :]) if name == "A" else (prow[:, :, :, 0], prow[:, :, :, 1])
                if name == "B":
                    source_halves()
                dve.wait_ge(s_rows, 16 * VT * (3 if name == "A" else 4))
                link(dve.tensor_copy(relR, key_rows))
                link(dve.tensor_copy(othR, oth_rows))
                link(dve.tensor_tensor(relR, relR, wide(tv128, P), ALU.subtract))
                reached("rows " + name)

            def list_columns(name, rel, idx):
                by_visit = lambda a: a[:, :].rearrange("p (g v) -> p g v", g=VT)
                evac("rel" + name, 1, lambda k, s: link(dve.tensor_copy(by_visit(rel), s)))
                evac("idx" + name, 1, lambda k, s: link(dve.tensor_copy(by_visit(idx), s)))
                if name == "A":
                    evac("weights", 1, lambda k, s: link(dve.tensor_copy(by_visit(wA), s)))

            def finish_degrees():
                link(dve.tensor_scalar(dinv[:, :], deg_ps[0], 1.0, None, ALU.add))
                link(dve.tensor_scalar(degin[:, :], deg_ps[0], 1.0, None, ALU.max))
                link(dve.tensor_scalar(hasin[:, :], deg_ps[0], 1.0, None, ALU.min))
                link(dve.reciprocal(degin[:, :], degin[:, :]))

            dve.wait_ge(s_list, 48)
            dve.wait_ge(s_deg, 1)
            list_firsts("A")
            list_chunks("A")
            list_rows("A")
            list_columns("A", relA, idxA)
            finish_degrees()
            reached("degrees")
            evac("turn mW", 1, lambda k, s: link(dve.tensor_copy(W[:, 13:15, :], s[:, 0:2, :])))
            dve.wait_ge(s_root, 1)
            link(dve.reciprocal(dinv[:, :], dinv[:, :]))
            dve.wait_ge(s_xin, 32)
            dve.wait_ge(s_tv, 16 * VT)

            def onehot(rel, first, j, at):
                dve.wait_ge(s_mm, at)
                dve.tensor_tensor(oh[:, j % 2, :, :], over(iota_f[:, 0:P], U),
                                  rel[:, first].rearrange("p (u o) -> p u o", o=1).to_broadcast([P, U, P]),
                                  ALU.is_equal).then_inc(s_oh, 1)

            def walk(k, rel, cuts={}, extra=None):
                if k:
                    dve.wait_ge(s_oh, k * (GROUPS + 1))
                onehot(rel, slice(0, U), 0, k * GROUPS + RING)
                for a, z in segments(cuts):
                    if a:
                        cuts[a]()
                    with dve.Fori(a, z) as i:
                        for j in range(RING):
                            g8 = i * (RING * U)
                            onehot(rel, bass.ds(g8 + (j + 1) * U, U), j + 1, i * RING + (k * GROUPS + j + RING))
                            if extra:
                                extra(i, j)
                            tiles = tiles_of(mybir.EngineType.DVE, g8 + j * U)
                            dve.wait_ge(s_mm, i * RING + (k * GROUPS + j + 1 + RING))
                            for u, t in enumerate(tiles):
                                dve.wait_ge(s_add, g8 + (U * (k * GROUPS + j) + u + 2 * U))
                                part = accf[:, bass.ds(t * P, P)]
                                dve.tensor_tensor(part, part, ps[:, j % 2, u, :], ALU.add).then_inc(s_add, 1)
                dve.wait_ge(s_add, U * GROUPS * (k + 1) + 2 * U)

            def layer_norm(m, name):
                tiles = lambda a, n: a[:, n * BT:(n + 1) * BT]
                for n in range(NB):
                    z, mean, var = batch_of(Z, n), tiles(stat[:, 0, :], n), tiles(stat[:, 1, :], n)
                    link(dve.tensor_reduce(mean, z, AX.X, ALU.add))
                    link(dve.tensor_scalar(mean, mean, 1.0 / D, None, ALU.mult))
                    link(dve.tensor_tensor(z, z, wide(mean), ALU.subtract))
                    link(dve.tensor_tensor(batch_of(Y, n), z, z, ALU.mult))
                    link(dve.tensor_reduce(var, batch_of(Y, n), AX.X, ALU.add))
                    link(dve.tensor_scalar(var, var, 1.0 / D, EPS, ALU.mult, ALU.add))
                    dve.sem_inc(s_var, 1)
                for n in range(NB):
                    dve.wait_ge(s_root, 1 + m * NB + n + 1)
                    link(dve.reciprocal(tiles(stat[:, 2, :], n), tiles(stat[:, 1, :], n)))
                    link(dve.tensor_tensor(batch_of(X, n), batch_of(Z, n), wide(tiles(stat[:, 2, :], n)), ALU.mult))
                    arose(name, n)

            def batch_of(buf, k):
                return buf[:, k * BT:(k + 1) * BT, :]

            dinv_of = lambda n: wide(dinv[:, n * BT:(n + 1) * BT])
            for n in range(NB):
                link(dve.tensor_tensor(batch_of(Y, n), batch_of(X, n), dinv_of(n), ALU.mult))
                arose("t0", n)
            dve.wait_ge(s_w, 16 * 23)

            def gcn(k):
                def of(n, s):
                    z = batch_of(Z, n)
                    link(dve.tensor_tensor(z, s, dinv_of(n), ALU.mult))
                    link(dve.tensor_tensor(z, z, over(brow[:, k, :], BT), ALU.add))
                    if k < 2:
                        link(dve.scalar_tensor_tensor(out=batch_of(Y, n), in0=z, scalar=0.0, in1=dinv_of(n), op0=ALU.max, op1=ALU.mult))
                        arose(f"t{k + 1}", n)
                    else:
                        link(dve.tensor_tensor(z, z, batch_of(X, n), ALU.add))
                return of

            def counting(i, j):
                if j % 2 == 0:
                    count_bin(i * 2 + j // 2, bass.ds(i * 2 + j // 2, 1))

            def numbering(i, j):
                if j % 2 == 0:
                    number_bin(i * 6 + 3 * (j // 2), bass.ds(i * 2 + j // 2, 1))

            for k in range(3):
                evac(f"self {k}", NB, lambda n, s: link(dve.tensor_copy(batch_of(acc, n), s)))
                walk(k, relA, extra=(counting, numbering, None)[k])
                if k == 0:
                    dve.wait_ge(s_bin, BINS2 + 1)
                    reached("counts")
                if k == 1:
                    dve.wait_ge(s_bin, 4 * BINS2 + 1)
                    link(dve.tensor_copy(posi[:, :], pos))
                    reached("positions")
                dve.wait_ge(s_tab, 16 * NB * (k + 1))
                evac(f"gcn {k}", NB, gcn(k))
                if k == 0:
                    bin_bases()
            layer_norm(0, "x1")

            evac("turn X1", NB, lambda n, s: link(dve.tensor_copy(batch_of(Y, n), s)))
            def x_l(n, s):
                link(dve.tensor_tensor(batch_of(Z, n), s, over(brow[:, 6, :], BT), ALU.add))
                arose("x_l", n)
            evac("x_l", NB, x_l)
            evac("x_r", NB, lambda n, s: link(dve.tensor_tensor(batch_of(V, n), s, over(brow[:, 7, :], BT), ALU.add)))
            We, att = brow[:, 9, :], brow[:, 10, :]

            dve.wait_ge(s_tab, stored("x_l"))
            dve.wait_ge(s_oh, 3 * (GROUPS + 1))
            onehot(relA, slice(0, U), 0, 3 * GROUPS + RING)
            with dve.Fori(0, ROUNDS) as i:
                for j in range(RING):
                    g8 = i * (RING * U)
                    at = i * (RING * 6) + 6 * j
                    onehot(relA, bass.ds(g8 + (j + 1) * U, U), j + 1, i * RING + (3 * GROUPS + j + RING))
                    dve.wait_ge(s_mm, i * RING + (3 * GROUPS + j + 1 + RING))
                    dve.wait_ge(s_gath[j], i * (16 * U) + 16 * U * (3 * ROUNDS + 1))
                    dve.tensor_tensor(sc_a, ps[:, j % 2, :, :], msg[:, j, :, :], ALU.add).then_inc(s_p1, 1)
                    dve.tensor_tensor(sc_b, over(We, U), wA[:, bass.ds(g8 + j * U, U)].rearrange("p (u o) -> p u o", o=1).to_broadcast([P, U, D]),
                                      ALU.mult).then_inc(s_p1, 1)
                    dve.wait_ge(s_p1, at + 2)
                    dve.tensor_tensor(sc_a, sc_a, sc_b, ALU.add).then_inc(s_p1, 1)
                    dve.wait_ge(s_p1, at + 3)
                    dve.scalar_tensor_tensor(out=sc_b, in0=sc_a, scalar=0.2, in1=sc_a, op0=ALU.mult, op1=ALU.max).then_inc(s_p1, 1)
                    dve.wait_ge(s_p1, at + 4)
                    dve.tensor_tensor(sc_a, sc_b, over(att, U), ALU.mult).then_inc(s_p1, 1)
                    dve.wait_ge(s_p1, at + 5)
                    dve.tensor_reduce(ext[:, bass.ds(g8 + j * U, U), 0:H], sc_a.rearrange("p u (h c) -> p u h c", h=H), AX.X, ALU.add).then_inc(s_p1, 1)
                    dve.wait_ge(s_p1, at + 6)
                    dve.wait_ge(s_store[j], i * 16 + 16)
                    dve.sem_inc(s_add, U)
            dve.wait_ge(s_add, U * GROUPS * 4 + 2 * U)
            dve.wait_ge(s_xlback, 16)
            link(dve.tensor_tensor(V[:, :, :], V[:, :, :], Z[:, :, :], ALU.add))

            def masks(k, s):
                link(dve.tensor_scalar(tmpR, s, 0.0, None, ALU.is_ge))
                link(dve.scalar_tensor_tensor(out=tmpR, in0=s, scalar=P - 0.5, in1=tmpR, op0=ALU.is_le, op1=ALU.mult))
                link(dve.scalar_tensor_tensor(out=keyR, in0=s, scalar=1.0, in1=tmpR, op0=ALU.add, op1=ALU.mult))
                link(dve.tensor_scalar(keyR, keyR, -1.0, None, ALU.add))
                link(dve.tensor_scalar(tmpR, tmpR, -1.0, BIG, ALU.add, ALU.mult))
            evac("rows of keys", 1, masks)
            link(dve.memset(penF, -BIG))
            link(dve.memset(penB, -BIG))
            link(dve.memset(A5[:, :, VT - 1, :], -BIG))
            link(dve.tensor_tensor(penF[:, :, 1:P], keyR[:, :, 1:P], keyR[:, :, 0:P - 1], ALU.is_equal))
            link(dve.tensor_scalar(penF[:, :, 1:P], penF[:, :, 1:P], -1.0, BIG, ALU.add, ALU.mult))
            link(dve.tensor_copy(penB[:, :, 0:P - 1], penF[:, :, 1:P]))
            link(dve.tensor_reduce(ends[:, 4, :, 0:1].rearrange("p g a -> p (g a)"), penF[:, :, 1:P], AX.X, ALU.min))
            evac("rows of weights", 1, lambda k, s: link(dve.tensor_tensor(A5[:, H, :, :], s, tmpR, ALU.add)))
            VL = VISITS - (VT - 1) * P

            def scores_rows(h):
                def of(k, s):
                    link(dve.tensor_tensor(A5[:, h, 0:VT - 1, :], s[:, 0:VT - 1, :], tmpR[:, 0:VT - 1, :], ALU.add))
                    link(dve.tensor_tensor(A5[0:VL, h, VT - 1, :], s[0:VL, VT - 1, :], tmpR[0:VL, VT - 1, :], ALU.add))
                return of
            for h in range(H):
                evac(f"rows of scores {h}", 1, scores_rows(h))
            flat = lambda a: a.rearrange("p g e -> p (g e)")
            for c in range(C5):
                link(dve.tensor_tensor_scan(flat(F5[:, c, :, :]), flat(penF), flat(A5[:, c, :, :]), -BIG, ALU.add, ALU.max))
                link(dve.tensor_tensor_scan(flat(A5[:, c, :, :])[:, ::-1], flat(penB)[:, ::-1], flat(A5[:, c, :, :])[:, ::-1], -BIG, ALU.add, ALU.max))
            bc = lambda a: a.to_broadcast([P, VT, C5])
            link(dve.tensor_copy(ends[:, 4, :, 1:C5], ends[:, 4, :, 0:1].to_broadcast([P, VT, C5 - 1])))
            link(dve.tensor_copy(ends[:, 0, :, :], F5[:, :, :, P - 1].rearrange("p c g -> p g c")))
            link(dve.tensor_copy(ends[:, 1, :, :], A5[:, :, :, 0].rearrange("p c g -> p g c")))
            link(dve.tensor_copy(ends[:, 2, :, :], bc(keyR[:, :, 0:1])))
            link(dve.tensor_copy(ends[:, 3, :, :], bc(keyR[:, :, P - 1:P])))
            reached("carry sources")
            for q in range(5):
                b = BATCH[f"ends {q}"]
                dve.wait_ge(s_pe, b + 1)
                link(dve.tensor_copy(rowbuf[q], pm[0:C5, b % 2, 0:VP]))
                dve.sem_inc(s_ev[b % 2], 1)
            rF, rB, rfirst, rlast, rwhole, rlink = rowbuf
            link(dve.memset(rlink[:, 0:1], -BIG))
            link(dve.tensor_tensor(rlink[:, 1:VP], rfirst[:, 1:VP], rlast[:, 0:VP - 1], ALU.is_equal))
            link(dve.tensor_scalar(rlink[:, 1:VP], rlink[:, 1:VP], -1.0, BIG, ALU.add, ALU.mult))
            link(dve.tensor_tensor(rfirst, rlink, rwhole, ALU.add))
            link(dve.memset(rlast[:, VP - 1:VP], -BIG))
            link(dve.tensor_tensor(rlast[:, 0:VP - 1], rlink[:, 1:VP], rwhole[:, 0:VP - 1], ALU.add))
            link(dve.tensor_tensor_scan(rF, rfirst, rF, -BIG, ALU.add, ALU.max))
            link(dve.tensor_tensor_scan(rB[:, ::-1], rlast[:, ::-1], rB[:, ::-1], -BIG, ALU.add, ALU.max))
            cF, cB, cL = crow
            for c in (cF[:, 0:1], cB[:, VP - 1:VP], cL[:, VP - 1:VP]):
                link(dve.memset(c, -BIG))
            link(dve.tensor_tensor(cF[:, 1:VP], rF[:, 0:VP - 1], rlink[:, 1:VP], ALU.add))
            link(dve.tensor_tensor(cB[:, 0:VP - 1], rB[:, 1:VP], rlink[:, 1:VP], ALU.add))
            link(dve.tensor_copy(cL[:, 0:VP - 1], rlink[:, 1:VP]))
            reached("carries")
            for q in range(3):
                evac(f"carries {q}", 1, lambda k, s: link(dve.tensor_copy(backs[:, q, :, :], s[:, :, 0:C5])))
            link(dve.tensor_tensor(F5, F5, A5, ALU.max))
            for q, end in ((0, 0), (1, P - 1)):
                link(dve.tensor_tensor(tmpR, keyR, keyR[:, :, end:end + 1].to_broadcast([P, VT, P]), ALU.is_equal))
                link(dve.tensor_scalar(tmpR, tmpR, -1.0, BIG, ALU.add, ALU.mult))
                for c in range(C5):
                    for g in range(VT):
                        link(dve.scalar_tensor_tensor(out=F5[:, c, g, :], in0=tmpR[:, g, :], scalar=backs[:, q, g, c:c + 1],
                                                      in1=F5[:, c, g, :], op0=ALU.add, op1=ALU.max))
            link(dve.tensor_scalar(lastR[:, :, 0:P - 1], penB[:, :, 0:P - 1], -1.0, None, ALU.is_lt))
            link(dve.tensor_scalar(lastR[:, :, P - 1:P], backs[:, 2, :, 0:1], -1.0, None, ALU.is_lt))
            reached("largest")
            evac("lasts", 1, lambda k, s: link(dve.tensor_copy(lastT.rearrange("p (g e) -> p g e", g=VT), s)))
            for c in range(C5):
                def shift(k, s):
                    m = s.rearrange("p g e -> p (g e)")[:, 0:VISITS]
                    link(dve.tensor_tensor(ext[:, :, H + c], m, lastT[:, 0:VISITS], ALU.mult))
                    if c < H:
                        link(dve.tensor_tensor(ext[:, :, c], ext[:, :, c], m, ALU.subtract))
                evac(f"largest {c}", 1, shift)
            link(dve.tensor_scalar(ext[:, :, 0:H], ext[:, :, 0:H], 0.0, None, ALU.min))
            link(dve.memset(accG, 0.0))
            reached("shifted")
            dve.wait_ge(s_exp, 1)

            dve.wait_ge(s_oh, 4 * (GROUPS + 1))
            onehot(relA, slice(0, U), 0, 4 * GROUPS + RING)

            def weigh(first, j, at):
                dve.wait_ge(s_back[j], at)
                m = msg[:, j, :, :].rearrange("p u (h c) -> p u h c", h=H)
                w = ext[:, first, 0:H].rearrange("p u (h o) -> p u h o", o=1).to_broadcast([P, U, H, HC])
                dve.tensor_tensor(m, m, w, ALU.mult).then_inc(s_msgs, 1)

            def sum_round(i, last):
                g8 = i * (RING * U)
                for j in range(RING):
                    if not (last and j == RING - 1):
                        onehot(relA, bass.ds(g8 + (j + 1) * U, U), j + 1, i * RING + (4 * GROUPS + j + RING))
                        weigh(bass.ds(g8 + (j + 1) * U, U), (j + 1) % RING, i * 16 + 16 + 16 * (j == RING - 1))
                    tiles = tiles_of(mybir.EngineType.DVE, g8 + j * U)
                    dve.wait_ge(s_mm, i * RING + (4 * GROUPS + j + 1 + RING))
                    for u, t in enumerate(tiles):
                        dve.wait_ge(s_add, g8 + (U * (4 * GROUPS + j) + u + 2 * U))
                        part = accG[:, bass.ds(t * GW, GW)]
                        dve.tensor_tensor(part, part, gsum(j % 2, u), ALU.add).then_inc(s_add, 1)

            weigh(slice(0, U), 0, 16)
            with dve.Fori(0, ROUNDS - 1) as i:
                sum_round(i, False)
            sum_round(ROUNDS - 1, True)
            dve.sem_inc(s_oh, 1)
            dve.wait_ge(s_add, U * GROUPS * 5 + 2 * U)

            aG = accG.rearrange("p (t a) -> p t a", a=GW)
            heads = lambda a: a.rearrange("p t (h c) -> p t h c", h=H)
            per_head = lambda a: a.rearrange("p t (h o) -> p t h o", o=1).to_broadcast([P, TILES, H, HC])
            m_in, m_all, c_in, c_self, den, a_self = small[4], small[5], small[0], small[1], small[2], small[3]
            dve.wait_ge(s_xlback, 32)
            link(dve.tensor_tensor(selfT, aG[:, :, GW - 1:GW].to_broadcast([P, TILES, D]), over(We), ALU.mult))
            link(dve.tensor_tensor(selfT, selfT, V[:, :, :], ALU.add))
            link(dve.scalar_tensor_tensor(out=selfT, in0=selfT, scalar=0.2, in1=selfT, op0=ALU.mult, op1=ALU.max))
            link(dve.tensor_tensor(selfT, selfT, over(att), ALU.mult))
            link(dve.tensor_reduce(a_self, heads(selfT), AX.X, ALU.add))
            link(dve.tensor_scalar(hasin[:, :], hasin[:, :], -1.0, BIG, ALU.add, ALU.mult))
            link(dve.tensor_tensor(m_in, aG[:, :, D + H:D + 2 * H], wide(hasin[:, :], H), ALU.add))
            link(dve.tensor_tensor(m_all, m_in, a_self, ALU.max))
            link(dve.tensor_tensor(c_in, m_in, m_all, ALU.subtract))
            link(dve.tensor_tensor(c_self, a_self, m_all, ALU.subtract))
            reached("self shifted")
            dve.wait_ge(s_exp, 2)
            link(dve.tensor_tensor(den, c_in, aG[:, :, D:D + H], ALU.mult))
            link(dve.tensor_tensor(den, den, c_self, ALU.add))
            link(dve.tensor_scalar(den, den, 1e-16, None, ALU.add))
            link(dve.reciprocal(den, den))
            link(dve.tensor_tensor(c_in, c_in, den, ALU.mult))
            link(dve.tensor_tensor(c_self, c_self, den, ALU.mult))
            link(dve.tensor_tensor(heads(selfT), heads(aG[:, :, 0:D]), per_head(c_in), ALU.mult))
            link(dve.tensor_tensor(heads(Z[:, :, :]), heads(Z[:, :, :]), per_head(c_self), ALU.mult))
            link(dve.tensor_tensor(Z[:, :, :], Z[:, :, :], selfT, ALU.add))
            link(dve.tensor_tensor(Z[:, :, :], Z[:, :, :], over(brow[:, 8, :]), ALU.add))
            link(dve.tensor_tensor(Z[:, :, :], Z[:, :, :], X[:, :, :], ALU.add))
            layer_norm(1, "x2")

            evac("turn X", NB, lambda n, s: link(dve.tensor_copy(batch_of(Y, n), s)))
            link(dve.memset(acc, 0.0))
            walk(5, relA, {3: lambda: list_firsts("B"), 9: lambda: list_chunks("B"), 18: lambda: list_rows("B"),
                                23: lambda: list_columns("B", relB, idxB)})

            def diagonal(n):
                dve.tensor_tensor(diag[:, n % 2, 0:BT, :], over(ident[:, :], BT), wide(degin[:, n * BT:(n + 1) * BT]), ALU.mult).then_inc(s_diag, 1)

            diagonal(0)
            for n in range(NB):
                if n + 1 < NB:
                    diagonal(n + 1)
                b = BATCH["rdeg"] + n
                dve.wait_ge(s_pe, b + 1)
                link(dve.tensor_tensor(batch_of(acc, n), batch_of(acc, n), pmv(b % 2), ALU.mult))
                dve.sem_inc(s_ev[b % 2], 1)
            reached("scaled")
            def p_rows(n, s):
                link(dve.tensor_copy(batch_of(Y, n), s))
                arose("p", n)
            evac("p", NB, p_rows)
            evac("q", NB, lambda n, s: link(dve.tensor_tensor(batch_of(acc, n), s, over(brow[:, 3, :], BT), ALU.add)))
            link(dve.tensor_tensor(Z[:, :, :], acc, X[:, :, :], ALU.add))
            link(dve.memset(acc, 0.0))

            def degrees_out(i, j):
                degree_step(hi_src, lo_src, bass.ds(i * (RING * U) + j * U, U), j % 2, i * RING + (COLS // U + j + 1))
            walk(6, relA, extra=degrees_out)
            for n in range(NB):
                a, z = batch_of(acc, n), batch_of(Z, n)
                link(dve.tensor_tensor(a, a, wide(degin[:, n * BT:(n + 1) * BT]), ALU.mult))
                link(dve.tensor_tensor(z, z, a, ALU.add))
            dve.wait_ge(s_tab, stored("p"))
            layer_norm(2, "x3")
            dve.wait_ge(s_deg, 2)
            link(dve.tensor_scalar(degout[:, :], deg_ps[1], 1.0, None, ALU.max))
            link(dve.reciprocal(degout[:, :], degout[:, :]))
            dve.wait_ge(s_tv, 32 * VT)

            def mean(k):
                def of(n, s):
                    z = batch_of(Z, n)
                    link(dve.tensor_tensor(z, s, wide(degout[:, n * BT:(n + 1) * BT]), ALU.mult))
                    link(dve.tensor_tensor(z, z, over(brow[:, 4 + k, :], BT), ALU.add))
                    if k == 0:
                        link(dve.tensor_scalar(batch_of(Y, n), z, 0.0, None, ALU.max))
                        arose("h3", n)
                    else:
                        link(dve.scalar_tensor_tensor(out=z, in0=z, scalar=0.0, in1=batch_of(X, n), op0=ALU.max, op1=ALU.add))
                return of
            for k in range(2):
                link(dve.memset(acc, 0.0))
                walk(7 + k, relB)
                evac(f"mean {k}", NB, mean(k))
            dve.wait_ge(s_tab, stored("h3"))
            layer_norm(3, "x4")


_INS = ["x", "src", "dst", "edge_weight", "L0_gnn_W1", "L0_gnn_b1", "L0_gnn_W2", "L0_gnn_b2", "L0_gnn_W3", "L0_gnn_b3",
        "L1_gnn_Wl", "L1_gnn_bl", "L1_gnn_Wr", "L1_gnn_br", "L1_gnn_We", "L1_gnn_att", "L1_gnn_bias",
        "L2_gnn_Wl1", "L2_gnn_bl1", "L2_gnn_Wr1", "L2_gnn_Wl2", "L2_gnn_bl2", "L2_gnn_Wr2",
        "L3_gnn_W1", "L3_gnn_b1", "L3_gnn_W2", "L3_gnn_b2"]


def kernel(**inputs):
    import numpy as _np
    import concourse.bacc as _bacc
    from concourse import mybir as _mybir
    from concourse.bass_utils import run_bass_kernel_spmd as _run

    nc = _bacc.Bacc("TRN2", target_bir_lowering=False, num_devices=1)
    arrays, args = {}, []
    for name in _INS:
        a = _np.ascontiguousarray(inputs[name])
        arrays[f"in_{name}_dram"] = a
        args.append(nc.dram_tensor(f"in_{name}_dram", a.shape, _mybir.dt.from_np(a.dtype), kind="ExternalInput").ap())
    shape = inputs["x"].shape
    args.append(nc.dram_tensor("out_0_dram", shape, _mybir.dt.float32, kind="ExternalOutput").ap())
    build(nc, *args)
    r = _run(nc, [arrays], core_ids=[0])
    return r.results[0]["out_0_dram"]
```

```python
from contextlib import ExitStack

import concourse.bass as bass
from concourse import mybir

ALU = mybir.AluOpType
ACT = mybir.ActivationFunctionType
AX = mybir.AxisListType
F32 = mybir.dt.float32
I32 = mybir.dt.int32
U32 = mybir.dt.uint32

P = 128
U = 8
RING = 4
EPS = 1e-5
FAR = 1 << 20


def build(nc, x, src, dst, edge_weight, W1, b1, W2, b2, W3, b3, gWl, gbl, gWr, gbr, gWe, gatt, gbias,
          sWl1, sbl1, sWr1, sWl2, sbl2, sWr2, mW1, mb1, mW2, mb2, out):
    N, D = x.shape
    E = src.shape[0]
    H, HC = gatt.shape
    HID = sWl1.shape[1]
    TILES = -(-N // P)
    CHUNKS = -(-E // P)
    VISITS = -(-(CHUNKS + TILES - 1) // (U * RING)) * U * RING
    GROUPS = VISITS // U
    ROUNDS = GROUPS // RING
    VT = -(-VISITS // P)
    COLS = -(-E // (P * 16)) * 16
    EPAD = COLS * P
    CH2 = EPAD // P
    NPAD = TILES * P
    BINS = TILES + 1
    BINS2 = 2 * ROUNDS
    NODES_LAST = N - (TILES - 1) * P
    TW = TILES * P
    assert D == P and CH2 >= CHUNKS and COLS % 16 == 0

    ctx = ExitStack()
    with ctx:
        def sb(name, shape, dt=F32):
            return ctx.enter_context(nc.sbuf_tensor(name, shape, dt))

        def pb(name, shape, dt=F32):
            return ctx.enter_context(nc.psum_tensor(name, shape, dt))

        def sem(name):
            return ctx.enter_context(nc.semaphore(name))

        def dram(name, shape, dt=F32):
            return nc.dram_tensor(name, shape, dt, kind="Internal").ap()

        tab = [dram(f"tab{k}", (NPAD, D)) for k in range(8)]
        edge_key = dram("edge_key", (CH2, P), I32)
        edge_oth = dram("edge_oth", (CH2, P), I32)
        gathered = dram("gathered", (VISITS // U * P, U * D))
        edge_w = dram("edge_w", (CH2, P))
        pairs = dram("pairs", (EPAD, 2), I32)

        BIG = 1e30
        BF = mybir.dt.bfloat16
        ident = sb("ident", [P, P])
        ones = sb("ones", [P, P])
        lower = sb("lower", [P, P])
        zeros = sb("zeros", [P, P])
        epsb = sb("epsb", [P, 1])
        iota_f = sb("iota_f", [P, P])
        chunk_no = sb("chunk_no", [1, COLS])
        vcol_i = sb("vcol_i", [P, VT], I32)
        vcol = sb("vcol", [P, VT])
        X = sb("X", [P, TILES, D])
        EXT = H + H + 1
        GW = D + EXT
        EXT0 = -(-TILES * GW // 64) * 64
        big = sb("big", [P, max(EXT0 + VISITS * EXT, 2 * TW)])
        acc = big[:, 0:TW].rearrange("p (t f) -> p t f", f=D)
        Y = big[:, TW:2 * TW].rearrange("p (t f) -> p t f", f=D)
        accG = big[:, 0:TILES * GW]
        ext = big[:, EXT0:EXT0 + VISITS * EXT].rearrange("p (v a) -> p v a", a=EXT)
        Z = sb("Z", [P, TILES, D])
        V = sb("V", [P, TILES, D])
        diag = sb("diag", [P, 2, U, P])
        rows_of = sb("rows_of", [P, RING, U, GW])
        msg = rows_of[:, :, :, 0:D]
        oh = sb("oh", [P, 2, U, P])
        idxA = sb("idxA", [P, VT * P], I32)
        relA = sb("relA", [P, VT * P])
        idxB = sb("idxB", [P, VT * P], I32)
        relB = sb("relB", [P, VT * P])
        lst = sb("lst", [P, 40])
        posi = sb("posi", [P, COLS], I32)
        wA = sb("wA", [P, VT * P])
        tiles_row = sb("tiles_row", [1, VT * P], I32)
        tvT = sb("tvT", [VT, P], I32)
        TAIL = 3 * 2 * U
        rec_tail = sb("rec_tail", [P, TAIL, 2], I32)
        stage = sb("stage", [P, 6 * U], I32)
        W = sb("W", [P, 15, D])
        bcol = sb("bcol", [P, 2])
        brow = sb("brow", [P, 11, D])
        degin = sb("degin", [P, TILES])
        dinv = sb("dinv", [P, TILES])
        degout = sb("degout", [P, TILES])
        dinv2 = sb("dinv2", [P, TILES])
        hasin = sb("hasin", [P, TILES])
        stat = sb("stat", [P, 3, TILES])

        banks = pb("banks", [P, 8, 512])
        ps = banks[:, 0:4, :].rearrange("p (h b) (u f) -> p h (b u) f", h=2, f=P)
        pm = banks[:, 4:8, :].rearrange("p (h b) n -> p h (b n)", h=2)

        s_edges = sem("s_edges")
        s_list = sem("s_list")
        s_first = sem("s_first")
        s_tv = sem("s_tv")
        s_rows = sem("s_rows")
        s_up = sem("s_up")
        s_mean = sem("s_mean")
        s_square = sem("s_square")
        s_summed = sem("s_summed")
        s_scaled = sem("s_scaled")
        s_scst = sem("s_scst")
        s_rectail = sem("s_rectail")
        s_root = sem("s_root")
        s_doh = sem("s_doh")
        s_dmm = sem("s_dmm")
        s_deg = sem("s_deg")
        s_diag = sem("s_diag")
        s_bin = sem("s_bin")
        s_oT = sem("s_oT")
        s_oTc = sem("s_oTc")
        s_p1 = sem("s_p1")
        s_xlback = sem("s_xlback")
        s_exp = sem("s_exp")
        s_msgs = sem("s_msgs")
        s_const = sem("s_const")
        s_xin = sem("s_xin")
        s_w = sem("s_w")
        s_chain = sem("s_chain")
        s_staged = sem("s_staged")
        s_pass = sem("s_pass")
        s_dpass = sem("s_dpass")
        s_gath = [sem(f"s_gath{j}") for j in range(RING)]
        s_oh = sem("s_oh")
        s_mm = sem("s_mm")
        s_add = sem("s_add")
        s_tab = sem("s_tab")
        s_pe = sem("s_pe")
        s_ev = [sem("s_ev0"), sem("s_ev1")]
        s_store = [sem(f"s_store{j}") for j in range(RING)]
        s_back = [sem(f"s_back{j}") for j in range(RING)]
        s_scat = [sem("s_scat0"), sem("s_scat1")]
        s_go = sem("s_go")
        s_out = sem("s_out")
        block = ctx.enter_context(nc.Block())
        Xf, Zf, Vf = [t[:, :, :].rearrange("p t f -> p (t f)") for t in (X, Z, V)]
        accf, Yf = big[:, 0:TW], big[:, TW:2 * TW]
        Yi, Zi = Yf.bitcast(I32), Zf.bitcast(I32)
        dst_far, src_zero = Yi[:, 0:COLS], Yi[:, COLS:2 * COLS]
        w_row = Yf[:, 2 * COLS:3 * COLS]
        src_far, dst_zero = relB[:, 0:COLS].bitcast(I32), idxB[:, 0:COLS]
        spare = big[:, 2 * TW:2 * TW + VISITS + P * U // 2].bitcast(BF)
        hi_src, lo_src = spare[:, 0:VISITS], spare[:, VISITS:2 * VISITS]
        iota8 = spare[:, 2 * VISITS:].rearrange("p (n u) -> p n u", u=U)
        hi_i, hi_f, lo_f = Zi[:, 0:COLS], Zf[:, COLS:2 * COLS], Zf[:, 2 * COLS:3 * COLS]
        hi_dst, lo_dst = [Zf[:, (3 + k) * COLS:(4 + k) * COLS].bitcast(BF)[:, 0:COLS] for k in range(2)]
        iota_i = Zi[:, 5 * COLS:5 * COLS + P]
        mask, cum, pos, onesw = [Vf[:, k * COLS:(k + 1) * COLS] for k in range(4)]
        cnt, base, tot, run = [Vf[:, 4 * COLS + 64 * k:4 * COLS + 64 * k + BINS2] for k in range(4)]
        firsts_i = Zi[0:1, 5 * COLS + P:6 * COLS + P]
        before, firsts_s = Zf[:, 6 * COLS + P:7 * COLS + P], Zi[0:1, 6 * COLS + P:7 * COLS + P]
        firsts = Vf[0:1, 5 * VT * P:5 * VT * P + COLS]
        cv, tv, tv128, tvc = [lst[:, 8 * k:8 * k + VT] for k in range(4)]
        cvi = lst[:, 32:32 + VT].bitcast(I32)
        rows = Vf[:, 0:3 * VT * P].rearrange("p (a g e) -> p g a e", a=3, g=VT)
        rowsi = Vf[:, 0:3 * VT * P].bitcast(I32).rearrange("p (a g e) -> p g a e", a=3, g=VT)
        prow = Vf[:, 0:2 * VT * P].bitcast(I32).rearrange("p (g e a) -> p g e a", g=VT, a=2)
        relR = Vf[:, 3 * VT * P:4 * VT * P].rearrange("p (g e) -> p g e", g=VT)
        othR = Vf[:, 4 * VT * P:5 * VT * P].rearrange("p (g e) -> p g e", g=VT)
        ohb = diag[:, :, :, :].rearrange("p b u f -> p (b u f)").bitcast(BF)
        ohl = ohb[:, 0:2 * P * U].rearrange("p (b n u) -> p b n u", b=2, u=U)
        ohh = ohb[:, 2 * P * U:2 * P * U + 2 * TILES * U].rearrange("p (b n u) -> p b n u", b=2, u=U)
        scat_pos = stage[:, 0:2 * U].rearrange("p (b u) -> p b u", b=2)
        scat_rec = stage[:, 2 * U:6 * U].rearrange("p (b u a) -> p b u a", b=2, a=2)
        deg_ps = [banks[:, b, 0:TILES] for b in (0, 6)]

        def gsum(h, u):
            return banks[:, 4 * h + u // 3, (u % 3) * GW:(u % 3 + 1) * GW]

        msgf = rows_of[:, :, :, :].rearrange("p j u f -> p (j u f)")
        VP = VT * P
        sc_a, sc_b = [Zf[:, k * U * D:(k + 1) * U * D].rearrange("p (u f) -> p u f", f=D) for k in range(2)]
        C5_ = H + 1
        A5 = Zf[:, 0:C5_ * VP].rearrange("p (c g e) -> p c g e", c=C5_, g=VT)
        F5 = big[:, 0:C5_ * VP].rearrange("p (c g e) -> p c g e", c=C5_, g=VT)
        keyR, penF, penB, lastR = [msgf[:, k * VP:(k + 1) * VP].rearrange("p (g e) -> p g e", g=VT) for k in range(4)]
        ohf = oh[:, :, :, :].rearrange("p b u f -> p (b u f)")
        ends = msgf[:, 4 * VP:4 * VP + 5 * VT * C5_].rearrange("p (q g c) -> p q g c", q=5, g=VT)
        backs = msgf[:, 4 * VP + 256:4 * VP + 256 + 3 * VT * C5_].rearrange("p (q g c) -> p q g c", q=3, g=VT)
        lastT = ohf[:, 0:VP]
        tmpR = ohf[:, VP:2 * VP].rearrange("p (g e) -> p g e", g=VT)
        diagf = diag[:, :, :, :].rearrange("p b u f -> p (b u f)")
        rowbuf = [Zf[0:C5_, C5_ * VP:(C5_ + 1) * VP], Zf[0:C5_, (C5_ + 1) * VP:(C5_ + 2) * VP],
                  big[0:C5_, C5_ * VP:(C5_ + 1) * VP], big[0:C5_, (C5_ + 1) * VP:(C5_ + 2) * VP],
                  diagf[0:C5_, 0:VP], diagf[0:C5_, VP:2 * VP]]
        crow = [rowbuf[4], rowbuf[2], rowbuf[3]]
        small = [msgf[:, k * TILES * H:(k + 1) * TILES * H].rearrange("p (t h) -> p t h", h=H) for k in range(6)]
        c12 = msgf[:, 0:2 * TILES * H]
        selfT = big[:, EXT0:EXT0 + TW].rearrange("p (t f) -> p t f", f=D)

        def pmv(h, n=7):
            return pm[:, h, 0:n * P].rearrange("p (t f) -> p t f", f=P)

        STAGES = [("broadcast A", 1), ("tvA", 1), ("relA", 1), ("idxA", 1), ("weights", 1), ("turn mW", 1)]
        BT = 7
        NB = TILES // BT
        assert NB * BT == TILES
        for k in range(3):
            STAGES += [(f"self {k}", NB), (f"gcn {k}", NB)] + [("bins", 1)] * (k == 0)
            if k == 2:
                del STAGES[-1]
                STAGES += [(f"gcn 2 batch {n}", 1) for n in range(NB)]
        STAGES += [("turn X1", NB), ("x_l", NB), ("x_r", NB), ("rows of keys", 1), ("rows of weights", 1)]
        STAGES += [(f"rows of scores {h}", 1) for h in range(H)]
        STAGES += [(f"ends {q}", 1) for q in range(5)] + [(f"carries {q}", 1) for q in range(3)]
        C5 = H + 1
        STAGES += [("lasts", 1)] + [(f"largest {c}", 1) for c in range(C5)]
        HC_N = -(-TW // 512)
        chunk_of_batch = lambda n: -(-(n + 1) * BT * P // 512) - 1
        HIDDEN = []
        for c in range(HC_N + 1):
            if c < HC_N:
                HIDDEN += [f"hidden {c} {a}" for a in range(2)]
            HIDDEN += [f"p {n}" for n in range(NB) if chunk_of_batch(n) == c - 1]
        STAGES += [("turn X", NB), ("broadcast B", 1), ("tvB", 1), ("relB", 1), ("idxB", 1), ("rdeg", NB)]
        for step in HIDDEN:
            STAGES += [(step, 1)]
        STAGES += [("q", NB), ("mean 0", NB)] + [(f"mean 1 batch {n}", 1) for n in range(NB)]
        BATCH, n0 = {}, 0
        for name, n in STAGES:
            BATCH[name] = n0
            n0 += n

        GO = ["halves", "firsts A", "cvA", "tvT A", "rows A", "degrees", "counts", "positions",
              "carry sources", "carries", "largest", "shifted", "self shifted",
              "firsts B", "cvB", "tvT B", "rows B"]
        UP = ["t0", "t1", "t2", "x1", "x_l", "x2", "p", "x3", "h3", "x4"]
        TABLES = ["t0", "t1", "t2", "x_l", "x2", "p", "x3", "h3"]

        def up(name, n=NB - 1):
            return UP.index(name) * NB + n + 1

        def stored(name):
            return (TABLES.index(name) + 1) * NB * 16

        def gathers_before(k):
            return k - (k > 4)

        def segments(cuts):
            at = [0, *sorted(cuts), ROUNDS]
            return list(zip(at, at[1:]))

        def go(name):
            return GO.index(name) + 1

        def tiles_of(engine, first):
            return nc.values_load_multi_w_load_instructions(
                tiles_row[0:1, bass.ds(first, U)], engines=[engine], min_val=0, max_val=TILES - 1,
                skip_runtime_bounds_check_because="t(v) is clipped to the last tile when the list is made")[1]

        @block.sync
        def _(sp):
            def row_layout(to, of, s):
                full = E // COLS
                sp.dma_start(to[0:full, :], of[0:full * COLS].rearrange("(p c) -> p c", c=COLS)).then_inc(s, 16)
                sp.dma_start(to[full:full + 1, 0:E - full * COLS],
                             of[full * COLS:E].rearrange("(p c) -> p c", p=1)).then_inc(s, 16)

            sp.wait_ge(s_const, 15)
            row_layout(dst_far, dst, s_edges)
            row_layout(src_far, src, s_edges)
            row_layout(src_zero, src, s_edges)
            row_layout(w_row, edge_weight, s_edges)
            row_layout(dst_zero, dst, s_edges)
            sp.wait_ge(s_edges, 16 * 10)
            for to, of in ((edge_key, dst_far), (edge_oth, src_zero), (edge_w, w_row)):
                sp.dma_start(to.rearrange("c e -> (c e)").rearrange("(p c) -> p c", c=COLS), of).then_inc(s_list, 16)
            sp.wait_ge(s_list, 48)
            with nc.allow_non_contiguous_dma(reason="the first key of each chunk"):
                sp.dma_start(firsts_i[:, 0:CH2], edge_key[:, 0:1].rearrange("c a -> a c")).then_inc(s_first, 16)
            sp.dma_start(X[:, 0:TILES - 1, :], x[0:(TILES - 1) * P, :].rearrange("(t p) f -> p t f", p=P)).then_inc(s_xin, 16)
            sp.dma_start(X[0:NODES_LAST, TILES - 1, :], x[(TILES - 1) * P:N, :]).then_inc(s_xin, 16)
            for k, w in enumerate((W1, W2, W3, gWl, gWr)):
                sp.dma_start(W[:, k, :], w).then_inc(s_w, 16)
            for k, w in ((5, sWl1), (7, sWr1)):
                sp.dma_start(W[:, k:k + 2, :], w.rearrange("f (a b) -> f a b", a=2)).then_inc(s_w, 16)
            for k, w in ((9, sWl2), (11, sWr2)):
                sp.dma_start(W[:, k:k + 2, :], w.rearrange("(a f) b -> f a b", a=2)).then_inc(s_w, 16)
            for k, w in ((13, mW1), (14, mW2)):
                sp.dma_start(W[:, k, :], w).then_inc(s_w, 16)
            for k, b in enumerate((b1, b2, b3, sbl2, mb1, mb2, gbl, gbr, gbias, gWe.rearrange("a b -> (a b)"), gatt.rearrange("a b -> (a b)"))):
                sp.dma_start(brow[:, k, :], b.rearrange("(a f) -> a f", a=1).to_broadcast([P, D])).then_inc(s_w, 16)
            with nc.allow_non_contiguous_dma(reason="256 numbers, one to a partition"):
                sp.dma_start(bcol[:, :], sbl1.rearrange("(a f) -> f a", a=2)).then_inc(s_w, 16)
            sp.wait_ge(s_go, go("tvT A"))
            for g in range(VT):
                sp.dma_start(tiles_row[0:1, g * P:(g + 1) * P], tvT[g:g + 1, :]).then_inc(s_tv, 16)

            def rows_out(k, n, buf):
                sp.dma_start(tab[k][n * BT * P:(n + 1) * BT * P, :].rearrange("(t p) f -> p t f", p=P),
                             buf[:, n * BT:(n + 1) * BT, :]).then_inc(s_tab, 16)

            def table(name, buf):
                for n in range(NB):
                    sp.wait_ge(s_up, up(name, n))
                    rows_out(TABLES.index(name), n, buf)

            table("t0", Y)
            table("t1", Y)
            table("t2", Y)
            table("x_l", Z)
            with sp.Fori(0, ROUNDS) as i:
                for j in range(RING):
                    sp.wait_ge(s_gath[j], i * (16 * U) + 16 * U * (3 * ROUNDS + 1))
                    sp.dma_start(gathered[bass.ds(i * (RING * P) + j * P, P), :].rearrange("p (u f) -> p u f", u=U), msg[:, j, :, :]).then_inc(s_store[j], 16)
            sp.wait_ge(s_add, U * GROUPS * 4 + 2 * U)
            sp.dma_start(Z[:, :, :], tab[3].rearrange("(t p) f -> p t f", p=P)).then_inc(s_xlback, 16)
            sp.wait_ge(s_go, go("shifted"))

            def read_back(a, z):
                with sp.Fori(a, z) as i:
                    for j in range(RING):
                        sp.wait_ge(s_mm, i * RING + (4 * GROUPS + j + 1))
                        sp.dma_start(msg[:, j, :, :], gathered[bass.ds(i * (RING * P) + j * P, P), :].rearrange("p (u f) -> p u f", u=U)).then_inc(s_back[j], 16)

            read_back(0, ROUNDS // 2)
            sp.dma_start(Z[:, :, :], tab[3].rearrange("(t p) f -> p t f", p=P)).then_inc(s_xlback, 16)
            read_back(ROUNDS // 2, ROUNDS)
            table("x2", X)
            for h in range(2):
                sp.wait_ge(s_scat[h], 16 * U * (COLS // (2 * U)))
            with nc.allow_non_contiguous_dma(reason="the first key of each chunk"):
                sp.dma_start(firsts_i[:, 0:CH2], pairs.rearrange("(c e) a -> c (e a)", e=P)[:, 0:1].rearrange("c a -> a c")).then_inc(s_first, 16)
            table("p", Y)
            sp.wait_ge(s_go, go("tvT B"))
            sp.wait_ge(s_add, U * GROUPS * 7 + 2 * U)
            for g in range(VT):
                sp.dma_start(tiles_row[0:1, g * P:(g + 1) * P], tvT[g:g + 1, :]).then_inc(s_tv, 16)
            table("x3", X)
            table("h3", Y)
            for n in range(NB):
                sp.wait_ge(s_up, up("x4", n))
                full = BT if n < NB - 1 else BT - 1
                sp.dma_start(out[n * BT * P:(n * BT + full) * P, :].rearrange("(t p) f -> p t f", p=P), X[:, n * BT:n * BT + full, :]).then_inc(s_out, 16)
            sp.dma_start(out[(TILES - 1) * P:N, :], X[0:NODES_LAST, TILES - 1, :]).then_inc(s_out, 16)
            sp.wait_ge(s_out, 16 * (NB + 1))

        @block.gpsimd
        def _(pool):
            pool.memset(dst_far, FAR).then_inc(s_const, 1)
            pool.memset(src_far, FAR).then_inc(s_const, 1)
            pool.memset(dst_zero, 0).then_inc(s_const, 1)
            pool.memset(src_zero, 0).then_inc(s_const, 1)
            pool.memset(w_row, 0.0).then_inc(s_const, 1)
            pool.memset(X[:, TILES - 1, :], 0.0).then_inc(s_const, 1)
            pool.memset(ident[:, :], 0.0).then_inc(s_const, 1)
            pool.memset(ones[:, :], 1.0).then_inc(s_const, 1)
            pool.memset(zeros[:, :], 0.0).then_inc(s_const, 1)
            pool.memset(epsb[:, :], EPS).then_inc(s_const, 1)
            pool.iota(iota_i, pattern=[[1, P]], base=0, channel_multiplier=0).then_inc(s_const, 1)
            pool.iota(chunk_no[:, :], pattern=[[1, COLS]], base=0, channel_multiplier=0, allow_small_or_imprecise_dtypes=True).then_inc(s_const, 1)
            pool.iota(vcol_i[:, :], pattern=[[P, VT]], base=0, channel_multiplier=1).then_inc(s_const, 1)
            pool.wait_ge(s_const, 13)
            pool.affine_select(out=ident[:, :], in_=ident[:, :], compare_op=ALU.not_equal, fill=1.0, base=0,
                               pattern=[[-1, P]], channel_multiplier=1).then_inc(s_const, 1)
            pool.affine_select(out=lower[:, :], in_=ones[:, :], compare_op=ALU.is_ge, fill=0.0, base=-1,
                               pattern=[[1, P]], channel_multiplier=-1).then_inc(s_const, 1)

            pool.wait_ge(s_go, go("cvA"))
            for g in range(VT):
                for a, of in enumerate((edge_key, edge_oth, edge_w)):
                    to = rows if a == 2 else rowsi
                    pool.indirect_dma_start(to[:, g, a, :], None, of[:, :],
                                            bass.IndirectOffsetOnAxis(ap=cvi[:, g:g + 1].bitcast(U32), axis=0)).then_inc(s_rows, 16)
            def gather_list_b():
                pool.wait_ge(s_go, go("cvB"))
                for g in range(VT):
                    pool.indirect_dma_start(prow[:, g, :, :].rearrange("p e a -> p (e a)"), None,
                                            pairs.rearrange("(c e) a -> c (e a)", e=P),
                                            bass.IndirectOffsetOnAxis(ap=cvi[:, g:g + 1].bitcast(U32), axis=0)).then_inc(s_rows, 16)

            def scatter(i, b):
                pool.wait_ge(s_scst, i * 2 + (b + 1))
                pool.sem_inc(s_pass, 1)
                for u in range(U):
                    pool.indirect_dma_start(pairs[:, :], bass.IndirectOffsetOnAxis(ap=scat_pos[:, b, u:u + 1].bitcast(U32), axis=0),
                                            scat_rec[:, b, u, :], None).then_inc(s_scat[b], 16)

            def walk(k, cuts={}):
                for a, z in segments(cuts):
                    if a:
                        cuts[a]()
                    with pool.Fori(a, z) as i:
                        for j in range(RING):
                            pool.wait_ge(s_staged, i * RING + (gathers_before(k) * GROUPS + j + 1))
                            pool.sem_inc(s_pass, 1)
                            for u in range(U):
                                pool.indirect_dma_start(msg[:, j, u, :], None, tab[gathers_before(k)][:, :],
                                                        bass.IndirectOffsetOnAxis(ap=stage[:, j * U + u:j * U + u + 1].bitcast(U32), axis=0)).then_inc(s_gath[j], 16)

            for k in range(4):
                walk(k)
            with pool.Fori(0, (COLS - TAIL) // (2 * U)) as i:
                for b in range(2):
                    scatter(i, b)
            pool.wait_ge(s_rectail, 1)
            for c in range(TAIL):
                pool.indirect_dma_start(pairs[:, :], bass.IndirectOffsetOnAxis(ap=posi[:, COLS - TAIL + c:COLS - TAIL + c + 1].bitcast(U32), axis=0),
                                        rec_tail[:, c, :], None).then_inc(s_scat[c // U % 2], 16)
            walk(5, {14: gather_list_b})
            for k in (6, 7, 8):
                walk(k)

        @block.scalar
        def _(act):
            def walk(k, idx):
                act.wait_ge(s_tab, 16 * NB * (gathers_before(k) + 1))
                with act.Fori(0, ROUNDS) as i:
                    for j in range(RING):
                        act.wait_ge(s_mm, i * RING + (k * GROUPS + j + 1))
                        act.copy(stage[:, j * U:(j + 1) * U], idx[:, bass.ds(i * (RING * U) + j * U, U)]).then_inc(s_staged, 1)

            def root(milestone, of, n):
                act.wait_ge(s_go, go(milestone))
                act.activation(of, of, ACT.Sqrt).then_inc(s_root, 1)

            def roots(m):
                for n in range(NB):
                    act.wait_ge(s_mean, m * NB + n + 1)
                    for t in range(n * BT, (n + 1) * BT):
                        last = act.activation(Y[:, t, :], Z[:, t, :], ACT.Square, bias=stat[:, 0, t:t + 1], accum_out=stat[:, 1, t:t + 1])
                    last.then_inc(s_square, 1)
                    act.wait_ge(s_square, m * NB + n + 1)
                    part = stat[:, 1, n * BT:(n + 1) * BT]
                    act.activation(part, part, ACT.Sqrt, bias=epsb[:, :], scale=1.0 / D).then_inc(s_root, 1)

            def rectified(k):
                for n in range(NB):
                    act.wait_ge(s_summed, k * NB + n + 1)
                    act.activation(Y[:, n * BT:(n + 1) * BT, :], Z[:, n * BT:(n + 1) * BT, :], ACT.Relu).then_inc(s_up, 1)

            root("degrees", dinv[:, :], 0)
            walk(0, idxA)
            rectified(0)
            walk(1, idxA)
            rectified(1)
            walk(2, idxA)
            roots(0)
            for n in range(NB):
                b = BATCH["turn X1"] + n
                act.wait_ge(s_pe, b + 1)
                act.copy(Y[:, n * BT:(n + 1) * BT, :], pmv(b % 2)).then_inc(s_ev[b % 2], 1)
            act.wait_ge(s_tab, stored("x_l"))
            with act.Fori(0, ROUNDS) as i:
                for j in range(RING):
                    act.wait_ge(s_add, i * (RING * U) + (U * (3 * GROUPS + j - RING + 1) + 2 * U))
                    act.copy(stage[:, j * U:(j + 1) * U], idxA[:, bass.ds(i * (RING * U) + j * U, U)]).then_inc(s_staged, 1)
                    act.wait_ge(s_oT, i * RING + (j + 1))
                    act.copy(diag[:, j % 2, :, :], pm[:, j % 2, :].rearrange("p (u f) -> p u f", f=P)).then_inc(s_oTc, 1)
            def stage_scatter(i, h, first=False):
                if not first:
                    act.wait_ge(s_scat[h], i * (16 * U))
                cols = slice(h * U, (h + 1) * U) if first else bass.ds(i * (2 * U) + h * U, U)
                act.copy(scat_rec[:, h, :, 0], src_far[:, cols])
                act.copy(scat_rec[:, h, :, 1], dst_zero[:, cols])
                act.copy(scat_pos[:, h, :], posi[:, cols]).then_inc(s_scst, 1)

            def stage_scatters(a, z):
                with act.Fori(a, z) as i:
                    for h in range(2):
                        stage_scatter(i, h)

            act.wait_ge(s_go, go("positions"))
            for j in range(RING):
                act.wait_ge(s_gath[j], 16 * U * 4 * ROUNDS)
            act.copy(rec_tail[:, :, 0], src_far[:, COLS - TAIL:])
            act.copy(rec_tail[:, :, 1], dst_zero[:, COLS - TAIL:]).then_inc(s_rectail, 1)
            for h in range(2):
                stage_scatter(0, h, True)
            stage_scatters(1, 9)
            act.wait_ge(s_go, go("shifted"))
            act.activation(ext[:, :, 0:H], ext[:, :, 0:H], ACT.Exp).then_inc(s_exp, 1)
            stage_scatters(9, 43)
            act.wait_ge(s_go, go("self shifted"))
            act.activation(c12, c12, ACT.Exp).then_inc(s_exp, 1)
            stage_scatters(43, (COLS - TAIL) // (2 * U))
            roots(1)
            for h in range(2):
                act.wait_ge(s_scat[h], 16 * U * (COLS // (2 * U)))
            walk(5, idxA)
            act.wait_ge(s_w, 16 * 23)
            for c in range(HC_N):
                for a in range(2):
                    b = BATCH[f"hidden {c} {a}"]
                    w = min(512, TW - c * 512)
                    act.wait_ge(s_pe, b + 1)
                    act.activation((Vf, Zf)[a][:, c * 512:c * 512 + w], pm[:, b % 2, 0:w], ACT.Relu,
                                   bias=bcol[:, a:a + 1]).then_inc(s_ev[b % 2], 1)
            walk(6, idxA)
            roots(2)
            walk(7, idxB)
            rectified(2)
            walk(8, idxB)
            roots(3)

        @block.tensor
        def _(pe):
            pe.sem_inc(s_mm, RING)
            pe.sem_inc(s_dmm, 2)
            pe.wait_ge(s_const, 15)

            def room(b):
                if b >= 2:
                    pe.wait_ge(s_ev[b % 2], (b - 2) // 2 + 1)

            def turns(stage_name, n, of, ready=None):
                for k in range(-(-n // BT)):
                    b = BATCH[stage_name] + k
                    room(b)
                    if ready:
                        pe.wait_ge(s_up, up(ready, k))
                    for i in range(min(BT, n - k * BT)):
                        m = of(k * BT + i)
                        last = pe.transpose(pm[0:m.shape[1], b % 2, i * P:i * P + m.shape[0]], m, ident[0:m.shape[0], 0:m.shape[0]])
                    last.then_inc(s_pe, 1)

            def broadcast_firsts(name):
                b = BATCH["broadcast " + name]
                pe.wait_ge(s_go, go("firsts " + name))
                room(b)
                pe.matmul(pm[:, b % 2, 0:512], ones[0:1, :], firsts[:, 0:512], start=True, stop=True)
                pe.matmul(pm[:, b % 2, 512:COLS], ones[0:1, :], firsts[:, 512:COLS], start=True, stop=True).then_inc(s_pe, 1)

            def turn_tiles(name):
                pe.wait_ge(s_go, go("cv" + name))
                turns("tv" + name, 1, lambda i: tvc)

            def turn_lists(name):
                pe.wait_ge(s_go, go("rows " + name))
                turns("rel" + name, VT, lambda g: relR[:, g, :])
                turns("idx" + name, VT, lambda g: othR[:, g, :])
                if name == "A":
                    turns("weights", VT, lambda g: rows[:, g, 2, :])

            def degree_step(b, h, sem_value):
                pe.wait_ge(s_doh, sem_value)
                for u in range(U):
                    last = pe.matmul(deg_ps[b], ohl[:, h, :, u], ohh[:, h, :, u], start=False, stop=False, skip_group_check=True)
                last.then_inc(s_dmm, 1)

            def degree_ends(b, first):
                last = pe.matmul(deg_ps[b], zeros[:, :], zeros[:, 0:TILES], start=first, stop=not first, skip_group_check=True)
                if not first:
                    last.then_inc(s_deg, 1)

            broadcast_firsts("A")
            turn_tiles("A")
            degree_ends(0, True)
            with pe.Fori(0, COLS // (2 * U)) as i:
                for h in range(2):
                    degree_step(0, h, i * 2 + (h + 1))
            degree_ends(0, False)
            turn_lists("A")
            pe.wait_ge(s_w, 16 * 23)
            turns("turn mW", 2, lambda i: W[:, 13 + i, :])

            def walk(k, nodes_first, cuts={}, degrees=False):
                for a, z in segments(cuts):
                    if a:
                        cuts[a]()
                    with pe.Fori(a, z) as i:
                        for j in range(RING):
                            G = i * RING + (k * GROUPS + j)
                            pe.wait_ge(s_oh, i * RING + (k * (GROUPS + 1) + j + 1))
                            pe.wait_ge(s_add, G * U + U)
                            pe.wait_ge(s_gath[j], i * (16 * U) + 16 * U * (gathers_before(k) * ROUNDS + 1))
                            for u in range(U):
                                if nodes_first:
                                    last = pe.matmul(ps[:, j % 2, u, :], oh[:, j % 2, u, :], msg[:, j, u, :], start=True, stop=True)
                                else:
                                    last = pe.matmul(ps[:, j % 2, u, :], msg[:, j, u, :], oh[:, j % 2, u, :], start=True, stop=True)
                            last.then_inc(s_mm, 1)
                            if degrees:
                                degree_step(1, j % 2, i * RING + (COLS // U + j + 1))

            def one_product(b, k, pairs_of):
                room(b)
                for i in range(BT):
                    ab = pairs_of(k * BT + i)
                    for n, (lhsT, rhs) in enumerate(ab):
                        last = pe.matmul(pm[:, b % 2, i * P:(i + 1) * P], lhsT, rhs, start=(n == 0), stop=(n == len(ab) - 1))
                last.then_inc(s_pe, 1)

            def products(stage_name, pairs_of):
                for k in range(NB):
                    one_product(BATCH[stage_name] + k, k, pairs_of)

            def degree_rows():
                for n in range(NB):
                    b = BATCH["rdeg"] + n
                    room(b)
                    pe.wait_ge(s_diag, n + 1)
                    for i in range(BT):
                        last = pe.matmul(pm[:, b % 2, i * P:(i + 1) * P], ones[:, :], diag[:, n % 2, i, :], start=True, stop=True)
                    last.then_inc(s_pe, 1)

            def passed(k):
                pe.wait_ge(s_add, U * GROUPS * (k + 1) + 2 * U)

            def bins():
                b = BATCH["bins"]
                pe.wait_ge(s_go, go("counts"))
                room(b)
                pe.matmul(pm[:, b % 2, 0:BINS2], lower[:, :], cnt, start=True, stop=True)
                pe.matmul(pm[:, b % 2, 512:512 + BINS2], ones[:, :], cnt, start=True, stop=True).then_inc(s_pe, 1)

            for k in range(3):
                turns(f"self {k}", TILES, lambda t: Y[:, t, :], f"t{k}")
                walk(k, False)
                passed(k)
                for n in range(NB):
                    one_product(BATCH[f"gcn {k}"] + n if k < 2 else BATCH[f"gcn 2 batch {n}"], n, lambda t: [(acc[:, t, :], W[:, k, :])])
                if k == 0:
                    bins()
            turns("turn X1", TILES, lambda t: X[:, t, :], "x1")
            for h in range(2):
                pe.wait_ge(s_ev[h], (BATCH["x_l"] + 1 - h) // 2)
            products("x_l", lambda t: [(Y[:, t, :], W[:, 3, :])])
            products("x_r", lambda t: [(Y[:, t, :], W[:, 4, :])])
            for h in range(2):
                pe.wait_ge(s_ev[h], (BATCH["rows of keys"] + 1 - h) // 2)
            with pe.Fori(0, ROUNDS) as i:
                for j in range(RING):
                    G = i * RING + (3 * GROUPS + j)
                    pe.wait_ge(s_oh, i * RING + (3 * (GROUPS + 1) + j + 1))
                    for u in range(U):
                        last = pe.transpose(pm[:, j % 2, u * P:(u + 1) * P], oh[:, j % 2, u, :], ident[:, :])
                    last.then_inc(s_oT, 1)
                    tiles = tiles_of(mybir.EngineType.PE, i * (RING * U) + j * U)
                    pe.wait_ge(s_oTc, i * RING + (j + 1))
                    pe.wait_ge(s_add, G * U + U)
                    for u, t in enumerate(tiles):
                        last = pe.matmul(ps[:, j % 2, u, :], diag[:, j % 2, u, :], Vf[:, bass.ds(t * P, P)], start=True, stop=True)
                    last.then_inc(s_mm, 1)

            pe.wait_ge(s_add, U * GROUPS * 4 + 2 * U)
            turns("rows of keys", VT, lambda g: relA[:, g * P:(g + 1) * P])
            turns("rows of weights", VT, lambda g: wA[:, g * P:(g + 1) * P])
            for h in range(H):
                turns(f"rows of scores {h}", VT, lambda g: ext[:, g * P:min((g + 1) * P, VISITS), h])
            pe.wait_ge(s_go, go("carry sources"))
            for q in range(5):
                turns(f"ends {q}", VT, lambda g: ends[:, q, g, :])
            pe.wait_ge(s_go, go("carries"))
            for q in range(3):
                turns(f"carries {q}", VT, lambda g: crow[q][:, g * P:(g + 1) * P])
            pe.wait_ge(s_go, go("largest"))
            turns("lasts", VT, lambda g: lastR[:, g, :])
            for c in range(C5):
                turns(f"largest {c}", VT, lambda g: F5[:, c, g, :])

            for h in range(2):
                pe.wait_ge(s_ev[h], (BATCH["turn X"] + 1 - h) // 2)
            with pe.Fori(0, ROUNDS) as i:
                for j in range(RING):
                    G = i * RING + (4 * GROUPS + j)
                    pe.wait_ge(s_oh, i * RING + (4 * (GROUPS + 1) + j + 1))
                    pe.wait_ge(s_add, G * U + U)
                    pe.wait_ge(s_msgs, i * RING + (j + 1))
                    for u in range(U):
                        last = pe.matmul(gsum(j % 2, u), oh[:, j % 2, u, :], rows_of[:, j, u, :], start=True, stop=True)
                    last.then_inc(s_mm, 1)
            passed(4)

            turns("turn X", TILES, lambda t: X[:, t, :], "x2")
            walk(5, False, {6: lambda: broadcast_firsts("B"), 12: lambda: turn_tiles("B"), 20: lambda: turn_lists("B"), 23: degree_rows})
            passed(5)
            for step in HIDDEN:
                b = BATCH[step]
                if step[0] == "h":
                    c, a = map(int, step.split()[1:])
                    w = min(512, TW - c * 512)
                    pe.wait_ge(s_scaled, min(NB, -(-(c + 1) * 512 // (BT * P))))
                    room(b)
                    pe.matmul(pm[:, b % 2, 0:w], W[:, 5 + a, :], accf[:, c * 512:c * 512 + w], start=True, stop=False)
                    pe.matmul(pm[:, b % 2, 0:w], W[:, 7 + a, :], Yf[:, c * 512:c * 512 + w], start=False, stop=True).then_inc(s_pe, 1)
                else:
                    n = int(step.split()[1])
                    for a in range(2):
                        done = BATCH[f"hidden {chunk_of_batch(n)} {a}"]
                        pe.wait_ge(s_ev[done % 2], done // 2 + 1)
                    one_product(b, n, lambda t: [(V[:, t, :], W[:, 9, :]), (Z[:, t, :], W[:, 10, :])])
            products("q", lambda t: [(V[:, t, :], W[:, 11, :]), (Z[:, t, :], W[:, 12, :])])
            for h in range(2):
                pe.wait_ge(s_ev[h], (BATCH["mean 0"] + 1 - h) // 2)
            degree_ends(1, True)
            walk(6, True, degrees=True)
            degree_ends(1, False)
            walk(7, False)
            passed(7)
            products("mean 0", lambda t: [(acc[:, t, :], W[:, 13, :])])
            walk(8, False)
            passed(8)
            for n in range(NB):
                one_product(BATCH[f"mean 1 batch {n}"], n, lambda t: [(acc[:, t, :], W[:, 14, :])])

        @block.vector
        def _(dve):
            n_chain = [0]
            n_go = [0]

            def link(ins):
                n_chain[0] += 1
                ins.then_inc(s_chain, 1)
                dve.wait_ge(s_chain, n_chain[0])

            def reached(name):
                n_go[0] += 1
                assert go(name) == n_go[0], name
                dve.sem_inc(s_go, 1)

            n_up = [0]

            def arose(name, n):
                n_up[0] += 1
                assert up(name, n) == n_up[0], name
                dve.sem_inc(s_up, 1)

            def summed(name, n):
                n_up[0] += 1
                assert up(name, n) == n_up[0], name
                dve.sem_inc(s_summed, 1)

            def wide(a, n=D):
                return a.rearrange("p (t o) -> p t o", o=1).to_broadcast([P, a.shape[1], n])

            def over(a, n=TILES):
                return a.rearrange("p (o f) -> p o f", o=1).to_broadcast([P, n, a.shape[1]])

            dve.sem_inc(s_add, 2 * U)
            dve.sem_inc(s_bin, 1)
            dve.wait_ge(s_const, 15)
            link(dve.tensor_copy(iota_f[:, :], iota_i))
            link(dve.tensor_copy(vcol[:, :], vcol_i[:, :]))
            dve.wait_ge(s_edges, 16 * 10)
            def node_halves(node, hi, lo):
                link(dve.tensor_scalar(hi_i, node, 7, None, ALU.logical_shift_right))
                link(dve.tensor_copy(hi_f, hi_i))
                link(dve.tensor_copy(lo_f, node))
                link(dve.scalar_tensor_tensor(out=lo, in0=hi_f, scalar=-128.0, in1=lo_f, op0=ALU.mult, op1=ALU.add))
                link(dve.tensor_scalar(hi, hi_f, float(BINS - 1), None, ALU.min))

            def source_halves():
                link(dve.memset(hi_src, float(BINS2 + 8)))
                link(dve.memset(lo_src, 0.0))
                link(dve.tensor_copy(iota8, iota_f[:, :].rearrange("p (n o) -> p n o", o=1).to_broadcast([P, P, U])))
                node_halves(src_far, hi_src[:, 0:COLS], lo_src[:, 0:COLS])

            source_halves()
            node_halves(dst_far, hi_dst, lo_dst)
            reached("halves")

            def degree_step(hi, lo, first, h, at):
                dve.wait_ge(s_dmm, at)
                cols = lambda a, n: a[:, first].rearrange("p (o u) -> p o u", o=1).to_broadcast([P, n, U])
                dve.tensor_tensor(ohh[:, h, :, :], iota8[:, 0:TILES, :], cols(hi, TILES), ALU.is_equal)
                dve.tensor_tensor(ohl[:, h, :, :], iota8, cols(lo, P), ALU.is_equal).then_inc(s_doh, 1)

            def count_bin(at, col):
                dve.wait_ge(s_bin, at + 1)
                dve.tensor_scalar(mask, hi_src[:, 0:COLS], iota_f[:, col], 0.0, ALU.is_equal, ALU.add,
                                  accum_out=cnt[:, col]).then_inc(s_bin, 1)

            def bin_bases():
                b = BATCH["bins"]
                dve.wait_ge(s_pe, b + 1)
                link(dve.tensor_copy(tot, pm[:, b % 2, 512:512 + BINS2]))
                link(dve.tensor_tensor_scan(run, ones[:, 0:BINS2], tot, 0.0, ALU.mult, ALU.add))
                link(dve.tensor_tensor(run, run, tot, ALU.subtract))
                link(dve.scalar_tensor_tensor(out=base, in0=run, scalar=-1.0, in1=pm[:, b % 2, 0:BINS2], op0=ALU.add, op1=ALU.add))
                dve.sem_inc(s_ev[b % 2], 1)
                link(dve.memset(pos, 0.0))
                link(dve.memset(onesw, 1.0))

            def number_bin(at, col):
                dve.wait_ge(s_bin, at + (BINS2 + 1))
                dve.tensor_scalar(mask, hi_src[:, 0:COLS], iota_f[:, col], None, ALU.is_equal).then_inc(s_bin, 1)
                dve.wait_ge(s_bin, at + (BINS2 + 2))
                dve.tensor_tensor_scan(cum, onesw, mask, base[:, col], ALU.mult, ALU.add).then_inc(s_bin, 1)
                dve.wait_ge(s_bin, at + (BINS2 + 3))
                dve.sem_inc(s_dpass, 1)
                dve.copy_predicated(pos, mask.bitcast(I32), cum).then_inc(s_bin, 1)

            def scale_add(out, sums, scale, add, n):
                for i in range(BT):
                    t = n * BT + i
                    last = dve.scalar_tensor_tensor(out=out[:, t, :], in0=sums[:, i, :], scalar=scale[:, t:t + 1], in1=add(t), op0=ALU.mult, op1=ALU.add)
                link(last)

            def evac(name, n, of, first=0):
                for k in range(first, first + n):
                    b = BATCH[name] + k - first
                    dve.wait_ge(s_pe, b + 1)
                    of(k, pmv(b % 2))
                    dve.sem_inc(s_ev[b % 2], 1)

            def list_firsts(name):
                dve.wait_ge(s_first, 16 if name == "A" else 32)
                link(dve.tensor_scalar(firsts_s, firsts_i, 7, None, ALU.logical_shift_right))
                link(dve.tensor_copy(firsts, firsts_s))
                link(dve.tensor_tensor(firsts, firsts, chunk_no[:, :], ALU.add))
                reached("firsts " + name)

            def list_chunks(name):
                b = BATCH["broadcast " + name]
                dve.wait_ge(s_pe, b + 1)
                for g in range(VT):
                    link(dve.tensor_scalar(before[:, 0:CHUNKS - 1], pm[:, b % 2, 1:CHUNKS], vcol[:, g:g + 1], None, ALU.is_le))
                    link(dve.tensor_reduce(cv[:, g:g + 1], before[:, 0:CHUNKS - 1], AX.X, ALU.add))
                dve.sem_inc(s_ev[b % 2], 1)
                link(dve.tensor_copy(cvi, cv))
                link(dve.tensor_tensor(tv, vcol[:, :], cv, ALU.subtract))
                link(dve.tensor_scalar(tv128, tv, 128.0, None, ALU.mult))
                link(dve.tensor_scalar(tvc, tv, float(TILES - 1), None, ALU.min))
                reached("cv" + name)

            def list_tiles(name):
                evac("tv" + name, 1, lambda k, s: link(dve.tensor_copy(tvT[:, :], s[0:VT, 0, :])))
                reached("tvT " + name)

            def list_rows(name):
                key_rows, oth_rows = (rowsi[:, :, 0, :], rowsi[:, :, 1, :]) if name == "A" else (prow[:, :, :, 0], prow[:, :, :, 1])
                if name == "B":
                    source_halves()
                dve.wait_ge(s_rows, 16 * VT * (3 if name == "A" else 4))
                link(dve.tensor_copy(relR, key_rows))
                link(dve.tensor_copy(othR, oth_rows))
                link(dve.tensor_tensor(relR, relR, wide(tv128, P), ALU.subtract))
                reached("rows " + name)

            def list_columns(name, rel, idx):
                by_visit = lambda a: a[:, :].rearrange("p (g v) -> p g v", g=VT)
                evac("rel" + name, 1, lambda k, s: link(dve.tensor_copy(by_visit(rel), s)))
                evac("idx" + name, 1, lambda k, s: link(dve.tensor_copy(by_visit(idx), s)))
                if name == "A":
                    evac("weights", 1, lambda k, s: link(dve.tensor_copy(by_visit(wA), s)))

            def finish_degrees():
                link(dve.tensor_scalar(dinv[:, :], deg_ps[0], 1.0, None, ALU.add))
                link(dve.tensor_scalar(degin[:, :], deg_ps[0], 1.0, None, ALU.max))
                link(dve.tensor_scalar(hasin[:, :], deg_ps[0], 1.0, None, ALU.min))
                link(dve.reciprocal(degin[:, :], degin[:, :]))

            list_firsts("A")
            list_chunks("A")
            list_tiles("A")
            with dve.Fori(0, COLS // (2 * U)) as i:
                for h in range(2):
                    degree_step(hi_dst, lo_dst, bass.ds(i * (2 * U) + h * U, U), h, i * 2 + (h + 1))
            dve.wait_ge(s_list, 48)
            dve.wait_ge(s_deg, 1)
            list_rows("A")
            list_columns("A", relA, idxA)
            finish_degrees()
            reached("degrees")
            evac("turn mW", 1, lambda k, s: link(dve.tensor_copy(W[:, 13:15, :], s[:, 0:2, :])))
            dve.wait_ge(s_root, 1)
            link(dve.reciprocal(dinv[:, :], dinv[:, :]))
            dve.wait_ge(s_xin, 32)
            dve.wait_ge(s_tv, 16 * VT)

            def onehot(rel, first, j, at):
                dve.wait_ge(s_mm, at)
                dve.tensor_tensor(oh[:, j % 2, :, :], over(iota_f[:, 0:P], U),
                                  rel[:, first].rearrange("p (u o) -> p u o", o=1).to_broadcast([P, U, P]),
                                  ALU.is_equal).then_inc(s_oh, 1)

            def walk(k, rel, cuts={}, extra=None):
                if k:
                    dve.wait_ge(s_oh, k * (GROUPS + 1))
                onehot(rel, slice(0, U), 0, k * GROUPS + RING)
                for a, z in segments(cuts):
                    if a:
                        cuts[a]()
                    with dve.Fori(a, z) as i:
                        for j in range(RING):
                            g8 = i * (RING * U)
                            onehot(rel, bass.ds(g8 + (j + 1) * U, U), j + 1, i * RING + (k * GROUPS + j + RING))
                            if extra:
                                extra(i, j)
                            tiles = tiles_of(mybir.EngineType.DVE, g8 + j * U)
                            dve.wait_ge(s_mm, i * RING + (k * GROUPS + j + 1 + RING))
                            for u, t in enumerate(tiles):
                                dve.wait_ge(s_add, g8 + (U * (k * GROUPS + j) + u + 2 * U))
                                part = accf[:, bass.ds(t * P, P)]
                                dve.tensor_tensor(part, part, ps[:, j % 2, u, :], ALU.add).then_inc(s_add, 1)
                dve.wait_ge(s_add, U * GROUPS * (k + 1) + 2 * U)

            def layer_norm(m, name, rows_of_batch=None):
                tiles = lambda a, n: a[:, n * BT:(n + 1) * BT]
                for n in range(NB):
                    if rows_of_batch:
                        rows_of_batch(n)
                    minus_mean = tiles(stat[:, 0, :], n)
                    link(dve.tensor_reduce(minus_mean, batch_of(Z, n), AX.X, ALU.add))
                    link(dve.tensor_scalar(minus_mean, minus_mean, -1.0 / D, None, ALU.mult))
                    dve.sem_inc(s_mean, 1)
                for n in range(NB):
                    dve.wait_ge(s_root, 1 + m * NB + n + 1)
                    link(dve.reciprocal(tiles(stat[:, 2, :], n), tiles(stat[:, 1, :], n)))
                    for t in range(n * BT, (n + 1) * BT):
                        last = dve.tensor_scalar(X[:, t, :], Z[:, t, :], stat[:, 0, t:t + 1], stat[:, 2, t:t + 1], ALU.add, ALU.mult)
                    link(last)
                    arose(name, n)

            def batch_of(buf, k):
                return buf[:, k * BT:(k + 1) * BT, :]

            dinv_of = lambda n: wide(dinv[:, n * BT:(n + 1) * BT])
            for n in range(NB):
                link(dve.tensor_tensor(batch_of(Y, n), batch_of(X, n), dinv_of(n), ALU.mult))
                arose("t0", n)
            dve.wait_ge(s_w, 16 * 23)

            link(dve.tensor_tensor(dinv2[:, :], dinv[:, :], dinv[:, :], ALU.mult))

            def gcn(k):
                def of(n, s):
                    scale_add(Z, s, dinv2 if k < 2 else dinv, lambda t: Z[:, t, :], n)
                    if k < 2:
                        summed(f"t{k + 1}", n)
                return of

            def counting(i, j):
                if j % 2 == 0:
                    count_bin(i * 2 + j // 2, bass.ds(i * 2 + j // 2, 1))

            def numbering(i, j):
                if j % 2 == 0:
                    number_bin(i * 6 + 3 * (j // 2), bass.ds(i * 2 + j // 2, 1))

            for k in range(3):
                evac(f"self {k}", NB, lambda n, s: link(dve.tensor_copy(batch_of(acc, n), s)))
                if k < 2:
                    link(dve.tensor_tensor(Z[:, :, :], over(brow[:, k, :]), wide(dinv[:, :]), ALU.mult))
                else:
                    link(dve.tensor_tensor(Z[:, :, :], over(brow[:, k, :]), X[:, :, :], ALU.add))
                walk(k, relA, extra=(counting, numbering, None)[k])
                if k == 0:
                    dve.wait_ge(s_bin, BINS2 + 1)
                    reached("counts")
                if k == 1:
                    dve.wait_ge(s_bin, 4 * BINS2 + 1)
                    link(dve.tensor_copy(posi[:, :], pos))
                    reached("positions")
                dve.wait_ge(s_tab, 16 * NB * (k + 1))
                if k < 2:
                    evac(f"gcn {k}", NB, gcn(k))
                if k == 0:
                    bin_bases()
            layer_norm(0, "x1", lambda n: evac(f"gcn 2 batch {n}", 1, gcn(2), n))

            def x_l(n, s):
                link(dve.tensor_tensor(batch_of(Z, n), s, over(brow[:, 6, :], BT), ALU.add))
                arose("x_l", n)
            evac("x_l", NB, x_l)
            evac("x_r", NB, lambda n, s: link(dve.tensor_tensor(batch_of(V, n), s, over(brow[:, 7, :], BT), ALU.add)))
            We, att = brow[:, 9, :], brow[:, 10, :]

            dve.wait_ge(s_tab, stored("x_l"))
            dve.wait_ge(s_oh, 3 * (GROUPS + 1))
            onehot(relA, slice(0, U), 0, 3 * GROUPS + RING)
            with dve.Fori(0, ROUNDS) as i:
                for j in range(RING):
                    g8 = i * (RING * U)
                    at = i * (RING * 6) + 6 * j
                    onehot(relA, bass.ds(g8 + (j + 1) * U, U), j + 1, i * RING + (3 * GROUPS + j + RING))
                    dve.wait_ge(s_mm, i * RING + (3 * GROUPS + j + 1 + RING))
                    dve.wait_ge(s_gath[j], i * (16 * U) + 16 * U * (3 * ROUNDS + 1))
                    dve.tensor_tensor(sc_a, ps[:, j % 2, :, :], msg[:, j, :, :], ALU.add).then_inc(s_p1, 1)
                    dve.tensor_tensor(sc_b, over(We, U), wA[:, bass.ds(g8 + j * U, U)].rearrange("p (u o) -> p u o", o=1).to_broadcast([P, U, D]),
                                      ALU.mult).then_inc(s_p1, 1)
                    dve.wait_ge(s_p1, at + 2)
                    dve.tensor_tensor(sc_a, sc_a, sc_b, ALU.add).then_inc(s_p1, 1)
                    dve.wait_ge(s_p1, at + 3)
                    dve.scalar_tensor_tensor(out=sc_b, in0=sc_a, scalar=0.2, in1=sc_a, op0=ALU.mult, op1=ALU.max).then_inc(s_p1, 1)
                    dve.wait_ge(s_p1, at + 4)
                    dve.tensor_tensor(sc_a, sc_b, over(att, U), ALU.mult).then_inc(s_p1, 1)
                    dve.wait_ge(s_p1, at + 5)
                    dve.tensor_reduce(ext[:, bass.ds(g8 + j * U, U), 0:H], sc_a.rearrange("p u (h c) -> p u h c", h=H), AX.X, ALU.add).then_inc(s_p1, 1)
                    dve.wait_ge(s_p1, at + 6)
                    dve.wait_ge(s_store[j], i * 16 + 16)
                    dve.sem_inc(s_add, U)
            dve.wait_ge(s_add, U * GROUPS * 4 + 2 * U)
            dve.wait_ge(s_xlback, 16)
            link(dve.tensor_tensor(V[:, :, :], V[:, :, :], Z[:, :, :], ALU.add))

            def masks(k, s):
                link(dve.tensor_scalar(tmpR, s, 0.0, None, ALU.is_ge))
                link(dve.scalar_tensor_tensor(out=tmpR, in0=s, scalar=P - 0.5, in1=tmpR, op0=ALU.is_le, op1=ALU.mult))
                link(dve.scalar_tensor_tensor(out=keyR, in0=s, scalar=1.0, in1=tmpR, op0=ALU.add, op1=ALU.mult))
                link(dve.tensor_scalar(keyR, keyR, -1.0, None, ALU.add))
                link(dve.tensor_scalar(tmpR, tmpR, -1.0, BIG, ALU.add, ALU.mult))
            evac("rows of keys", 1, masks)
            link(dve.memset(penF, -BIG))
            link(dve.memset(penB, -BIG))
            link(dve.memset(A5[:, :, VT - 1, :], -BIG))
            link(dve.tensor_tensor(penF[:, :, 1:P], keyR[:, :, 1:P], keyR[:, :, 0:P - 1], ALU.is_equal))
            link(dve.tensor_scalar(penF[:, :, 1:P], penF[:, :, 1:P], -1.0, BIG, ALU.add, ALU.mult))
            link(dve.tensor_copy(penB[:, :, 0:P - 1], penF[:, :, 1:P]))
            link(dve.tensor_reduce(ends[:, 4, :, 0:1].rearrange("p g a -> p (g a)"), penF[:, :, 1:P], AX.X, ALU.min))
            evac("rows of weights", 1, lambda k, s: link(dve.tensor_tensor(A5[:, H, :, :], s, tmpR, ALU.add)))
            VL = VISITS - (VT - 1) * P

            def scores_rows(h):
                def of(k, s):
                    link(dve.tensor_tensor(A5[:, h, 0:VT - 1, :], s[:, 0:VT - 1, :], tmpR[:, 0:VT - 1, :], ALU.add))
                    link(dve.tensor_tensor(A5[0:VL, h, VT - 1, :], s[0:VL, VT - 1, :], tmpR[0:VL, VT - 1, :], ALU.add))
                return of
            for h in range(H):
                evac(f"rows of scores {h}", 1, scores_rows(h))
            flat = lambda a: a.rearrange("p g e -> p (g e)")
            for c in range(C5):
                link(dve.tensor_tensor_scan(flat(F5[:, c, :, :]), flat(penF), flat(A5[:, c, :, :]), -BIG, ALU.add, ALU.max))
                link(dve.tensor_tensor_scan(flat(A5[:, c, :, :])[:, ::-1], flat(penB)[:, ::-1], flat(A5[:, c, :, :])[:, ::-1], -BIG, ALU.add, ALU.max))
            bc = lambda a: a.to_broadcast([P, VT, C5])
            link(dve.tensor_copy(ends[:, 4, :, 1:C5], ends[:, 4, :, 0:1].to_broadcast([P, VT, C5 - 1])))
            link(dve.tensor_copy(ends[:, 0, :, :], F5[:, :, :, P - 1].rearrange("p c g -> p g c")))
            link(dve.tensor_copy(ends[:, 1, :, :], A5[:, :, :, 0].rearrange("p c g -> p g c")))
            link(dve.tensor_copy(ends[:, 2, :, :], bc(keyR[:, :, 0:1])))
            link(dve.tensor_copy(ends[:, 3, :, :], bc(keyR[:, :, P - 1:P])))
            reached("carry sources")
            for q in range(5):
                b = BATCH[f"ends {q}"]
                dve.wait_ge(s_pe, b + 1)
                link(dve.tensor_copy(rowbuf[q], pm[0:C5, b % 2, 0:VP]))
                dve.sem_inc(s_ev[b % 2], 1)
            rF, rB, rfirst, rlast, rwhole, rlink = rowbuf
            link(dve.memset(rlink[:, 0:1], -BIG))
            link(dve.tensor_tensor(rlink[:, 1:VP], rfirst[:, 1:VP], rlast[:, 0:VP - 1], ALU.is_equal))
            link(dve.tensor_scalar(rlink[:, 1:VP], rlink[:, 1:VP], -1.0, BIG, ALU.add, ALU.mult))
            link(dve.tensor_tensor(rfirst, rlink, rwhole, ALU.add))
            link(dve.memset(rlast[:, VP - 1:VP], -BIG))
            link(dve.tensor_tensor(rlast[:, 0:VP - 1], rlink[:, 1:VP], rwhole[:, 0:VP - 1], ALU.add))
            link(dve.tensor_tensor_scan(rF, rfirst, rF, -BIG, ALU.add, ALU.max))
            link(dve.tensor_tensor_scan(rB[:, ::-1], rlast[:, ::-1], rB[:, ::-1], -BIG, ALU.add, ALU.max))
            cF, cB, cL = crow
            for c in (cF[:, 0:1], cB[:, VP - 1:VP], cL[:, VP - 1:VP]):
                link(dve.memset(c, -BIG))
            link(dve.tensor_tensor(cF[:, 1:VP], rF[:, 0:VP - 1], rlink[:, 1:VP], ALU.add))
            link(dve.tensor_tensor(cB[:, 0:VP - 1], rB[:, 1:VP], rlink[:, 1:VP], ALU.add))
            link(dve.tensor_copy(cL[:, 0:VP - 1], rlink[:, 1:VP]))
            reached("carries")
            for q in range(3):
                evac(f"carries {q}", 1, lambda k, s: link(dve.tensor_copy(backs[:, q, :, :], s[:, :, 0:C5])))
            link(dve.tensor_tensor(F5, F5, A5, ALU.max))
            for q, end in ((0, 0), (1, P - 1)):
                link(dve.tensor_tensor(tmpR, keyR, keyR[:, :, end:end + 1].to_broadcast([P, VT, P]), ALU.is_equal))
                link(dve.tensor_scalar(tmpR, tmpR, -1.0, BIG, ALU.add, ALU.mult))
                for c in range(C5):
                    for g in range(VT):
                        link(dve.scalar_tensor_tensor(out=F5[:, c, g, :], in0=tmpR[:, g, :], scalar=backs[:, q, g, c:c + 1],
                                                      in1=F5[:, c, g, :], op0=ALU.add, op1=ALU.max))
            link(dve.tensor_scalar(lastR[:, :, 0:P - 1], penB[:, :, 0:P - 1], -1.0, None, ALU.is_lt))
            link(dve.tensor_scalar(lastR[:, :, P - 1:P], backs[:, 2, :, 0:1], -1.0, None, ALU.is_lt))
            reached("largest")
            evac("lasts", 1, lambda k, s: link(dve.tensor_copy(lastT.rearrange("p (g e) -> p g e", g=VT), s)))
            for c in range(C5):
                def shift(k, s):
                    m = s.rearrange("p g e -> p (g e)")[:, 0:VISITS]
                    link(dve.tensor_tensor(ext[:, :, H + c], m, lastT[:, 0:VISITS], ALU.mult))
                    if c < H:
                        link(dve.tensor_tensor(ext[:, :, c], ext[:, :, c], m, ALU.subtract))
                evac(f"largest {c}", 1, shift)
            link(dve.tensor_scalar(ext[:, :, 0:H], ext[:, :, 0:H], 0.0, None, ALU.min))
            link(dve.memset(accG, 0.0))
            reached("shifted")
            dve.wait_ge(s_exp, 1)

            dve.wait_ge(s_oh, 4 * (GROUPS + 1))

            def matrices(first, n, j, u0):
                return dve.tensor_tensor(oh[:, j % 2, u0:u0 + n, :], over(iota_f[:, 0:P], n),
                                         relA[:, first].rearrange("p (u o) -> p u o", o=1).to_broadcast([P, n, P]), ALU.is_equal)

            def weigh(first, n, j, u0):
                m = msg[:, j, u0:u0 + n, :].rearrange("p u (h c) -> p u h c", h=H)
                w = ext[:, first, 0:H].rearrange("p u (h o) -> p u h o", o=1).to_broadcast([P, n, H, HC])
                dve.tensor_copy(rows_of[:, j, u0:u0 + n, D:GW], ext[:, first, :])
                return dve.tensor_tensor(m, m, w, ALU.mult)

            for j in range(2):
                dve.wait_ge(s_mm, 4 * GROUPS + RING)
                matrices(slice(j * U, (j + 1) * U), U, j, 0).then_inc(s_oh, 1)
                dve.wait_ge(s_back[j], 16)
                weigh(slice(j * U, (j + 1) * U), U, j, 0).then_inc(s_msgs, 1)

            def sum_round(i, last):
                g8 = i * (RING * U)
                for j in range(RING):
                    more = not (last and j >= RING - 2)
                    tiles = tiles_of(mybir.EngineType.DVE, g8 + j * U)
                    dve.wait_ge(s_mm, i * RING + (4 * GROUPS + j + 1 + RING))
                    if more:
                        dve.wait_ge(s_back[(j + 2) % RING], i * 16 + 16 + 16 * (j >= RING - 2))
                    for u, t in enumerate(tiles):
                        dve.wait_ge(s_add, g8 + (U * (4 * GROUPS + j) + u + 2 * U))
                        part = accG[:, bass.ds(t * GW, GW)]
                        dve.tensor_tensor(part, part, gsum(j % 2, u), ALU.add).then_inc(s_add, 1)
                        if more:
                            u0 = u // 2 * 2
                            first = bass.ds(g8 + ((j + 2) * U + u0), 2)
                            if u % 2 == 0:
                                made, s_made = matrices(first, 2, j, u0), s_oh
                            else:
                                made, s_made = weigh(first, 2, (j + 2) % RING, u0), s_msgs
                            if u >= U - 2:
                                made.then_inc(s_made, 1)

            with dve.Fori(0, ROUNDS - 1) as i:
                sum_round(i, False)
            sum_round(ROUNDS - 1, True)
            dve.sem_inc(s_oh, 1)
            dve.wait_ge(s_add, U * GROUPS * 5 + 2 * U)

            aG = accG.rearrange("p (t a) -> p t a", a=GW)
            heads = lambda a: a.rearrange("p t (h c) -> p t h c", h=H)
            per_head = lambda a: a.rearrange("p t (h o) -> p t h o", o=1).to_broadcast([P, TILES, H, HC])
            m_in, m_all, c_in, c_self, den, a_self = small[4], small[5], small[0], small[1], small[2], small[3]
            dve.wait_ge(s_xlback, 32)
            link(dve.tensor_tensor(selfT, aG[:, :, GW - 1:GW].to_broadcast([P, TILES, D]), over(We), ALU.mult))
            link(dve.tensor_tensor(selfT, selfT, V[:, :, :], ALU.add))
            link(dve.scalar_tensor_tensor(out=selfT, in0=selfT, scalar=0.2, in1=selfT, op0=ALU.mult, op1=ALU.max))
            link(dve.tensor_tensor(selfT, selfT, over(att), ALU.mult))
            link(dve.tensor_reduce(a_self, heads(selfT), AX.X, ALU.add))
            link(dve.tensor_scalar(hasin[:, :], hasin[:, :], -1.0, BIG, ALU.add, ALU.mult))
            link(dve.tensor_tensor(m_in, aG[:, :, D + H:D + 2 * H], wide(hasin[:, :], H), ALU.add))
            link(dve.tensor_tensor(m_all, m_in, a_self, ALU.max))
            link(dve.tensor_tensor(c_in, m_in, m_all, ALU.subtract))
            link(dve.tensor_tensor(c_self, a_self, m_all, ALU.subtract))
            reached("self shifted")
            dve.wait_ge(s_exp, 2)
            link(dve.tensor_tensor(den, c_in, aG[:, :, D:D + H], ALU.mult))
            link(dve.tensor_tensor(den, den, c_self, ALU.add))
            link(dve.tensor_scalar(den, den, 1e-16, None, ALU.add))
            link(dve.reciprocal(den, den))
            link(dve.tensor_tensor(c_in, c_in, den, ALU.mult))
            link(dve.tensor_tensor(c_self, c_self, den, ALU.mult))
            link(dve.tensor_tensor(heads(selfT), heads(aG[:, :, 0:D]), per_head(c_in), ALU.mult))
            link(dve.tensor_tensor(heads(Z[:, :, :]), heads(Z[:, :, :]), per_head(c_self), ALU.mult))
            link(dve.tensor_tensor(Z[:, :, :], Z[:, :, :], selfT, ALU.add))
            link(dve.tensor_tensor(Z[:, :, :], Z[:, :, :], over(brow[:, 8, :]), ALU.add))
            link(dve.tensor_tensor(Z[:, :, :], Z[:, :, :], X[:, :, :], ALU.add))
            layer_norm(1, "x2")

            evac("turn X", NB, lambda n, s: link(dve.tensor_copy(batch_of(Y, n), s)))
            link(dve.memset(acc, 0.0))
            def diagonal(n):
                dve.tensor_tensor(diag[:, n % 2, 0:BT, :], over(ident[:, :], BT), wide(degin[:, n * BT:(n + 1) * BT]), ALU.mult).then_inc(s_diag, 1)

            def degree_rows():
                diagonal(0)
                for n in range(NB):
                    if n + 1 < NB:
                        diagonal(n + 1)
                    b = BATCH["rdeg"] + n
                    dve.wait_ge(s_pe, b + 1)
                    link(dve.tensor_copy(batch_of(Z, n), pmv(b % 2)))
                    dve.sem_inc(s_ev[b % 2], 1)

            def rows_and_tiles_b():
                list_tiles("B")
                list_rows("B")

            walk(5, relA, {3: lambda: list_firsts("B"), 9: lambda: list_chunks("B"), 18: rows_and_tiles_b,
                           22: lambda: list_columns("B", relB, idxB), 23: degree_rows})

            for n in range(NB):
                link(dve.tensor_tensor(batch_of(acc, n), batch_of(acc, n), batch_of(Z, n), ALU.mult))
                dve.sem_inc(s_scaled, 1)

            def p_rows(n, s):
                link(dve.tensor_copy(batch_of(Y, n), s))
                arose("p", n)
            for n in range(NB):
                evac(f"p {n}", 1, p_rows, n)
            evac("q", NB, lambda n, s: link(dve.tensor_tensor(batch_of(acc, n), s, over(brow[:, 3, :], BT), ALU.add)))
            link(dve.tensor_tensor(Z[:, :, :], acc, X[:, :, :], ALU.add))
            link(dve.memset(acc, 0.0))

            def degrees_out(i, j):
                degree_step(hi_src, lo_src, bass.ds(i * (RING * U) + j * U, U), j % 2, i * RING + (COLS // U + j + 1))
            walk(6, relA, extra=degrees_out)
            dve.wait_ge(s_tab, stored("p"))
            layer_norm(2, "x3", lambda n: scale_add(Z, batch_of(acc, n), degin, lambda t: Z[:, t, :], n))
            dve.wait_ge(s_deg, 2)
            link(dve.tensor_scalar(degout[:, :], deg_ps[1], 1.0, None, ALU.max))
            link(dve.reciprocal(degout[:, :], degout[:, :]))
            dve.wait_ge(s_tv, 32 * VT)

            def mean(k):
                def of(n, s):
                    z = batch_of(Z, n)
                    scale_add(Z, s, degout, lambda t: brow[:, 4 + k, :], n)
                    if k == 0:
                        summed("h3", n)
                    else:
                        link(dve.scalar_tensor_tensor(out=z, in0=z, scalar=0.0, in1=batch_of(X, n), op0=ALU.max, op1=ALU.add))
                return of
            link(dve.memset(acc, 0.0))
            walk(7, relB)
            evac("mean 0", NB, mean(0))
            link(dve.memset(acc, 0.0))
            walk(8, relB)
            dve.wait_ge(s_tab, stored("h3"))
            layer_norm(3, "x4", lambda n: evac(f"mean 1 batch {n}", 1, mean(1), n))


_INS = ["x", "src", "dst", "edge_weight", "L0_gnn_W1", "L0_gnn_b1", "L0_gnn_W2", "L0_gnn_b2", "L0_gnn_W3", "L0_gnn_b3",
        "L1_gnn_Wl", "L1_gnn_bl", "L1_gnn_Wr", "L1_gnn_br", "L1_gnn_We", "L1_gnn_att", "L1_gnn_bias",
        "L2_gnn_Wl1", "L2_gnn_bl1", "L2_gnn_Wr1", "L2_gnn_Wl2", "L2_gnn_bl2", "L2_gnn_Wr2",
        "L3_gnn_W1", "L3_gnn_b1", "L3_gnn_W2", "L3_gnn_b2"]


def kernel(**inputs):
    import numpy as _np
    import concourse.bacc as _bacc
    from concourse import mybir as _mybir
    from concourse.bass_utils import run_bass_kernel_spmd as _run

    nc = _bacc.Bacc("TRN2", target_bir_lowering=False, num_devices=1)
    arrays, args = {}, []
    for name in _INS:
        a = _np.ascontiguousarray(inputs[name])
        arrays[f"in_{name}_dram"] = a
        args.append(nc.dram_tensor(f"in_{name}_dram", a.shape, _mybir.dt.from_np(a.dtype), kind="ExternalInput").ap())
    shape = inputs["x"].shape
    args.append(nc.dram_tensor("out_0_dram", shape, _mybir.dt.float32, kind="ExternalOutput").ap())
    build(nc, *args)
    r = _run(nc, [arrays], core_ids=[0])
    return r.results[0]["out_0_dram"]
```
